# Optimizing a Trainium2 kernel written in Bass

```python
import numpy as np
import jax
import jax.numpy as jnp

def _softmax(x, axis=-1):
    return jax.nn.softmax(x, axis=axis)

def _gelu(x):
    return jax.nn.gelu(x, approximate=True)

def _silu(x):
    return jax.nn.silu(x)

def _sigmoid(x):
    return jax.nn.sigmoid(x)

def _layernorm(x, axis=-1, eps=1e-05):
    m = jnp.mean(x, axis=axis, keepdims=True)
    v = jnp.var(x, axis=axis, keepdims=True)
    return (x - m) / jnp.sqrt(v + eps)

def _scatter_add(tgt, idx, src, axis=0):
    return tgt.at[idx].add(src)

def _segment_sum(src, seg, n):
    return jax.ops.segment_sum(src, seg, n)
kernel_name = 'mk_decoder_postln_d1_seqx_r4_697dad'

def setup_inputs(seed: int=0):
    np.random.seed(seed)
    _w = jnp.asarray

    def _rec_inputs():
        import jax
        import jax.numpy as jnp
        _rk = jax.random.key(seed)
        x = -0.0003929 + 0.9999 * jax.random.normal(jax.random.fold_in(_rk, 1), (8, 112, 512), jnp.float32)
        _lenS = 112 - jax.random.randint(jax.random.fold_in(_rk, 7), (8,), 0, max(1, 112 // 4) + 1, jnp.int32)
        _lenS2 = 375 - jax.random.randint(jax.random.fold_in(_rk, 8), (8,), 0, max(1, 375 // 4) + 1, jnp.int32)
        _ctx_2048P = jax.random.normal(jax.random.fold_in(_rk, 11), (8, 16, 512), jnp.float32)
        _ctx_2048c = jax.random.dirichlet(jax.random.fold_in(_rk, 511), 0.3 * jnp.ones((16,), jnp.float32), (8, 375))
        _ctx_2048t = jnp.einsum('bsk,bkd->bsd', _ctx_2048c, _ctx_2048P)
        _ctx_2048t = _ctx_2048t * jax.lax.rsqrt(jnp.mean(jnp.square(_ctx_2048t)) + 1e-12) * 0.953939
        ctx_2048 = -1.39393e-06 + 0.999914 * (_ctx_2048t + 0.3 * jax.random.normal(jax.random.fold_in(_rk, 611), (8, 375, 512), jnp.float32))
        itok_BxS_0_1023 = jax.random.randint(jax.random.fold_in(_rk, 12), (8, 112), 0, 256, jnp.int32)
        return (x, ctx_2048, itok_BxS_0_1023)
    x, ctx_2048, itok_BxS_0_1023 = _rec_inputs()

    def _L0_attn_setup():
        import jax, jax.numpy as jnp
        import numpy as np
        D_MODEL = 512
        NUM_HEADS = 16
        HEAD_DIM = D_MODEL // NUM_HEADS
        LAYER_IDX = 0
        NUM_LAYERS = 13
        REINIT_LAMBDA = 0.8

        def _heads(t, B, S):
            return t.reshape(B, S, NUM_HEADS, HEAD_DIM).transpose(0, 2, 1, 3)
        key = jax.random.key(seed)
        ks = jax.random.split(key, 8)
        B, S = (2, 512)
        x = jax.random.normal(ks[0], (B, S, D_MODEL), dtype=jnp.float32)
        init = 1.0 / np.sqrt(D_MODEL)

        def w(k):
            return jax.random.uniform(k, (D_MODEL, D_MODEL), dtype=jnp.float32, minval=-init, maxval=init)
        lam_init = REINIT_LAMBDA * ((LAYER_IDX + 1) / NUM_LAYERS)
        return {'x': x, 'q1_w': w(ks[1]), 'k1_w': w(ks[2]), 'q2_w': w(ks[3]), 'k2_w': w(ks[4]), 'v_w': w(ks[5]), 'o_w': w(ks[6]), 'lambda_param': jnp.full((NUM_HEADS,), lam_init, dtype=jnp.float32)}
    _L0_attn_all = _L0_attn_setup()
    _L0_attn_in = {k: v for k, v in _L0_attn_all.items() if k in ('q1_w', 'k1_w', 'q2_w', 'k2_w', 'v_w', 'o_w', 'lambda_param')}
    del _L0_attn_all

    def _L0_xattn_setup():
        import jax, jax.numpy as jnp
        import numpy as np
        B, Lq, Lk = (2, 1024, 256)
        Q_DIM, KV_DIM = (512, 512)
        H, HD = (16, 128)
        KVC, QC, R = (128, 192, 64)
        LOOKBACK = 8
        NEG = -1e+30

        def _rope(x, L):
            half = x.shape[-1] // 2
            inv_freq = 1.0 / 10000.0 ** (jnp.arange(half, dtype=jnp.float32) / half)
            ang = jnp.arange(L, dtype=jnp.float32)[:, None] * inv_freq
            cos, sin = (jnp.cos(ang), jnp.sin(ang))
            x1, x2 = (x[..., :half], x[..., half:])
            return jnp.concatenate([x1 * cos - x2 * sin, x1 * sin + x2 * cos], axis=-1)
        key = jax.random.key(seed)
        ks = jax.random.split(key, 11)

        def w(k, shape, fan_in):
            return jax.random.normal(k, shape, jnp.float32) / np.sqrt(fan_in).astype(np.float32)
        return {'q': jax.random.normal(ks[0], (B, Lq, Q_DIM), jnp.float32), 'kv': jax.random.normal(ks[1], (B, Lk, KV_DIM), jnp.float32), 'seg_id': jnp.sort(jax.random.randint(ks[2], (B, Lq), 0, Lk), axis=-1), 'W_kvc': w(ks[3], (KV_DIM, KVC), KV_DIM), 'W_dq': w(ks[4], (Q_DIM, QC), Q_DIM), 'W_uq': w(ks[5], (QC, H * HD), QC), 'W_qr': w(ks[6], (QC, H * R), QC), 'W_uk': w(ks[7], (KVC, H * HD), KVC), 'W_kr': w(ks[8], (KVC, R), KVC), 'W_uv': w(ks[9], (KVC, H * HD), KVC), 'W_o': w(ks[10], (H * HD, Q_DIM), H * HD)}
    _L0_xattn_all = _L0_xattn_setup()
    _L0_xattn_in = {k: v for k, v in _L0_xattn_all.items() if k in ('W_kvc', 'W_dq', 'W_uq', 'W_qr', 'W_uk', 'W_kr', 'W_uv', 'W_o')}
    del _L0_xattn_all

    def _L0_ffn_setup():
        import jax, jax.numpy as jnp
        import numpy as np
        FP8_MAX = 448.0
        GLOBAL_DIV = 448.0 * 6.0

        def _fp8(x):
            return x.astype(jnp.float8_e4m3fn).astype(jnp.float32)

        def _reorder_quantize_x(x, idx):
            scale = jnp.max(jnp.abs(x)) / GLOBAL_DIV
            xr = (x / scale)[:, idx]
            scale_x = jnp.max(jnp.abs(xr), axis=1, keepdims=True) / FP8_MAX
            qx = _fp8(xr / scale_x)
            return (qx, scale_x, scale)

        def _qlinear(qx, scale_x, scale, W, idx, out_idx=None):
            Wr = W[:, idx]
            w_scale = jnp.max(jnp.abs(Wr), axis=1, keepdims=True) / FP8_MAX
            qw = _fp8(Wr / w_scale)
            y = qx * scale_x @ (qw * w_scale).T * scale
            if out_idx is not None:
                y = y[:, out_idx]
            return y
        key = jax.random.key(seed)
        ks = jax.random.split(key, 6)
        B, S, H, I = (2, 256, 512, 1408)
        return {'x': jax.random.normal(ks[0], (B, S, H), jnp.float32), 'w_gate': jax.random.normal(ks[1], (I, H), jnp.float32) * 0.02, 'w_up': jax.random.normal(ks[2], (I, H), jnp.float32) * 0.02, 'w_down': jax.random.normal(ks[3], (H, I), jnp.float32) * 0.02, 'up_reorder_index': jax.random.permutation(ks[4], jnp.arange(H, dtype=jnp.int64)), 'down_reorder_index': jax.random.permutation(ks[5], jnp.arange(I, dtype=jnp.int64))}
    _L0_ffn_all = _L0_ffn_setup()
    _L0_ffn_in = {k: v for k, v in _L0_ffn_all.items() if k in ('w_gate', 'w_up', 'w_down', 'up_reorder_index', 'down_reorder_index')}
    del _L0_ffn_all
    return {'x': x, 'ctx_2048': ctx_2048, 'itok_BxS_0_1023': itok_BxS_0_1023, 'L0_attn_q1_w': _L0_attn_in['q1_w'], 'L0_attn_k1_w': _L0_attn_in['k1_w'], 'L0_attn_q2_w': _L0_attn_in['q2_w'], 'L0_attn_k2_w': _L0_attn_in['k2_w'], 'L0_attn_v_w': _L0_attn_in['v_w'], 'L0_attn_o_w': _L0_attn_in['o_w'], 'L0_attn_lambda_param': _L0_attn_in['lambda_param'], 'L0_xattn_W_kvc': _L0_xattn_in['W_kvc'], 'L0_xattn_W_dq': _L0_xattn_in['W_dq'], 'L0_xattn_W_uq': _L0_xattn_in['W_uq'], 'L0_xattn_W_qr': _L0_xattn_in['W_qr'], 'L0_xattn_W_uk': _L0_xattn_in['W_uk'], 'L0_xattn_W_kr': _L0_xattn_in['W_kr'], 'L0_xattn_W_uv': _L0_xattn_in['W_uv'], 'L0_xattn_W_o': _L0_xattn_in['W_o'], 'L0_ffn_w_gate': _L0_ffn_in['w_gate'], 'L0_ffn_w_up': _L0_ffn_in['w_up'], 'L0_ffn_w_down': _L0_ffn_in['w_down'], 'L0_ffn_up_reorder_index': _L0_ffn_in['up_reorder_index'], 'L0_ffn_down_reorder_index': _L0_ffn_in['down_reorder_index']}

def reference(x, ctx_2048, itok_BxS_0_1023, L0_attn_q1_w, L0_attn_k1_w, L0_attn_q2_w, L0_attn_k2_w, L0_attn_v_w, L0_attn_o_w, L0_attn_lambda_param, L0_xattn_W_kvc, L0_xattn_W_dq, L0_xattn_W_uq, L0_xattn_W_qr, L0_xattn_W_uk, L0_xattn_W_kr, L0_xattn_W_uv, L0_xattn_W_o, L0_ffn_w_gate, L0_ffn_w_up, L0_ffn_w_down, L0_ffn_up_reorder_index, L0_ffn_down_reorder_index):
    import jax
    import jax.numpy as jnp

    def _L0_attn_ref(x, q1_w, k1_w, q2_w, k2_w, v_w, o_w, lambda_param):
        import jax, jax.numpy as jnp
        import numpy as np
        D_MODEL = 512
        NUM_HEADS = 16
        HEAD_DIM = D_MODEL // NUM_HEADS
        LAYER_IDX = 0
        NUM_LAYERS = 13
        REINIT_LAMBDA = 0.8

        def _heads(t, B, S):
            return t.reshape(B, S, NUM_HEADS, HEAD_DIM).transpose(0, 2, 1, 3)
        B, S, _ = x.shape
        q1 = _heads(x @ q1_w.T, B, S)
        k1 = _heads(x @ k1_w.T, B, S)
        q2 = _heads(x @ q2_w.T, B, S)
        k2 = _heads(x @ k2_w.T, B, S)
        v = _heads(x @ v_w.T, B, S)
        scale = jnp.sqrt(jnp.float32(HEAD_DIM))
        attn1 = jax.nn.softmax(jnp.einsum('bhqd,bhkd->bhqk', q1, k1) / scale, axis=-1)
        attn2 = jax.nn.softmax(jnp.einsum('bhqd,bhkd->bhqk', q2, k2) / scale, axis=-1)
        lam = lambda_param.reshape(1, NUM_HEADS, 1, 1)
        out = jnp.einsum('bhqk,bhkd->bhqd', attn1 - lam * attn2, v)
        out = out.transpose(0, 2, 1, 3).reshape(B, S, D_MODEL)
        return out @ o_w.T

    def _L0_xattn_ref(q, kv, seg_id, W_kvc, W_dq, W_uq, W_qr, W_uk, W_kr, W_uv, W_o):
        import jax, jax.numpy as jnp
        import numpy as np
        B, Lq, Lk = (2, 1024, 256)
        Q_DIM, KV_DIM = (512, 512)
        H, HD = (16, 128)
        KVC, QC, R = (128, 192, 64)
        LOOKBACK = 8
        NEG = -1e+30

        def _rope(x, L):
            half = x.shape[-1] // 2
            inv_freq = 1.0 / 10000.0 ** (jnp.arange(half, dtype=jnp.float32) / half)
            ang = jnp.arange(L, dtype=jnp.float32)[:, None] * inv_freq
            cos, sin = (jnp.cos(ang), jnp.sin(ang))
            x1, x2 = (x[..., :half], x[..., half:])
            return jnp.concatenate([x1 * cos - x2 * sin, x1 * sin + x2 * cos], axis=-1)
        b, lq, _ = q.shape
        lk = kv.shape[1]
        kv_c = kv @ W_kvc
        q_c = q @ W_dq
        q_nope = (q_c @ W_uq).reshape(b, lq, H, HD).transpose(0, 2, 1, 3)
        q_rope = (q_c @ W_qr).reshape(b, lq, H, R).transpose(0, 2, 1, 3)
        k_nope = (kv_c @ W_uk).reshape(b, lk, H, HD)
        v = (kv_c @ W_uv).reshape(b, lk, H, HD)
        k_rope = kv_c @ W_kr
        q_rope = _rope(q_rope, lq)
        k_rope = _rope(k_rope, lk)
        scale = 1.0 / np.sqrt(HD + R).astype(np.float32)
        scores = (jnp.einsum('bhqd,bkhd->bhqk', q_nope, k_nope) + jnp.einsum('bhqr,bkr->bhqk', q_rope, k_rope)) * scale
        k_ids = jnp.arange(lk)[None, None, :]
        qs = seg_id[:, :, None]
        good = (k_ids <= qs) & (k_ids >= qs - LOOKBACK)
        scores = jnp.where(good[:, None, :, :], scores, NEG)
        attn = jax.nn.softmax(scores, axis=-1)
        out = jnp.einsum('bhqk,bkhd->bqhd', attn, v).reshape(b, lq, H * HD)
        return out @ W_o

    def _L0_ffn_ref(x, w_gate, w_up, w_down, up_reorder_index, down_reorder_index):
        import jax, jax.numpy as jnp
        import numpy as np
        FP8_MAX = 448.0
        GLOBAL_DIV = 448.0 * 6.0

        def _fp8(x):
            return x.astype(jnp.float8_e4m3fn).astype(jnp.float32)

        def _reorder_quantize_x(x, idx):
            scale = jnp.max(jnp.abs(x)) / GLOBAL_DIV
            xr = (x / scale)[:, idx]
            scale_x = jnp.max(jnp.abs(xr), axis=1, keepdims=True) / FP8_MAX
            qx = _fp8(xr / scale_x)
            return (qx, scale_x, scale)

        def _qlinear(qx, scale_x, scale, W, idx, out_idx=None):
            Wr = W[:, idx]
            w_scale = jnp.max(jnp.abs(Wr), axis=1, keepdims=True) / FP8_MAX
            qw = _fp8(Wr / w_scale)
            y = qx * scale_x @ (qw * w_scale).T * scale
            if out_idx is not None:
                y = y[:, out_idx]
            return y
        B, S, H = x.shape
        xf = x.reshape(B * S, H)
        qx, sx, sc = _reorder_quantize_x(xf, up_reorder_index)
        g = _qlinear(qx, sx, sc, w_gate, up_reorder_index, out_idx=down_reorder_index)
        u = _qlinear(qx, sx, sc, w_up, up_reorder_index, out_idx=down_reorder_index)
        t = jax.nn.silu(g) * u
        qt, st, sct = _reorder_quantize_x(t, down_reorder_index)
        y = _qlinear(qt, st, sct, w_down, down_reorder_index)
        return y.reshape(B, S, H)
    x = _layernorm(x + _L0_attn_ref(x, L0_attn_q1_w, L0_attn_k1_w, L0_attn_q2_w, L0_attn_k2_w, L0_attn_v_w, L0_attn_o_w, L0_attn_lambda_param), axis=-1)
    x = _layernorm(x + _L0_xattn_ref(x, ctx_2048, itok_BxS_0_1023, L0_xattn_W_kvc, L0_xattn_W_dq, L0_xattn_W_uq, L0_xattn_W_qr, L0_xattn_W_uk, L0_xattn_W_kr, L0_xattn_W_uv, L0_xattn_W_o), axis=-1)
    x = _layernorm(x + _L0_ffn_ref(x, L0_ffn_w_gate, L0_ffn_w_up, L0_ffn_w_down, L0_ffn_up_reorder_index, L0_ffn_down_reorder_index), axis=-1)
    return x

_drawn_inputs = setup_inputs


def setup_inputs(seed=0):
    import zlib

    import numpy as np

    out = dict(_drawn_inputs(seed))
    spreads = {'L0_attn_lambda_param': (0.0615384615957737, 0.6)}
    factors = {'L0_attn_q1_w': 4.251, 'L0_attn_k1_w': 3.725, 'L0_attn_q2_w': 8.0, 'L0_attn_k2_w': 8.0}
    for name, (base, spread) in spreads.items():
        noise = np.random.default_rng([zlib.crc32(name.encode()), seed]).standard_normal(out[name].shape)
        drawn = base * np.exp(spread * noise) if base else spread * noise
        out[name] = jnp.asarray(drawn.astype(out[name].dtype))
    for name, factor in factors.items():
        out[name] = (out[name] * factor).astype(out[name].dtype)
    return out
```

```python
from contextlib import ExitStack

import numpy as np

import concourse.bass as bass
from concourse import mybir

ALU = mybir.AluOpType
ACT = mybir.ActivationFunctionType
F32 = mybir.dt.float32
BF16 = mybir.dt.bfloat16
I32 = mybir.dt.int32
U32 = mybir.dt.uint32
AX = mybir.AxisListType

P = 128
B, T, D = 8, 112, 512
DC = D // P
NH, HD = 16, 32
HG = 4
NJ = NH // HG
LK = 375
KTILES, KROWS = 3, 125
KVC, QC, ROPE, XHD = 128, 192, 64, 128
QH = QC // 2
SPAN = 9
GQ = 7
NG = T // GQ
GK = 64
NT = NG * GK // P
TROWS = LK + 1
KW = KVC + 2 * ROPE
F = 1408
FC = F // P
FCH = [(0, 512), (512, 512), (1024, 384)]
FP8_MAX = 448.0
NEG = -1e30
EPS = 1e-5
MAGIC_MIN = 1.5 * 2.0 ** 14



class Chain:

    def __init__(self, eng, sem):
        self.eng, self.sem, self.base, self.n = eng, sem, 0, 0

    def __call__(self, ins):
        ins.then_inc(self.sem, 1)
        self.n += 1
        self.eng.wait_ge(self.sem, self.base + self.n)

    def turn(self, start, step, per):
        self.base, self.n = start + step * per, 0

    def turned(self, start, steps, per):
        assert self.n == per, (self.n, per)
        self.base, self.n = start + steps * per, 0

    @property
    def value(self):
        return self.base + self.n



def magic_bits(dve, scaled_bits):
    return dve.tensor_scalar(scaled_bits, scaled_bits, 0x7F800000, 0x00400000, ALU.bitwise_and, ALU.bitwise_or)


def magic_add(dve, y, magic):
    return dve.scalar_tensor_tensor(y, magic, MAGIC_MIN, y, ALU.max, ALU.add)


def magic_sub(dve, minus_q, summed, magic):
    return dve.scalar_tensor_tensor(minus_q, magic, MAGIC_MIN, summed, ALU.max, ALU.subtract)


def build(nc, a, out):
    table = nc.dram_tensor("key_table", [B * TROWS, KW], F32)

    table_rows = table[:].rearrange("(b r) n -> b r n", b=B)
    top = ExitStack()
    with top:
        def sem(name):
            return top.enter_context(nc.semaphore(name))

        def keep(name, shape, dt=F32):
            return top.enter_context(nc.sbuf_tensor(name, shape, dt))

        x_all = keep("x_all", [T, B, D])
        ident = keep("ident", [P, P])
        identb = keep("identb", [P, P], BF16)
        ones = keep("ones", [P, P])
        wdq = keep("wdq", [P, DC, QC])
        wqn = keep("wqn", [QH, 2, NH, XHD])
        wqr = keep("wqr", [QH, 2, NH, 2 * ROPE])
        rope_q = keep("rope_q", [P, T])
        gate_w = keep("gate_w", [P, DC, F], BF16)
        up_w = keep("up_w", [P, DC, F], BF16)
        down_w = keep("down_w", [P, FC, D], BF16)
        gate_s = keep("gate_s", [T, F])
        up_s = keep("up_s", [T, F])
        down_s = keep("down_s", [T, D])
        stats = keep("stats", [T, B, 6])
        mv = keep("mv", [T, B, 2])
        rstd = keep("rstd", [T, B])
        seg_rows = keep("seg_rows", [T, B * NG])
        row_idx = keep("row_idx", [P, B * NT], I32)
        off_mask = keep("off_mask", [T, GK])

        consts_in = sem("consts_in")
        weights_in = sem("weights_in")
        xwq_in = sem("xwq_in")
        x_in = sem("x_in")
        dve_chain = sem("dve_chain")
        chain = Chain(nc.vector, dve_chain)

        var_set = sem("var_set")
        std_set = sem("std_set")

        def layer_norm(dve, turn, done=None):
            for b in range(B):
                last = dve.bn_aggr(mv[:, b, :], stats[:, b, :])
            chain(last)
            chain(dve.tensor_scalar(rstd[:], mv[:, :, 1], EPS, None, ALU.add))
            dve.nop().then_inc(var_set, 1)
            dve.wait_ge(std_set, turn)
            chain(dve.reciprocal(rstd[:], rstd[:]))
            for b in range(B):
                last = dve.tensor_scalar(x_all[:, b, :], x_all[:, b, :], mv[:, b, 0:1], rstd[:, b:b + 1],
                                         ALU.subtract, ALU.mult)
                if done is not None:
                    last.then_inc(done, 1)
            if done is None:
                chain(last)

        with ExitStack() as st:
            def sb(name, shape, dt=F32):
                return st.enter_context(nc.sbuf_tensor(name, shape, dt))

            def ps(name, shape, dt=F32):
                return st.enter_context(nc.psum_tensor(name, shape, dt))

            ctx_t = [sb(f"ctx_t{k}", [P, DC, LK]) for k in range(2)]
            wkvx = sb("wkvx", [P, DC, 2 * P])
            wkvc_t = sb("wkvc_t", [P, D])
            wkr2 = sb("wkr2", [P, 2 * ROPE])
            rope_k = sb("rope_k", [KROWS, KTILES, 2 * ROPE])
            key_rows = [sb(f"key_rows{k}", [KROWS, KTILES, KW]) for k in range(2)]
            rot = sb("rot", [KROWS, KTILES, 2 * ROPE])
            mean_row = [sb(f"mean_row{k}", [1, KW]) for k in range(2)]
            wuq_t = sb("wuq_t", [P, NH, QC])
            wuk_t = sb("wuk_t", [P, NH, KVC])
            raw_gu = [[sb(f"raw_gu{m}{k}", [P, D]) for k in range(2)] for m in range(2)]
            raw_d = sb("raw_d", [P, F])
            mag = sb("mag", [P, F])
            mag_u = mag[:].bitcast(U32)
            summ = sb("summ", [P, F])
            qt = sb("qt", [P, F], BF16)
            amax = sb("amax", [P, 1])
            wsc = sb("wsc", [P, 1])
            inv = sb("inv", [P, 2])
            diag = sb("diag", [P, P])
            order = sb("order", [P, FC], I32)
            order_c = [sb(f"order_c{k}", [P, 1], I32) for k in range(2)]
            seg_i = sb("seg_i", [T, B * NG], I32)
            seg_k = sb("seg_k", [P, B * NT], I32)
            seg_f = sb("seg_f", [P, B * NT])
            row_c = sb("row_c", [P, 2])
            row_base = sb("row_base", [P, B * NT])

            key_ps = ps("key_ps", [P, 2, 1024])
            join_ps = ps("join_ps", [P, 512])
            ft_ps = ps("ft_ps", [P, 2048], BF16)
            sc_ps = ps("sc_ps", [T, 512])

            ctx_in = [sem(f"ctx_in{k}") for k in range(2)]
            key_mm = sem("key_mm")
            mean_mm = sem("mean_mm")
            kvc_out = sem("kvc_out")
            rope_out = sem("rope_out")
            mean_out = sem("mean_out")
            table_out = [sem(f"table_out{k}") for k in range(2)]
            join_mm = sem("join_mm")
            join_out = sem("join_out")
            ones_set = sem("ones_set")
            idx_set = sem("idx_set")
            raw_in = [sem(f"raw_in{k}") for k in range(2)]
            gathers = sem("gathers")
            raw_free = sem("raw_free")
            down_in = sem("down_in")
            ord_in = sem("ord_in")
            ord_c = sem("ord_c")
            inv_set = sem("inv_set")
            scaled = sem("scaled")
            quant = sem("quant")
            ft_mm = sem("ft_mm")
            ft_out = sem("ft_out")

            block = st.enter_context(nc.Block())
            KV_DMAS = 2 * 16

            def gather_rows(pool, c, half, first=False):
                if not first:
                    pool.wait_ge(raw_free, c - 1)
                    pool.sem_inc(gathers, 1)
                pool.tensor_copy(order_c[half][:], order[:, bass.ds(c, 1)]).then_inc(ord_c, 1)
                pool.wait_ge(ord_c, c + 1)
                pool.sem_inc(gathers, 1)
                for m, name in enumerate(("w_gate", "w_up")):
                    pool.indirect_dma_start(raw_gu[m][half][:], None, a[name],
                                            bass.IndirectOffsetOnAxis(order_c[half][:], 0)).then_inc(raw_in[half], 16)

            def keys_of(half):
                return key_ps[0:KROWS, half, 0:768].rearrange("p (k n) -> p k n", k=KTILES)

            @block.sync
            def _(sp):
                for t_, n_ in ((ident, "ident"), (identb, "identb"), (off_mask, "off_mask"), (rope_q, "rope_q"),
                               (rope_k, "rope_k"), (row_c, "row_c"), (row_base, "row_base"),
                               (seg_i, "seg_rows"), (seg_k, "seg_keys")):
                    sp.dma_start(t_[:], a[n_]).then_inc(consts_in, 16)
                sp.dma_start(wkvc_t[:], a["w_kvc_t"]).then_inc(weights_in, 16)
                sp.dma_start(wkr2[:], a["w_kr2"]).then_inc(weights_in, 16)
                sp.dma_start(wkvx[:, :, 0:P], a["w_kvc"]).then_inc(weights_in, 16)
                sp.dma_start(wuq_t[:], a["w_uq_t"]).then_inc(weights_in, 16)
                sp.dma_start(wuk_t[:], a["w_uk_t"]).then_inc(weights_in, 16)
                for half in range(2):
                    sp.dma_start(ctx_t[half][:], a["ctx_t"][half]).then_inc(ctx_in[half], 16)
                with sp.Fori(1, B // 2) as i:
                    for half in range(2):
                        b = 2 * i + half
                        sp.wait_ge(key_mm, b - 1)
                        sp.dma_start(ctx_t[half][:], a["ctx_t"][b]).then_inc(ctx_in[half], 16)
                sp.dma_start(x_all[:], a["x"].rearrange("b t d -> t b d")).then_inc(x_in, 16)
                sp.dma_start(wdq[:], a["w_dq"]).then_inc(xwq_in, 16)
                sp.dma_start(wqr[:], a["w_qr2"]).then_inc(xwq_in, 16)

            @block.gpsimd
            def _(pool):
                pool.memset(ones[:], 1.0).then_inc(ones_set, 1)
                pool.dma_start(order[:], a["order"]).then_inc(ord_in, 16)
                pool.wait_ge(ord_in, 16)
                for half in range(2):
                    gather_rows(pool, half, half, True)
                with pool.Fori(1, FC // 2) as i:
                    for half in range(2):
                        gather_rows(pool, 2 * i + half, half)
                gather_rows(pool, FC - 1, 0)
                with pool.Fori(0, DC) as n:
                    pool.wait_ge(quant, 2 * FC + n)
                    pool.dma_start(raw_d[:], a["w_down"][n]).then_inc(down_in, 16)

            @block.scalar
            def _(act):
                act.sem_inc(ft_out, 1)
                act.wait_ge(join_mm, 1)
                act.activation(wkvx[:, :, P:2 * P], join_ps[:].rearrange("p (c n) -> p c n", c=DC),
                               ACT.Copy).then_inc(join_out, 1)
                def keys(b, half, i, first=False):
                    act.wait_ge(key_mm, b + 1)
                    if not first:
                        act.wait_ge(table_out[half], i * KV_DMAS)
                    act.activation(key_rows[half][:, :, 0:KVC], keys_of(half)[:, :, 0:KVC],
                                   ACT.Copy).then_inc(kvc_out, 1)
                    act.wait_ge(mean_mm, b + 1)
                    act.activation(mean_row[half][:], key_ps[0:1, half, 768:768 + KW], ACT.Copy,
                                   scale=1.0 / LK).then_inc(mean_out, 1)
                    act.wait_ge(kvc_out, b + 1)
                    act.dma_start(table_rows[b, 0:LK].rearrange("(k p) n -> p k n", k=KTILES),
                                  key_rows[half][:]).then_inc(table_out[half], 16)
                    act.wait_ge(mean_out, b + 1)
                    act.dma_start(table_rows[b, LK:TROWS], mean_row[half][:]).then_inc(table_out[half], 16)

                for half in range(2):
                    keys(half, half, 0, True)
                with act.Fori(1, B // 2) as i:
                    for half in range(2):
                        keys(2 * i + half, half, i)
                for k in range(NH // 2):
                    act.wait_ge(join_mm, k + 2)
                    act.activation(wqn[:, :, 2 * k:2 * k + 2, :],
                                   join_ps[0:QH, :].rearrange("p (h j n) -> p j h n", h=2, j=2),
                                   ACT.Copy).then_inc(join_out, 1)

                def scale(n, w, width):
                    act.wait_ge(inv_set, n + 1)
                    act.activation(mag[:, 0:width], w, ACT.Copy, scale=inv[:, 1:2])
                    act.activation(summ[:, 0:width], w, ACT.Copy, scale=inv[:, 0:1]).then_inc(scaled, 1)

                def store_gu(c, half):
                    for m, (w, s) in enumerate(((gate_w, gate_s), (up_w, up_s))):
                        scale(2 * c + m, raw_gu[m][half][:], D)
                        act.wait_ge(ft_mm, 2 * c + m + 2)
                        act.activation(w[:, :, bass.ds(c * P, P)],
                                       ft_ps[:, 0:D].rearrange("p (h n) -> p h n", h=DC), ACT.Copy)
                        act.activation(s[:, bass.ds(c * P, P)], sc_ps[:, 0:P], ACT.Copy).then_inc(ft_out, 1)

                with act.Fori(0, FC // 2) as i:
                    for half in range(2):
                        store_gu(2 * i + half, half)
                store_gu(FC - 1, 0)
                with act.Fori(0, DC) as n:
                    scale(2 * FC + n, raw_d[:], F)
                    act.wait_ge(ft_mm, 2 * FC + n + 2)
                    act.activation(down_w[:, :, bass.ds(n * P, P)],
                                   ft_ps[:, 0:F].rearrange("p (h n) -> p h n", h=FC), ACT.Copy)
                    act.activation(down_s[:, bass.ds(n * P, P)], sc_ps[:, 0:P], ACT.Copy).then_inc(ft_out, 1)
                for half in range(2):
                    act.wait_ge(table_out[half], B // 2 * KV_DMAS)

            @block.tensor
            def _(pe):
                pe.sem_inc(ft_mm, 1)
                pe.wait_ge(weights_in, 16 * 5)
                for c in range(DC):
                    mm = pe.matmul(join_ps[:, c * P:(c + 1) * P], wkvc_t[:, c * P:(c + 1) * P], wkr2[:],
                                   start=True, stop=True)
                mm.then_inc(join_mm, 1)
                pe.wait_ge(join_out, 1)
                pe.wait_ge(ones_set, 1)
                with pe.Fori(0, B // 2) as i:
                    for half in range(2):
                        b = 2 * i + half
                        pe.wait_ge(ctx_in[half], 16 * (i + 1))
                        for k in range(KTILES):
                            for c in range(DC):
                                mm = pe.matmul(key_ps[0:KROWS, half, k * 256:(k + 1) * 256],
                                               ctx_t[half][:, c, k * KROWS:(k + 1) * KROWS], wkvx[:, c, :],
                                               start=(c == 0), stop=(c == DC - 1))
                        mm.then_inc(key_mm, 1)
                        pe.wait_ge(kvc_out, b + 1)
                        pe.wait_ge(rope_out, b + 1)
                        for k in range(KTILES):
                            mm = pe.matmul(key_ps[0:1, half, 768:768 + KW], ones[0:KROWS, 0:1],
                                           key_rows[half][:, k, :], start=(k == 0), stop=(k == KTILES - 1))
                        mm.then_inc(mean_mm, 1)
                for k in range(NH // 2):
                    pe.wait_ge(join_out, k + 1)
                    for h in range(2):
                        for j in range(2):
                            n = 2 * h + j
                            mm = pe.matmul(join_ps[0:QH, n * P:(n + 1) * P],
                                           wuq_t[:, 2 * k + h, j * QH:(j + 1) * QH], wuk_t[:, 2 * k + h, :],
                                           start=True, stop=True)
                    mm.then_inc(join_mm, 1)
                pe.wait_ge(consts_in, 16 * 9)

                def turn_tile(n, chunks):
                    pe.wait_ge(quant, n + 1)
                    pe.wait_ge(ft_out, n + 1)
                    for h in range(chunks):
                        pe.transpose(ft_ps[:, h * P:(h + 1) * P], qt[:, h * P:(h + 1) * P], identb[:])
                    pe.matmul(sc_ps[:, 0:P], ones[:, 0:T], diag[:], start=True, stop=True).then_inc(ft_mm, 1)

                with pe.Fori(0, FC) as c:
                    for m in range(2):
                        turn_tile(2 * c + m, DC)
                with pe.Fori(0, DC) as n:
                    turn_tile(2 * FC + n, FC)

            @block.vector
            def _(dve):
                dve.wait_ge(consts_in, 16 * 9)
                chain(dve.tensor_copy(seg_f[:], seg_k[:]))
                chain(dve.tensor_scalar(seg_f[:], seg_f[:], row_c[:, 0:1], 0.0, ALU.add, ALU.max))
                chain(dve.tensor_scalar(seg_f[:], seg_f[:], float(LK - 1), row_c[:, 1:2], ALU.min, ALU.mult))
                chain(dve.tensor_tensor(row_idx[:], seg_f[:], row_base[:], ALU.add))
                chain(dve.tensor_copy(seg_rows[:], seg_i[:]))
                start = chain.value

                def rotate_keys(b, half, i, first=False):
                    chain.turn(start, b, 1)
                    dve.wait_ge(key_mm, b + 1)
                    if not first:
                        dve.wait_ge(table_out[half], i * KV_DMAS)
                    dve.wait_ge(kvc_out, b + 1)
                    chain(dve.tensor_tensor(rot[:], keys_of(half)[:, :, KVC:KVC + 2 * ROPE], rope_k[:], ALU.mult))
                    for n in (KVC, KVC + ROPE):
                        last = dve.tensor_tensor(key_rows[half][:, :, n:n + ROPE], rot[:, :, 0:ROPE],
                                                 rot[:, :, ROPE:2 * ROPE], ALU.add)
                    last.then_inc(rope_out, 1)

                for half in range(2):
                    rotate_keys(half, half, 0, True)
                with dve.Fori(1, B // 2) as i:
                    for half in range(2):
                        rotate_keys(2 * i + half, half, i)
                chain.turned(start, B, 1)

                PER = 5

                def quantise(n, w, width, free=None):
                    chain(dve.tensor_reduce(amax[:], w, AX.X, ALU.max, apply_absolute_value=True))
                    chain(dve.tensor_scalar(wsc[:], amax[:], 1.0 / FP8_MAX, None, ALU.mult))
                    chain(dve.reciprocal(inv[:, 0:1], wsc[:]))
                    dve.tensor_scalar(inv[:, 1:2], inv[:, 0:1], 2.0 ** 20, None, ALU.mult).then_inc(inv_set, 1)
                    dve.wait_ge(ft_mm, n + 1)
                    dve.tensor_scalar(diag[:], ident[:], wsc[:, 0:1], None, ALU.mult)
                    dve.wait_ge(scaled, n + 1)
                    if free is not None:
                        dve.nop().then_inc(free, 1)
                    chain(magic_bits(dve, mag_u[:, 0:width]))
                    chain(magic_add(dve, summ[:, 0:width], mag[:, 0:width]))
                    magic_sub(dve, qt[:, 0:width], summ[:, 0:width], mag[:, 0:width]).then_inc(quant, 1)

                start = chain.value
                with dve.Fori(0, FC // 2) as i:
                    for half in range(2):
                        c = 2 * i + half
                        dve.wait_ge(raw_in[half], 32 * (i + 1))
                        for m in range(2):
                            chain.turn(start, 2 * c + m, PER)
                            quantise(2 * c + m, raw_gu[m][half][:], D, raw_free if m else None)
                dve.wait_ge(raw_in[0], 32 * (FC // 2 + 1))
                for m in range(2):
                    chain.turn(start, 2 * (FC - 1) + m, PER)
                    quantise(2 * (FC - 1) + m, raw_gu[m][0][:], D, raw_free if m else None)
                with dve.Fori(0, DC) as n:
                    dve.wait_ge(down_in, 16 * (n + 1))
                    chain.turn(start, 2 * FC + n, PER)
                    quantise(2 * FC + n, raw_d[:], F)
                chain.turned(start, 2 * FC + DC, PER)


        with ExitStack() as st:
            def sb(name, shape, dt=F32):
                return st.enter_context(nc.sbuf_tensor(name, shape, dt))

            def ps(name, shape, dt=F32):
                return st.enter_context(nc.psum_tensor(name, shape, dt))

            w_in = [sb(f"w_in{m}", [P, DC, D]) for m in range(5)]
            w_out = sb("w_out", [P, DC, D])
            x_t = [sb(f"x_t{k}", [P, DC, T]) for k in range(2)]
            qk = [[sb(f"qk{m}{k}", [P, NJ, T]) for k in range(2)] for m in range(4)]
            v = [sb(f"v{k}", [T, D]) for k in range(2)]
            prob = [sb(f"prob{k}", [T, HG, 2, T]) for k in range(2)]
            att = [sb(f"att{k}", [T, HG, T]) for k in range(2)]
            att_t = [sb(f"att_t{k}", [T, HG, T]) for k in range(2)]
            o_t = sb("o_t", [P, NJ, T])
            lam = sb("lam", [T, NJ, HG])
            smax = sb("smax", [T, HG, 2])
            ssum = sb("ssum", [T, HG, 2])
            sinv = sb("sinv", [T, HG, 2])

            proj_ps = ps("proj_ps", [P, 2, 512])
            score_ps = ps("score_ps", [T, HG, 512])
            att_ps = ps("att_ps", [T, 512])
            o_ps = ps("o_ps", [P, 512])

            w_sem = [sem(f"w_sem{m}") for m in range(6)]
            lam_in = sem("lam_in")
            xt_in = [sem(f"xt_in{k}") for k in range(2)]
            proj_mm = sem("proj_mm")
            proj_out = sem("proj_out")
            score_mm = sem("score_mm")
            score_sub = sem("score_sub")
            prob_exp = sem("prob_exp")
            att_set = sem("att_set")
            att_turn = sem("att_turn")
            att_out = sem("att_out")
            pv_mm = sem("pv_mm")
            o_out = sem("o_out")
            y_mm = sem("y_mm")
            y_out = sem("y_out")

            block = st.enter_context(nc.Block())

            def v_count(b):
                return 5 * (b + 1)

            @block.sync
            def _(sp):
                for k in range(2):
                    sp.dma_start(x_t[k][:], a["x_t"][k]).then_inc(xt_in[k], 16)
                for m, name in enumerate(("w_q1", "w_k1", "w_q2", "w_k2", "w_v")):
                    sp.dma_start(w_in[m][:], a[name]).then_inc(w_sem[m], 16)
                sp.dma_start(w_out[:], a["w_attn_o"]).then_inc(w_sem[5], 16)
                sp.dma_start(lam[:], a["lam"]).then_inc(lam_in, 16)
                with sp.Fori(1, B // 2) as i:
                    for half in range(2):
                        b = 2 * i + half
                        sp.wait_ge(proj_mm, v_count(b - 2))
                        sp.dma_start(x_t[half][:], a["x_t"][b]).then_inc(xt_in[half], 16)

            @block.tensor
            def _(pe):
                def project(b, half, i, m, bank):
                    if m == 0:
                        pe.wait_ge(xt_in[half], 16 * (i + 1))
                    for j in range(NJ):
                        if m == 4:
                            break
                        for c in range(DC):
                            mm = pe.matmul(proj_ps[:, bank, j * T:(j + 1) * T], w_in[m][:, c, j * P:(j + 1) * P],
                                           x_t[half][:, c, :], start=(c == 0), stop=(c == DC - 1))
                    if m == 4:
                        for c in range(DC):
                            mm = pe.matmul(proj_ps[0:T, bank, :], x_t[half][:, c, :], w_in[4][:, c, :],
                                           start=(c == 0), stop=(c == DC - 1))
                    mm.then_inc(proj_mm, 1)

                for m in range(5):
                    pe.wait_ge(w_sem[m], 16)
                    if m >= 2:
                        pe.wait_ge(proj_out, m - 1)
                    project(0, 0, 0, m, m % 2)
                pe.wait_ge(w_sem[5], 16)

                def scores(b, half, j):
                    if j == 0:
                        pe.wait_ge(proj_out, 5 * b + 5)
                    pe.wait_ge(score_sub, 4 * b + j + 1)
                    for s in range(2):
                        for r in range(HG):
                            rows = slice(r * HD, (r + 1) * HD)
                            mm = pe.matmul(score_ps[:, r, s * T:(s + 1) * T], qk[2 * s][half][rows, j, :],
                                           qk[2 * s + 1][half][rows, j, :], start=True, stop=True)
                    mm.then_inc(score_mm, 1)

                def turn(b, j):
                    pe.wait_ge(att_set, 4 * b + j + 1)
                    pe.wait_ge(att_out, 4 * b + j + 1)
                    for r in range(HG):
                        mm = pe.transpose(att_ps[:, r * T:(r + 1) * T], att[j % 2][:, r, :], ident[0:T, 0:T])
                    mm.then_inc(att_turn, 1)

                def heads_out(b, half, j):
                    pe.wait_ge(att_out, 4 * b + j + 2)
                    for r in range(HG):
                        h = HG * j + r
                        mm = pe.matmul(o_ps[r * HD:(r + 1) * HD, j * T:(j + 1) * T],
                                       v[half][:, h * HD:(h + 1) * HD], att_t[j % 2][:, r, :],
                                       start=True, stop=True)
                    if j == NJ - 1:
                        mm.then_inc(pv_mm, 1)

                def batch(b, half, i, last):
                    def ahead(m):
                        if last:
                            return
                        if m == 0:
                            pe.wait_ge(proj_out, 5 * b + 5)
                        elif m == 1:
                            pe.wait_ge(y_out, b + 1)
                        else:
                            pe.wait_ge(proj_out, 5 * b + 5 + m - 1)
                        project(b + 1, 1 - half, i + half, m, (m + 1) % 2)

                    scores(b, half, 0)
                    ahead(0)
                    scores(b, half, 1)
                    turn(b, 0)
                    ahead(1)
                    scores(b, half, 2)
                    heads_out(b, half, 0)
                    turn(b, 1)
                    ahead(2)
                    scores(b, half, 3)
                    heads_out(b, half, 1)
                    turn(b, 2)
                    ahead(3)
                    heads_out(b, half, 2)
                    turn(b, 3)
                    ahead(4)
                    heads_out(b, half, 3)
                    pe.wait_ge(o_out, b + 1)
                    if last:
                        pe.wait_ge(y_out, b + 1)
                    else:
                        pe.wait_ge(proj_out, 5 * b + 9)
                    for j in range(NJ):
                        mm = pe.matmul(proj_ps[0:T, 0, :], o_t[:, j, :], w_out[:, j, :],
                                       start=(j == 0), stop=(j == NJ - 1))
                    mm.then_inc(y_mm, 1)

                with pe.Fori(0, B // 2 - 1) as i:
                    for half in range(2):
                        batch(2 * i + half, half, i, False)
                batch(B - 2, 0, B // 2 - 1, False)
                batch(B - 1, 1, B // 2 - 1, True)

            @block.scalar
            def _(act):
                def store(b, half, m, bank):
                    act.wait_ge(proj_mm, 5 * b + m + 1)
                    if m == 4:
                        act.activation(v[half][:], proj_ps[0:T, bank, :], ACT.Copy).then_inc(proj_out, 1)
                    else:
                        act.activation(qk[m][half][:], proj_ps[:, bank, 0:NJ * T].rearrange("p (j t) -> p j t", j=NJ),
                                       ACT.Copy, scale=1.0 if m % 2 else HD ** -0.5).then_inc(proj_out, 1)

                def exp(b, j):
                    act.wait_ge(score_sub, 4 * b + j + 2)
                    act.activation(prob[j % 2][:], prob[j % 2][:], ACT.Exp).then_inc(prob_exp, 1)

                def store_att(b, j):
                    act.wait_ge(att_turn, 4 * b + j + 1)
                    act.activation(att_t[j % 2][:], att_ps[:, 0:HG * T].rearrange("p (r t) -> p r t", r=HG),
                                   ACT.Copy).then_inc(att_out, 1)

                act.sem_inc(att_out, 1)
                for m in range(5):
                    store(0, 0, m, m % 2)

                def batch(b, half, last):
                    def ahead(m):
                        if not last:
                            store(b + 1, 1 - half, m, (m + 1) % 2)

                    exp(b, 0)
                    ahead(0)
                    exp(b, 1)
                    store_att(b, 0)
                    ahead(1)
                    exp(b, 2)
                    store_att(b, 1)
                    ahead(2)
                    exp(b, 3)
                    store_att(b, 2)
                    ahead(3)
                    store_att(b, 3)
                    ahead(4)
                    act.wait_ge(pv_mm, b + 1)
                    act.activation(o_t[:], o_ps[:, 0:NJ * T].rearrange("p (j t) -> p j t", j=NJ),
                                   ACT.Copy).then_inc(o_out, 1)

                with act.Fori(0, B // 2 - 1) as i:
                    for half in range(2):
                        batch(2 * i + half, half, False)
                batch(B - 2, 0, False)
                batch(B - 1, 1, True)
                act.wait_ge(var_set, 1)
                act.activation(rstd[:], rstd[:], ACT.Sqrt).then_inc(std_set, 1)

            @block.vector
            def _(dve):
                def shift(b, j):
                    dve.wait_ge(score_mm, 4 * b + j + 1)
                    s = score_ps[:, :, 0:2 * T].rearrange("p r (s k) -> p r s k", s=2)
                    chain(dve.tensor_reduce(smax[:], s, AX.X, ALU.max))
                    dve.tensor_tensor(prob[j % 2][:], s, smax[:].unsqueeze(3).broadcast_to([T, HG, 2, T]),
                                      ALU.subtract).then_inc(score_sub, 1)

                def combine(b, j):
                    p = prob[j % 2]
                    dve.wait_ge(prob_exp, 4 * b + j + 1)
                    chain(dve.tensor_reduce(ssum[:], p[:], AX.X, ALU.add))
                    chain(dve.reciprocal(sinv[:], ssum[:]))
                    chain(dve.tensor_tensor(sinv[:, :, 1], sinv[:, :, 1], lam[:, j, :], ALU.mult))
                    chain(dve.tensor_tensor(p[:], p[:], sinv[:].unsqueeze(3).broadcast_to([T, HG, 2, T]), ALU.mult))
                    dve.tensor_tensor(att[j % 2][:], p[:, :, 0, :], p[:, :, 1, :], ALU.subtract).then_inc(att_set, 1)

                def add_y(b):
                    dve.wait_ge(y_mm, b + 1)
                    x_b = x_all[:, b, :]
                    chain(dve.tensor_tensor(x_b, x_b, proj_ps[0:T, 0, :], ALU.add))
                    dve.nop().then_inc(y_out, 1)
                    chain(dve.bn_stats(stats[:, b, :], x_b))

                def batch(b):
                    shift(b, 0)
                    shift(b, 1)
                    combine(b, 0)
                    shift(b, 2)
                    combine(b, 1)
                    shift(b, 3)
                    combine(b, 2)
                    combine(b, 3)
                    add_y(b)

                dve.sem_inc(score_sub, 1)
                dve.sem_inc(y_out, 1)
                PER = NJ * 5 + 2
                dve.wait_ge(lam_in, 16)
                dve.wait_ge(x_in, 16)
                start = chain.value
                with dve.Fori(0, B) as b:
                    chain.turn(start, b, PER)
                    batch(b)
                chain.turned(start, B, PER)
                layer_norm(dve, 1)

        with ExitStack() as st:
            def sb(name, shape, dt=F32):
                return st.enter_context(nc.sbuf_tensor(name, shape, dt))

            def ps(name, shape, dt=F32):
                return st.enter_context(nc.psum_tensor(name, shape, dt))

            wvo = sb("wvo", [P, NH, D])
            q_all = sb("q_all", [P, 2, T, NH])
            wuv_t = q_all[:].rearrange("p a t h -> p (a t h)")[:, 0:NH * KVC].rearrange("p (h c) -> p h c", h=NH)
            k_t = sb("k_t", [P, 2, NG * GK])
            rows_kv = [sb(f"rows_kv{k}", [P, NT, KW]) for k in range(2)]
            x_b = sb("x_b", [T, D])
            xb_t = sb("xb_t", [P, DC, T])
            qc_t = sb("qc_t", [QH, 2, T])
            prob = sb("xprob", [T, NG, GK])
            outside = sb("outside", [T, NG, GK], BF16)
            prob_t = sb("prob_t", [P, NT, T])
            oc_t = sb("oc_t", [P, NG, GQ, NH])
            idx_b = [sb(f"idx_b{k}", [P, NT], I32) for k in range(2)]
            windowed = sb("windowed", [T, B * NG])
            xmax = sb("xmax", [T, NG])
            xsum = sb("xsum", [T, NG])

            RING = 5
            ring = ps("ring", [P, RING, 512])
            s_ps = ps("s_ps", [T, NG * GK])
            y_ps = ps("y_ps", [T, 512])

            uvw_in = sem("uvw_in")
            rows_in = [sem(f"rows_in{k}") for k in range(2)]
            idx_out = sem("idx_out")
            idx_go = sem("idx_go")
            xb_out = sem("xb_out")
            vo_mm = sem("vo_mm")
            vo_out = sem("vo_out")
            fill = sem("fill")
            drain_act = sem("drain_act")
            drain_dve = sem("drain_dve")
            s_mm = sem("s_mm")
            s_sub = sem("s_sub")
            s_exp = sem("s_exp")
            p_set = sem("p_set")
            y2_mm = sem("y2_mm")
            y2_out = sem("y2_out")

            LEAD = "AA" + "AAAA" + "DDDD" + "AAAA"
            TAIL = "AA" + "AAAA"
            PERIOD = len(LEAD) + len(TAIL)
            A_PER, D_PER = (LEAD + TAIL).count("A"), (LEAD + TAIL).count("D")
            ORDER = LEAD + (LEAD + TAIL) * 3

            def lead_at(ahead, m):
                return len(LEAD) + m if ahead else m

            def tail_at(m, last=False):
                return (1 if last else 2) * len(LEAD) + m

            def drained(n, who):
                return ORDER[:n + 1].count(who)

            def s_ps_bank(h):
                return ring[:, h % 2, :]

            block = st.enter_context(nc.Block())

            @block.sync
            def _(sp):
                sp.dma_start(wuv_t, a["w_uv_t"]).then_inc(uvw_in, 16)
                sp.dma_start(wvo[:], a["w_o"]).then_inc(uvw_in, 16)

            @block.gpsimd
            def _(pool):
                def fetch(b, half, first=False):
                    if not first:
                        pool.wait_ge(fill, (b - 2) * PERIOD + tail_at(5) + 1)
                        pool.sem_inc(idx_go, 1)
                    pool.tensor_copy(idx_b[half][:], row_idx[:, bass.ds(b * NT, NT)]).then_inc(idx_out, 1)
                    pool.wait_ge(idx_out, b + 1)
                    pool.sem_inc(idx_go, 1)
                    for t in range(NT):
                        pool.indirect_dma_start(rows_kv[half][:, t, :], None, table[:],
                                                bass.IndirectOffsetOnAxis(idx_b[half][:, t:t + 1], 0))\
                            .then_inc(rows_in[half], 16)

                def copy_x(b):
                    pool.tensor_copy(x_b[:], x_all[:, b, :]).then_inc(xb_out, 1)

                pool.tensor_copy(x_b[:], x_all[:, 0, :]).then_inc(xb_out, 1)
                for half in range(2):
                    fetch(half, half, True)

                pool.wait_ge(fill, 1)
                copy_x(1)
                with pool.Fori(1, B // 2) as i:
                    for half in range(2):
                        b = 2 * i + half
                        pool.wait_ge(fill, (b - 1) * PERIOD - len(TAIL) + 1)
                        pool.sem_inc(idx_go, 1)
                        copy_x(b)
                        fetch(b, half)

            @block.tensor
            def _(pe):
                def ring_free(b, n):
                    if n >= RING:
                        pe.wait_ge(drain_act, b * A_PER + drained(n - RING, "A"))
                        if drained(n - RING, "D"):
                            pe.wait_ge(drain_dve, b * D_PER + drained(n - RING, "D"))

                def lead(b, half, i, ahead):
                    def bank(m):
                        ring_free(b, lead_at(ahead, m))
                        return ring[:, lead_at(ahead, m) % RING, :]

                    r = bank(0)
                    pe.wait_ge(xb_out, b + ahead + 1)
                    for c in range(DC):
                        mm = pe.transpose(r[:, c * T:(c + 1) * T], x_b[:, c * P:(c + 1) * P], ident[0:T, 0:T])
                    mm.then_inc(fill, 1)
                    r = bank(1)
                    pe.wait_ge(drain_act, b * A_PER + drained(lead_at(ahead, 0), "A"))
                    for j in range(2):
                        for c in range(DC):
                            mm = pe.matmul(r[0:QH, j * T:(j + 1) * T], wdq[:, c, j * QH:(j + 1) * QH], xb_t[:, c, :],
                                           start=(c == 0), stop=(c == DC - 1))
                    mm.then_inc(fill, 1)
                    for part, w in enumerate((wqn, wqr)):
                        for k in range(4):
                            r = bank(2 + 4 * part + k)
                            pe.wait_ge(drain_act, b * A_PER + drained(lead_at(ahead, 1), "A"))
                            for h in range(4):
                                for j in range(2):
                                    mm = pe.matmul(r[:, h * T:(h + 1) * T], w[:, j, 4 * k + h, :], qc_t[:, j, :],
                                                   start=(j == 0), stop=(j == 1))
                            mm.then_inc(fill, 1)
                    pe.wait_ge(rows_in[half], 16 * NT * (i + 1))
                    for k in range(4):
                        r = bank(10 + k)
                        for t in range(4):
                            rows = rows_kv[half][:, 4 * (k % 2) + t, :]
                            src = rows[:, 0:KVC] if k < 2 else rows[:, KVC:KW]
                            mm = pe.transpose(r[:, t * P:(t + 1) * P], src, ident[:])
                        mm.then_inc(fill, 1)

                def scores(b, n):
                    pe.wait_ge(drain_act, b * A_PER + drained(n, "A"))
                    pe.wait_ge(drain_dve, b * D_PER + drained(n, "D"))
                    for g in range(NG):
                        for part in range(2):
                            q = q_all[:, part, g * GQ:(g + 1) * GQ, :].rearrange("p q h -> p (q h)")
                            mm = pe.matmul(s_ps[:, g * GK:(g + 1) * GK], q, k_t[:, part, g * GK:(g + 1) * GK],
                                           start=(part == 0), stop=(part == 1))
                    mm.then_inc(s_mm, 1)

                def tail(b, half, last):
                    def bank(m):
                        ring_free(b, tail_at(m, last))
                        return ring[:, tail_at(m, last) % RING, :]

                    pe.wait_ge(p_set, b + 1)
                    flat = prob[:].rearrange("p g k -> p (g k)")
                    for k in range(2):
                        r = bank(k)
                        for t in range(4):
                            n = 4 * k + t
                            mm = pe.transpose(r[:, t * T:(t + 1) * T], flat[:, n * P:(n + 1) * P], ident[0:T, 0:T])
                        mm.then_inc(fill, 1)
                    for k in range(2):
                        even, odd = bank(2 + 2 * k), bank(3 + 2 * k)
                        pe.wait_ge(drain_act, b * A_PER + drained(tail_at(k, last), "A"))
                        for t in range(4):
                            n = 4 * k + t
                            for r, rows in ((even, slice(0, GK)), (odd, slice(GK, P))):
                                mm = pe.matmul(r[:, t * T:(t + 1) * T], rows_kv[half][rows, n, 0:KVC],
                                               prob_t[rows, n, :], start=True, stop=True)
                                if t == 3:
                                    mm.then_inc(fill, 1)
                    pe.wait_ge(drain_act, b * A_PER + drained(tail_at(5, last), "A"))
                    pe.wait_ge(y2_out, b + 1)
                    for h in range(NH):
                        mm = pe.matmul(y_ps[:], oc_t[:].rearrange("p g q h -> p (g q) h")[:, :, h], wvo[:, h, :],
                                       start=(h == 0), stop=(h == NH - 1))
                    mm.then_inc(y2_mm, 1)

                pe.wait_ge(uvw_in, 32)
                for h in range(NH):
                    if h >= 2:
                        pe.wait_ge(vo_out, h - 1)
                    pe.matmul(s_ps_bank(h), wuv_t[:, h, :], wvo[:, h, :], start=True, stop=True).then_inc(vo_mm, 1)
                pe.wait_ge(vo_out, NH)
                lead(0, 0, 0, 0)
                with pe.Fori(0, B // 2 - 1) as i:
                    for half in range(2):
                        b = 2 * i + half
                        scores(b, len(LEAD) - 1)
                        lead(b, 1 - half, i + half, 1)
                        tail(b, half, False)
                for b in (B - 2, B - 1):
                    scores(b, len(LEAD) - 1)
                    if b == B - 2:
                        lead(b, 1, B // 2 - 1, 1)
                    tail(b, b % 2, b == B - 1)

            @block.scalar
            def _(act):
                def store(b, n, dst, rows=P, width=512, scale=1.0, **kw):
                    src = ring[0:rows, n % RING, 0:width]
                    if kw:
                        src = src.rearrange("p (u v) -> p u v", **kw)
                    act.wait_ge(fill, b * PERIOD + n + 1)
                    act.activation(dst, src, ACT.Copy, scale=scale).then_inc(drain_act, 1)

                def lead_head(b, ahead):
                    store(b, lead_at(ahead, 0), xb_t[:], width=DC * T, u=DC)
                    store(b, lead_at(ahead, 1), qc_t[:], rows=QH, width=2 * T, scale=(XHD + ROPE) ** -0.5, u=2)

                def lead_rest(b, ahead):
                    for k in range(4):
                        store(b, lead_at(ahead, 2 + k), q_all[:, 0, :, 4 * k:4 * k + 4].rearrange("p t h -> p h t"), width=4 * T, u=4)
                    for k in range(4):
                        store(b, lead_at(ahead, 10 + k), k_t[:, k // 2, (k % 2) * 512:(k % 2 + 1) * 512])

                def exp(b):
                    act.wait_ge(s_sub, b + 1)
                    act.activation(prob[:], prob[:], ACT.Exp).then_inc(s_exp, 1)

                def tail(b, last):
                    for k in range(2):
                        store(b, tail_at(k, last), prob_t[:, 4 * k:4 * k + 4, :], width=4 * T, u=4)
                    oc = oc_t[:].rearrange("p (s e) q h -> p s e (q h)", e=2)
                    for k in range(2):
                        for odd in range(2):
                            store(b, tail_at(2 + 2 * k + odd, last), oc[:, 4 * k:4 * k + 4, odd, :], width=4 * T, u=4)

                for h in range(NH):
                    act.wait_ge(vo_mm, h + 1)
                    act.activation(wvo[:, h, :], s_ps_bank(h), ACT.Copy).then_inc(vo_out, 1)
                lead_head(0, 0)
                lead_rest(0, 0)

                def batch(b, last):
                    if not last:
                        lead_head(b, 1)
                    exp(b)
                    if not last:
                        lead_rest(b, 1)
                    tail(b, last)

                with act.Fori(0, B - 1) as b:
                    batch(b, False)
                batch(B - 1, True)
                act.wait_ge(var_set, 2)
                act.activation(rstd[:], rstd[:], ACT.Sqrt).then_inc(std_set, 1)

            @block.vector
            def _(dve):
                def rotate(b, ahead, k):
                    n = lead_at(ahead, 6 + k)
                    dve.wait_ge(fill, b * PERIOD + n + 1)
                    dve.tensor_tensor(q_all[:, 1, :, 4 * k:4 * k + 4].rearrange("p t h -> p h t"),
                                      ring[:, n % RING, 0:4 * T].rearrange("p (h t) -> p h t", h=4),
                                      rope_q[:].unsqueeze(1).broadcast_to([P, 4, T]), ALU.mult).then_inc(drain_dve, 1)

                def window(b):
                    segs = seg_rows[:, bass.ds(b * NG, NG)]
                    chain(dve.tensor_tensor(prob[:], segs.unsqueeze(2).broadcast_to([T, NG, GK]),
                                            off_mask[:].unsqueeze(1).broadcast_to([T, NG, GK]), ALU.add))
                    chain(dve.tensor_scalar(outside[:], prob[:], 0.0, None, ALU.is_lt))
                    chain(dve.scalar_tensor_tensor(outside[:], prob[:], float(LK - 1), outside[:], ALU.is_gt, ALU.max))
                    chain(dve.tensor_copy(outside[:, :, GK - 1], windowed[:, bass.ds(b * NG, NG)]))

                def shift(b):
                    dve.wait_ge(s_mm, b + 1)
                    chain(dve.scalar_tensor_tensor(prob[:], outside[:], NEG,
                                                   s_ps[:].rearrange("p (g k) -> p g k", g=NG), ALU.mult, ALU.add))
                    chain(dve.tensor_reduce(xmax[:], prob[:], AX.X, ALU.max))
                    dve.tensor_tensor(prob[:], prob[:], xmax[:].unsqueeze(2).broadcast_to([T, NG, GK]),
                                      ALU.subtract).then_inc(s_sub, 1)

                def normalise(b):
                    dve.wait_ge(s_exp, b + 1)
                    chain(dve.tensor_reduce(xsum[:], prob[:], AX.X, ALU.add))
                    chain(dve.reciprocal(xsum[:], xsum[:]))
                    dve.tensor_tensor(prob[:], prob[:], xsum[:].unsqueeze(2).broadcast_to([T, NG, GK]),
                                      ALU.mult).then_inc(p_set, 1)

                def add_y(b):
                    dve.wait_ge(y2_mm, b + 1)
                    x = x_all[:, b, :]
                    chain(dve.tensor_tensor(x, x, y_ps[:], ALU.add))
                    dve.nop().then_inc(y2_out, 1)
                    chain(dve.bn_stats(stats[:, b, :], x))

                def batch(b, last):
                    window(b)
                    shift(b)
                    if not last:
                        rotate(b, 1, 0)
                        rotate(b, 1, 1)
                    normalise(b)
                    if not last:
                        rotate(b, 1, 2)
                        rotate(b, 1, 3)
                    add_y(b)

                dve.sem_inc(y2_out, 1)
                chain(dve.tensor_scalar(windowed[:], seg_rows[:], 0.0, None, ALU.is_ge))
                chain(dve.scalar_tensor_tensor(windowed[:], seg_rows[:], float(LK - 1 + SPAN - 1), windowed[:],
                                               ALU.is_le, ALU.mult))
                for k in range(4):
                    rotate(0, 0, k)
                start = chain.value
                PER = 4 + 2 + 2 + 2
                with dve.Fori(0, B - 1) as b:
                    chain.turn(start, b, PER)
                    batch(b, False)
                chain.turn(start, B - 1, PER)
                batch(B - 1, True)
                chain.turned(start, B, PER)
                layer_norm(dve, 2)

        with ExitStack() as st:
            def sb(name, shape, dt=F32):
                return st.enter_context(nc.sbuf_tensor(name, shape, dt))

            def ps(name, shape, dt=F32):
                return st.enter_context(nc.psum_tensor(name, shape, dt))

            xy = sb("xy", [T, D])
            xmag = sb("xmag", [T, D])
            xq = sb("xq", [T, D], BF16)
            xq_t = sb("xq_t", [P, DC, T], BF16)
            gate = sb("gate", [T, 2, 512])
            upv = sb("upv", [T, 2, 512])
            hid = sb("hid", [T, F])
            hy = sb("hy", [T, F])
            hmag = sb("hmag", [T, F])
            hq = sb("hq", [T, F], BF16)
            hq_t = sb("hq_t", [P, FC, T], BF16)
            ysum = sb("ysum", [T, D])
            xs = [sb(f"xs{k}", [T, 4]) for k in range(2)]
            hs = [sb(f"hs{k}", [T, 4]) for k in range(2)]

            gu_ps = ps("gu_ps", [T, 2, 2, 512])
            xt_ps = ps("xt_ps", [P, 1024], BF16)
            ht_ps = ps("ht_ps", [P, 2048], BF16)
            y3_ps = ps("y3_ps", [T, 512])

            xinv_set = sem("xinv_set")
            x_scaled = sem("x_scaled")
            xq_set = sem("xq_set")
            xt_mm = sem("xt_mm")
            xt_out = sem("xt_out")
            gu_mm = sem("gu_mm")
            gu_out = sem("gu_out")
            gate_set = sem("gate_set")
            silu_out = sem("silu_out")
            hinv_set = sem("hinv_set")
            h_scaled = sem("h_scaled")
            hq_set = sem("hq_set")
            ht_mm = sem("ht_mm")
            ht_out = sem("ht_out")
            y3_mm = sem("y3_mm")
            y3_out = sem("y3_out")
            normed = sem("normed")
            stored = sem("stored")

            NCH = len(FCH)
            block = st.enter_context(nc.Block())

            @block.sync
            def _(sp):
                for b in range(B):
                    sp.wait_ge(normed, b + 1)
                    sp.dma_start(out[b], x_all[:, b, :]).then_inc(stored, 16)
                sp.wait_ge(stored, 16 * B)

            @block.tensor
            def _(pe):
                def turn_x(b):
                    pe.wait_ge(xq_set, b + 1)
                    for c in range(DC):
                        mm = pe.transpose(xt_ps[:, c * P:c * P + T], xq[:, c * P:(c + 1) * P], identb[0:T, 0:T])
                    mm.then_inc(xt_mm, 1)

                def gate_up(b, half):
                    pe.wait_ge(xt_out, b + 1)
                    for n, (at, width) in enumerate(FCH):
                        pe.wait_ge(gu_out, NCH * b + n + 1)
                        for m, w in enumerate((gate_w, up_w)):
                            for c in range(DC):
                                mm = pe.matmul(gu_ps[:, (NCH * half + n) % 2, m, 0:width], xq_t[:, c, :],
                                               w[:, c, at:at + width], start=(c == 0), stop=(c == DC - 1))
                        mm.then_inc(gu_mm, 1)

                def batch(b, half, last):
                    gate_up(b, half)
                    pe.wait_ge(hq_set, b + 1)
                    for c in range(FC):
                        mm = pe.transpose(ht_ps[:, c * P:c * P + T], hq[:, c * P:(c + 1) * P], identb[0:T, 0:T])
                    mm.then_inc(ht_mm, 1)
                    if not last:
                        turn_x(b + 1)
                    pe.wait_ge(ht_out, b + 1)
                    pe.wait_ge(y3_out, b + 1)
                    for c in range(FC):
                        mm = pe.matmul(y3_ps[:], hq_t[:, c, :], down_w[:, c, :], start=(c == 0), stop=(c == FC - 1))
                    mm.then_inc(y3_mm, 1)

                turn_x(0)
                with pe.Fori(0, B // 2 - 1) as i:
                    for half in range(2):
                        batch(2 * i + half, half, False)
                batch(B - 2, 0, False)
                batch(B - 1, 1, True)

            @block.scalar
            def _(act):
                def scale_x(b, half):
                    act.wait_ge(xinv_set, b + 1)
                    act.activation(xmag[:], x_all[:, b, :], ACT.Copy, scale=xs[half][:, 3:4])
                    act.activation(xy[:], x_all[:, b, :], ACT.Copy, scale=xs[half][:, 2:3]).then_inc(x_scaled, 1)

                def store_x(b):
                    act.wait_ge(xt_mm, b + 1)
                    act.activation(xq_t[:], xt_ps[:, 0:DC * P].rearrange("p (c t) -> p c t", c=DC)[:, :, 0:T],
                                   ACT.Copy).then_inc(xt_out, 1)

                def batch(b, half, last):
                    for n, (at, width) in enumerate(FCH):
                        g = gate[:, (NCH * half + n) % 2, 0:width]
                        act.wait_ge(gate_set, NCH * b + n + 1)
                        act.activation(g, g, ACT.Silu).then_inc(silu_out, 1)
                    act.wait_ge(hinv_set, b + 1)
                    act.activation(hmag[:], hid[:], ACT.Copy, scale=hs[half][:, 3:4])
                    act.activation(hy[:], hid[:], ACT.Copy, scale=hs[half][:, 2:3]).then_inc(h_scaled, 1)
                    if not last:
                        scale_x(b + 1, 1 - half)
                    act.wait_ge(ht_mm, b + 1)
                    act.activation(hq_t[:], ht_ps[:, 0:FC * P].rearrange("p (c t) -> p c t", c=FC)[:, :, 0:T],
                                   ACT.Copy).then_inc(ht_out, 1)
                    if not last:
                        store_x(b + 1)

                scale_x(0, 0)
                store_x(0)
                with act.Fori(0, B // 2 - 1) as i:
                    for half in range(2):
                        batch(2 * i + half, half, False)
                batch(B - 2, 0, False)
                batch(B - 1, 1, True)
                act.wait_ge(var_set, 3)
                act.activation(rstd[:], rstd[:], ACT.Sqrt).then_inc(std_set, 1)

            @block.vector
            def _(dve):
                def scales(s, src, signal):
                    chain(dve.tensor_reduce(s[:, 0:1], src, AX.X, ALU.max, apply_absolute_value=True))
                    chain(dve.tensor_scalar(s[:, 1:2], s[:, 0:1], 1.0 / FP8_MAX, None, ALU.mult))
                    chain(dve.reciprocal(s[:, 2:3], s[:, 1:2]))
                    dve.tensor_scalar(s[:, 3:4], s[:, 2:3], 2.0 ** 20, None, ALU.mult).then_inc(signal, 1)

                def round_to(q, y, mag, signal):
                    chain(magic_bits(dve, mag[:].bitcast(U32)))
                    chain(magic_add(dve, y[:], mag[:]))
                    magic_sub(dve, q[:], y[:], mag[:]).then_inc(signal, 1)

                def round_x(b):
                    dve.wait_ge(x_scaled, b + 1)
                    round_to(xq, xy, xmag, xq_set)

                def gated(b, half, n):
                    at, width = FCH[n]
                    k = (NCH * half + n) % 2
                    dve.wait_ge(gu_mm, NCH * b + n + 1)
                    dve.scalar_tensor_tensor(gate[:, k, 0:width], gu_ps[:, k, 0, 0:width], xs[half][:, 1:2],
                                             gate_s[:, at:at + width], ALU.mult, ALU.mult).then_inc(gate_set, 1)
                    dve.scalar_tensor_tensor(upv[:, k, 0:width], gu_ps[:, k, 1, 0:width], xs[half][:, 1:2],
                                             up_s[:, at:at + width], ALU.mult, ALU.mult).then_inc(gu_out, 1)

                def hidden(b, half, n):
                    at, width = FCH[n]
                    k = (NCH * half + n) % 2
                    dve.wait_ge(silu_out, NCH * b + n + 1)
                    dve.wait_ge(gu_out, NCH * b + n + 3)
                    chain(dve.tensor_tensor(hid[:, at:at + width], gate[:, k, 0:width], upv[:, k, 0:width], ALU.mult))

                def add_y(b, half):
                    dve.wait_ge(y3_mm, b + 1)
                    chain(dve.scalar_tensor_tensor(ysum[:], y3_ps[:], hs[half][:, 1:2], down_s[:], ALU.mult, ALU.mult))
                    dve.nop().then_inc(y3_out, 1)
                    x = x_all[:, b, :]
                    chain(dve.tensor_tensor(x, x, ysum[:], ALU.add))
                    chain(dve.bn_stats(stats[:, b, :], x))

                def batch(b, half, first, last):
                    gated(b, half, 0)
                    gated(b, half, 1)
                    if not first:
                        add_y(b - 1, 1 - half)
                    hidden(b, half, 0)
                    gated(b, half, 2)
                    hidden(b, half, 1)
                    hidden(b, half, 2)
                    scales(hs[half], hid[:], hinv_set)
                    if not last:
                        scales(xs[1 - half], x_all[:, b + 1, :], xinv_set)
                    dve.wait_ge(h_scaled, b + 1)
                    round_to(hq, hy, hmag, hq_set)
                    if not last:
                        round_x(b + 1)

                dve.sem_inc(gu_out, 2)
                dve.sem_inc(y3_out, 1)
                scales(xs[0], x_all[:, 0, :], xinv_set)
                round_x(0)
                batch(0, 0, True, False)
                start = chain.value
                PER = 3 + 3 + 3 + 3 + 2 + 2
                with dve.Fori(0, B // 2 - 1) as i:
                    for half in range(2):
                        chain.turn(start, 2 * i + half, PER)
                        batch(2 * i + half + 1, 1 - half, False, False)
                chain.turned(start, B - 2, PER)
                batch(B - 1, 1, False, True)
                add_y(B - 1, 1)
                layer_norm(dve, 3, normed)


def rope_tables():
    half = ROPE // 2
    inv_freq = (np.float32(1.0) / np.float32(10000.0) ** (np.arange(half, dtype=np.float32) / np.float32(half)))
    ang = np.arange(LK, dtype=np.float32)[:, None] * inv_freq.astype(np.float32)
    c, s = np.cos(ang), np.sin(ang)
    return np.concatenate([c, c, -s, s], axis=1).astype(np.float32)


def kernel(x, ctx_2048, itok_BxS_0_1023, L0_attn_q1_w, L0_attn_k1_w, L0_attn_q2_w, L0_attn_k2_w, L0_attn_v_w,
           L0_attn_o_w, L0_attn_lambda_param, L0_xattn_W_kvc, L0_xattn_W_dq, L0_xattn_W_uq, L0_xattn_W_qr,
           L0_xattn_W_uk, L0_xattn_W_kr, L0_xattn_W_uv, L0_xattn_W_o, L0_ffn_w_gate, L0_ffn_w_up, L0_ffn_w_down,
           L0_ffn_up_reorder_index, L0_ffn_down_reorder_index):
    import concourse.bacc as bacc
    from concourse.bass_utils import run_bass_kernel_spmd
    import ml_dtypes

    def rows(w):
        return np.ascontiguousarray(w.reshape(-1, P, w.shape[1]).transpose(1, 0, 2))

    def swap(w):
        w = w.reshape(w.shape[0], -1, 2, ROPE // 2)
        return w[:, :, ::-1, :].reshape(w.shape[0], -1)

    x, ctx, seg = np.asarray(x), np.asarray(ctx_2048), np.asarray(itok_BxS_0_1023)
    uq, uk, uv = (np.asarray(w) for w in (L0_xattn_W_uq, L0_xattn_W_uk, L0_xattn_W_uv))
    qr, kr = np.asarray(L0_xattn_W_qr), np.asarray(L0_xattn_W_kr)
    lam = np.asarray(L0_attn_lambda_param).reshape(1, NJ, HG)
    table = rope_tables()

    col = np.arange(GK)
    in_span = col < GQ * SPAN
    query = np.arange(T) // NH
    off = np.where(in_span[None, :] & (query[:, None] == col[None, :] // SPAN),
                   -(col % SPAN)[None, :], NEG).astype(np.float32)
    row_c = np.stack([np.where(in_span, -(col % SPAN), 0), in_span], 1).astype(np.float32)
    base = np.arange(B)[None, :] * TROWS + np.where(in_span, 0, LK)[:, None]
    base = np.repeat(np.concatenate([base, base]), NT, axis=1).astype(np.float32)
    groups = seg.reshape(B, NG, GQ)
    seg_rows = np.repeat(groups.transpose(2, 0, 1).reshape(GQ, B * NG), NH, axis=0)
    by_col = np.concatenate([np.repeat(groups, SPAN, axis=2), groups[:, :, 0:1]], axis=2)
    seg_keys = by_col.reshape(B * NT, P).T

    qr3 = qr.reshape(QC, NH, ROPE)
    qs3 = swap(qr).reshape(QC, NH, ROPE)
    arrays = {
        "x": x,
        "x_t": x.reshape(B, T, DC, P).transpose(0, 3, 2, 1),
        "w_q1": rows(np.asarray(L0_attn_q1_w).T), "w_k1": rows(np.asarray(L0_attn_k1_w).T),
        "w_q2": rows(np.asarray(L0_attn_q2_w).T), "w_k2": rows(np.asarray(L0_attn_k2_w).T),
        "w_v": rows(np.asarray(L0_attn_v_w).T), "w_attn_o": rows(np.asarray(L0_attn_o_w).T),
        "lam": np.broadcast_to(lam, (T, NJ, HG)),
        "ctx_t": ctx.reshape(B, LK, DC, P).transpose(0, 3, 2, 1),
        "w_kvc": rows(np.asarray(L0_xattn_W_kvc)), "w_kvc_t": np.asarray(L0_xattn_W_kvc).T,
        "w_kr2": np.concatenate([kr, swap(kr)], axis=1),
        "w_dq": rows(np.asarray(L0_xattn_W_dq)),
        "w_uq_t": uq.reshape(QC, NH, XHD).transpose(2, 1, 0), "w_uk_t": uk.reshape(KVC, NH, XHD).transpose(2, 1, 0),
        "w_qr2": np.concatenate([qr3, qs3], axis=2).reshape(2, QH, NH, 2 * ROPE).transpose(1, 0, 2, 3),
        "w_uv_t": uv.reshape(KVC, NH, XHD).transpose(2, 1, 0), "w_o": rows(np.asarray(L0_xattn_W_o)),
        "w_gate": np.asarray(L0_ffn_w_gate), "w_up": np.asarray(L0_ffn_w_up),
        "w_down": np.asarray(L0_ffn_w_down).reshape(DC, P, F),
        "order": np.asarray(L0_ffn_down_reorder_index).reshape(FC, P).T,
        "seg_rows": seg_rows, "seg_keys": seg_keys,
        "ident": np.eye(P, dtype=np.float32), "identb": np.eye(P).astype(ml_dtypes.bfloat16),
        "off_mask": off, "row_c": np.concatenate([row_c, row_c]), "row_base": base,
        "rope_q": table[:T].T, "rope_k": table.reshape(KTILES, KROWS, 2 * ROPE).transpose(1, 0, 2),
    }
    arrays = {n: np.ascontiguousarray(v) for n, v in arrays.items()}
    nc = bacc.Bacc("TRN2", target_bir_lowering=False, num_devices=1)
    ins = {n: nc.dram_tensor(f"in_{n}", v.shape, mybir.dt.from_np(v.dtype), kind="ExternalInput").ap()
           for n, v in arrays.items()}
    out = nc.dram_tensor("out", (B, T, D), F32, kind="ExternalOutput").ap()
    build(nc, ins, out)
    r = run_bass_kernel_spmd(nc, [{f"in_{n}": v for n, v in arrays.items()}], core_ids=[0])
    return r.results[0]["out"]
```

```python
from contextlib import ExitStack

import numpy as np

import concourse.bass as bass
from concourse import mybir

ALU = mybir.AluOpType
ACT = mybir.ActivationFunctionType
F32 = mybir.dt.float32
BF16 = mybir.dt.bfloat16
I32 = mybir.dt.int32
U32 = mybir.dt.uint32
AX = mybir.AxisListType

P = 128
B, T, D = 8, 112, 512
DC = D // P
NH, HD = 16, 32
HG = 4
NJ = NH // HG
NPROJ = 5
LK = 375
KTILES, KROWS = 3, 125
KVC, QC, ROPE, XHD = 128, 192, 64, 128
QH = QC // 2
SPAN = 9
GQ = 7
NG = T // GQ
GK = 64
NT = NG * GK // P
TROWS = LK + 1
KW = KVC + ROPE
F = 1408
FC = F // P
FCH = [(0, 512), (512, 512), (1024, 384)]
DOWN_LO = 6 * P
DOWN_COLS = ((0, DOWN_LO), (DOWN_LO, F))
FP8_MAX = 448.0
NEG = -1e30
EPS = 1e-5
MAGIC_MIN = 1.5 * 2.0 ** 14



class Chain:

    def __init__(self, eng, sem):
        self.eng, self.sem, self.base, self.n = eng, sem, 0, 0

    def __call__(self, ins):
        ins.then_inc(self.sem, 1)
        self.n += 1
        self.eng.wait_ge(self.sem, self.base + self.n)

    def turn(self, start, step, per):
        self.base, self.n = start + step * per, 0

    def turned(self, start, steps, per):
        assert self.n == per, (self.n, per)
        self.base, self.n = start + steps * per, 0

    @property
    def value(self):
        return self.base + self.n



def magic_bits(dve, scaled_bits):
    return dve.tensor_scalar(scaled_bits, scaled_bits, 0x7F800000, 0x00400000, ALU.bitwise_and, ALU.bitwise_or)


def magic_add(dve, y, magic):
    return dve.scalar_tensor_tensor(y, magic, MAGIC_MIN, y, ALU.max, ALU.add)


def magic_sub(dve, minus_q, summed, magic):
    return dve.scalar_tensor_tensor(minus_q, magic, MAGIC_MIN, summed, ALU.max, ALU.subtract)


def build(nc, a, out):
    table = nc.dram_tensor("key_table", [B * TROWS, KW], F32)

    table_rows = table[:].rearrange("(b r) n -> b r n", b=B)
    top = ExitStack()
    with top:
        def sem(name):
            return top.enter_context(nc.semaphore(name))

        def keep(name, shape, dt=F32):
            return top.enter_context(nc.sbuf_tensor(name, shape, dt))

        x_all = keep("x_all", [T, B, D])
        ident = keep("ident", [P, P])
        identb = keep("identb", [P, P], BF16)
        ones = keep("ones", [P, P])
        wdq = keep("wdq", [P, DC, QC])
        wqn = keep("wqn", [QH, 2, NH, XHD])
        gate_w = keep("gate_w", [P, DC, F], BF16)
        up_w = keep("up_w", [P, DC, F], BF16)
        down_w = keep("down_w", [P, FC, D], BF16)
        gate_s = keep("gate_s", [T, F])
        up_s = keep("up_s", [T, F])
        down_s = keep("down_s", [T, D])
        stats = keep("stats", [T, B, 6])
        mv = keep("mv", [T, B, 2])
        rstd = keep("rstd", [T, B])
        seg_rows = keep("seg_rows", [T, B * NG])
        row_idx = keep("row_idx", [P, B * NT], I32)
        off_mask = keep("off_mask", [T, GK])

        consts_in = sem("consts_in")
        weights_in = sem("weights_in")
        xwq_in = sem("xwq_in")
        x_in = sem("x_in")
        dve_chain = sem("dve_chain")
        chain = Chain(nc.vector, dve_chain)

        var_set = sem("var_set")
        std_set = sem("std_set")

        def layer_norm(dve, turn, done=None):
            for b in range(B):
                last = dve.bn_aggr(mv[:, b, :], stats[:, b, :])
            chain(last)
            chain(dve.tensor_scalar(rstd[:], mv[:, :, 1], EPS, None, ALU.add))
            dve.nop().then_inc(var_set, 1)
            dve.wait_ge(std_set, turn)
            chain(dve.reciprocal(rstd[:], rstd[:]))
            for b in range(B):
                last = dve.tensor_scalar(x_all[:, b, :], x_all[:, b, :], mv[:, b, 0:1], rstd[:, b:b + 1],
                                         ALU.subtract, ALU.mult)
                if done is not None:
                    last.then_inc(done, 1)
            if done is None:
                chain(last)

        weights = top.enter_context(ExitStack())
        w_in = weights.enter_context(nc.sbuf_tensor("w_in", [P, NPROJ, DC, D], F32))
        w_in_sem = sem("w_in_sem")
        w_out_sem = sem("w_out_sem")

        with ExitStack() as st:
            def sb(name, shape, dt=F32):
                return st.enter_context(nc.sbuf_tensor(name, shape, dt))

            def ps(name, shape, dt=F32):
                return st.enter_context(nc.psum_tensor(name, shape, dt))

            ctx_uq = sb("ctx_uq", [P, NH * QC])
            ctx_t = [ctx_uq[:, k * DC * LK:(k + 1) * DC * LK].rearrange("p (c n) -> p c n", c=DC) for k in range(2)]
            wuq_t = ctx_uq[:].rearrange("p (h n) -> p h n", h=NH)
            wuk_t = sb("wuk_t", [P, NH, KVC])
            wkvx = sb("wkvx", [P, DC, 2 * P])
            wkvc_t = sb("wkvc_t", [P, D])
            wkr2 = sb("wkr2", [P, 2 * ROPE])
            rope_k = sb("rope_k", [KROWS, KTILES, 2 * ROPE])
            key_rows = [sb(f"key_rows{k}", [KROWS, KTILES, KW]) for k in range(2)]
            rot = sb("rot", [KROWS, KTILES, 2 * ROPE])
            mean_row = [sb(f"mean_row{k}", [1, KW]) for k in range(2)]
            raw = [sb(f"raw{k}", [P, F]) for k in range(2)]
            mag = [sb(f"mag{k}", [P, DOWN_LO]) for k in range(2)]
            summ = [sb(f"summ{k}", [P, DOWN_LO]) for k in range(2)]
            qt = [sb(f"qt{k}", [P, DOWN_LO], BF16) for k in range(2)]
            amax = sb("amax", [P, 1])
            wsc = [sb(f"wsc{k}", [P, 1]) for k in range(2)]
            inv = [sb(f"inv{k}", [P, 2]) for k in range(2)]
            diag = [sb(f"diag{k}", [P, P]) for k in range(2)]
            order = sb("order", [P, FC], I32)
            order_c = [sb(f"order_c{k}", [P, 1], I32) for k in range(2)]
            seg_i = sb("seg_i", [T, B * NG], I32)
            seg_k = sb("seg_k", [P, B * NT], I32)
            seg_f = sb("seg_f", [P, B * NT])
            row_c = sb("row_c", [P, 2])
            row_base = sb("row_base", [P, B * NT])

            key_ps = ps("key_ps", [P, 2, 1024])
            join_ps = ps("join_ps", [P, 2, 512])
            mean_ps = join_ps[0:1, 1, 0:KW]
            piece_ps = ps("piece_ps", [P, 2, 512])

            ctx_in = [sem(f"ctx_in{k}") for k in range(2)]
            key_mm = sem("key_mm")
            mean_mm = sem("mean_mm")
            kvc_out = sem("kvc_out")
            rope_out = sem("rope_out")
            mean_out = sem("mean_out")
            table_out = [sem(f"table_out{k}") for k in range(2)]
            wuq_in = sem("wuq_in")
            join_mm = sem("join_mm")
            join_out = sem("join_out")
            ones_set = sem("ones_set")
            raw_in = [sem(f"raw_in{k}") for k in range(2)]
            gathers = sem("gathers")
            ord_in = sem("ord_in")
            ord_c = sem("ord_c")
            inv_set = sem("inv_set")
            scaled = sem("scaled")
            quant = sem("quant")
            piece_mm = sem("piece_mm")
            piece_out = sem("piece_out")

            block = st.enter_context(nc.Block())
            KV_DMAS = 2 * 16
            DOWN_PAIRS = DC

            def gather_rows(pool, c, half, first=False):
                if not first:
                    pool.wait_ge(scaled, 2 * c - 2)
                    pool.sem_inc(gathers, 1)
                pool.tensor_copy(order_c[half][:], order[:, bass.ds(c, 1)]).then_inc(ord_c, 1)
                pool.wait_ge(ord_c, c + 1)
                pool.sem_inc(gathers, 1)
                for m, name in enumerate(("w_gate", "w_up")):
                    pool.indirect_dma_start(raw[half][:, m * D:(m + 1) * D], None, a[name],
                                            bass.IndirectOffsetOnAxis(order_c[half][:], 0)).then_inc(raw_in[half], 16)

            def keys_of(half):
                return key_ps[0:KROWS, half, 0:768].rearrange("p (k n) -> p k n", k=KTILES)

            @block.sync
            def _(sp):
                for t_, n_ in ((wkvc_t, "w_kvc_t"), (wkr2, "w_kr2")):
                    sp.dma_start(t_[:], a[n_]).then_inc(weights_in, 16)
                sp.dma_start(wkvx[:, :, 0:P], a["w_kvc"]).then_inc(weights_in, 16)
                sp.dma_start(ctx_t[0], a["ctx_t"][0]).then_inc(ctx_in[0], 16)
                for t_, n_ in ((ident, "ident"), (identb, "identb"), (off_mask, "off_mask"),
                               (rope_k, "rope_k"), (row_c, "row_c"), (row_base, "row_base"),
                               (seg_i, "seg_rows"), (seg_k, "seg_keys")):
                    sp.dma_start(t_[:], a[n_]).then_inc(consts_in, 16)
                sp.dma_start(ctx_t[1], a["ctx_t"][1]).then_inc(ctx_in[1], 16)

                def store_keys(b, half):
                    sp.wait_ge(kvc_out, b + 1)
                    sp.wait_ge(rope_out, b + 1)
                    sp.dma_start(table_rows[b, 0:LK].rearrange("(k p) n -> p k n", k=KTILES),
                                 key_rows[half][:]).then_inc(table_out[half], 16)

                def store_mean(b, half):
                    sp.wait_ge(mean_out, b + 1)
                    sp.dma_start(table_rows[b, LK:TROWS], mean_row[half][:]).then_inc(table_out[half], 16)

                def turn(b, half, first=False):
                    sp.wait_ge(key_mm, b + 1)
                    sp.dma_start(ctx_t[half], a["ctx_t"][b + 2]).then_inc(ctx_in[half], 16)
                    if not first:
                        sp.dma_start(w_in[:, bass.ds(b - 1, 1)], a["w_in"][bass.ds(b - 1, 1)]
                                     .rearrange("m p c n -> p m c n")).then_inc(w_in_sem, 16)
                    store_keys(b, half)
                    if not first:
                        store_mean(b - 1, 1 - half)

                turn(0, 0, True)
                turn(1, 1)
                with sp.Fori(1, B // 2 - 1) as i:
                    for half in range(2):
                        turn(2 * i + half, half)
                sp.dma_start(wuk_t[:], a["w_uk_t"]).then_inc(wuq_in, 16)
                for b in (B - 2, B - 1):
                    store_keys(b, b % 2)
                    store_mean(b - 1, (b - 1) % 2)
                store_mean(B - 1, 1)
                sp.wait_ge(key_mm, B)
                sp.dma_start(wuq_t, a["w_uq_t"]).then_inc(wuq_in, 16)
                sp.dma_start(x_all[:], a["x"].rearrange("b t d -> t b d")).then_inc(x_in, 16)
                sp.dma_start(wdq[:], a["w_dq"]).then_inc(xwq_in, 16)
                for half in range(2):
                    sp.wait_ge(table_out[half], B // 2 * KV_DMAS)

            @block.gpsimd
            def _(pool):
                pool.memset(ones[:], 1.0).then_inc(ones_set, 1)
                pool.dma_start(order[:], a["order"]).then_inc(ord_in, 16)
                pool.wait_ge(ord_in, 16)
                for half in range(2):
                    gather_rows(pool, half, half, True)
                with pool.Fori(1, FC // 2) as i:
                    for half in range(2):
                        gather_rows(pool, 2 * i + half, half)
                gather_rows(pool, FC - 1, 0)
                for n in range(DOWN_PAIRS):
                    pool.wait_ge(scaled, 2 * (FC + n) - 2)
                    pool.dma_start(raw[(FC + n) % 2][:], a["w_down"][n]).then_inc(raw_in[(FC + n) % 2], 16)

            @block.scalar
            def _(act):
                act.sem_inc(piece_out, 2)
                act.wait_ge(join_mm, 1)
                act.activation(wkvx[:, :, P:2 * P], join_ps[:, 0, :].rearrange("p (c n) -> p c n", c=DC),
                               ACT.Copy).then_inc(join_out, 1)

                def scale(p, src, k, slot):
                    act.wait_ge(inv_set, p + 1)
                    act.wait_ge(quant, p + 1)
                    width = src.shape[-1]
                    act.activation(mag[k][:, 0:width], src, ACT.Copy, scale=inv[slot][:, 1:2])
                    act.activation(summ[k][:, 0:width], src, ACT.Copy, scale=inv[slot][:, 0:1]).then_inc(scaled, 1)

                def scale_gu(i, half):
                    for m in range(2):
                        scale(2 * i + m, raw[half][:, m * D:(m + 1) * D], m, m)

                def scale_down(n):
                    for m, (at, end) in enumerate(DOWN_COLS):
                        scale(2 * (FC + n) + m, raw[(FC + n) % 2][:, at:end], m, n % 2)

                def store_gu(i):
                    for m, (w, s) in enumerate(((gate_w, gate_s), (up_w, up_s))):
                        act.wait_ge(piece_mm, 2 * i + m + 3)
                        act.activation(w[:, :, bass.ds(i * P, P)],
                                       piece_ps[:].bitcast(BF16)[:, m, 0:D].rearrange("p (h n) -> p h n", h=DC),
                                       ACT.Copy)
                        act.activation(s[:, bass.ds(i * P, P)], piece_ps[0:T, m, 512 - P:512],
                                       ACT.Copy).then_inc(piece_out, 1)

                def store_down(n):
                    for m, (at, end) in enumerate(DOWN_COLS):
                        act.wait_ge(piece_mm, 2 * (FC + n) + m + 3)
                        if m == 0:
                            act.activation(down_s[:, n * P:(n + 1) * P], piece_ps[0:T, m, 512 - P:512], ACT.Copy)
                        act.activation(down_w[:, at // P:end // P, n * P:(n + 1) * P],
                                       piece_ps[:].bitcast(BF16)[:, m, 0:end - at].rearrange("p (h n) -> p h n", n=P),
                                       ACT.Copy).then_inc(piece_out, 1)

                def store_mean(b, half):
                    act.wait_ge(mean_mm, b + 1)
                    act.activation(mean_row[half][:], mean_ps, ACT.Copy, scale=1.0 / LK).then_inc(mean_out, 1)

                def turn(b, half, i, peeled=False):
                    scale_gu(b, half)
                    act.wait_ge(key_mm, b + 1)
                    if not peeled:
                        act.wait_ge(table_out[half], i * KV_DMAS)
                    act.activation(key_rows[half][:, :, 0:KVC], keys_of(half)[:, :, 0:KVC],
                                   ACT.Copy).then_inc(kvc_out, 1)
                    if not (peeled and half == 0):
                        store_mean(b - 1, 1 - half)
                        store_gu(b - 1)

                turn(0, 0, 0, True)
                turn(1, 1, 0, True)
                with act.Fori(1, B // 2) as i:
                    for half in range(2):
                        turn(2 * i + half, half, i)
                store_mean(B - 1, 1)
                for i in range(B, FC + DOWN_PAIRS):
                    if i < FC:
                        scale_gu(i, i % 2)
                    else:
                        scale_down(i - FC)
                    if i <= FC:
                        store_gu(i - 1)
                    else:
                        store_down(i - 1 - FC)
                    for k in range(2 * (i - B), min(2 * (i - B) + 2, NH // 2)):
                        act.wait_ge(join_mm, k + 2)
                        act.activation(wqn[:, :, 2 * k:2 * k + 2, :],
                                       join_ps[0:QH, k % 2, :].rearrange("p (h j n) -> p j h n", h=2, j=2),
                                       ACT.Copy).then_inc(join_out, 1)
                store_down(DOWN_PAIRS - 1)

            @block.tensor
            def _(pe):
                pe.sem_inc(piece_mm, 2)
                pe.wait_ge(weights_in, 16 * 3)
                for c in range(DC):
                    mm = pe.matmul(join_ps[:, 0, c * P:(c + 1) * P], wkvc_t[:, c * P:(c + 1) * P], wkr2[:],
                                   start=True, stop=True)
                mm.then_inc(join_mm, 1)
                pe.wait_ge(join_out, 1)
                pe.wait_ge(ones_set, 1)

                def mean(b, half, first=False):
                    pe.wait_ge(kvc_out, b + 1)
                    pe.wait_ge(rope_out, b + 1)
                    if not first:
                        pe.wait_ge(mean_out, b)
                    for k in range(KTILES):
                        mm = pe.matmul(mean_ps, ones[0:KROWS, 0:1], key_rows[half][:, k, :],
                                       start=(k == 0), stop=(k == KTILES - 1))
                    mm.then_inc(mean_mm, 1)

                def turn_pair(i, cols, scales):
                    for m, (at, end) in enumerate(cols):
                        p = 2 * i + m
                        pe.wait_ge(quant, p + 3)
                        pe.wait_ge(piece_out, p + 1)
                        for h in range((end - at) // P):
                            mm = pe.transpose(piece_ps[:].bitcast(BF16)[:, m, h * P:(h + 1) * P],
                                              qt[m][:, h * P:(h + 1) * P], identb[:])
                        if m < scales:
                            mm = pe.matmul(piece_ps[0:T, m, 512 - P:512], ones[:, 0:T], diag[m][:],
                                           start=True, stop=True)
                        mm.then_inc(piece_mm, 1)

                GU_COLS = ((0, D), (0, D))

                def turn(b, half, i, first=False):
                    pe.wait_ge(ctx_in[half], 16 * (i + 1))
                    if not (isinstance(b, int) and b < 2):
                        pe.wait_ge(rope_out, b - 1)
                    for k in range(KTILES):
                        for c in range(DC):
                            mm = pe.matmul(key_ps[0:KROWS, half, k * 256:(k + 1) * 256],
                                           ctx_t[half][:, c, k * KROWS:(k + 1) * KROWS], wkvx[:, c, :],
                                           start=(c == 0), stop=(c == DC - 1))
                    mm.then_inc(key_mm, 1)
                    if not first:
                        mean(b - 1, 1 - half, isinstance(b, int) and b == 1)
                        turn_pair(b - 1, GU_COLS, 2)

                turn(0, 0, 0, True)
                pe.wait_ge(consts_in, 16 * 8)
                turn(1, 1, 0)
                with pe.Fori(1, B // 2) as i:
                    for half in range(2):
                        turn(2 * i + half, half, i)
                mean(B - 1, 1)
                pe.wait_ge(wuq_in, 32)
                pe.wait_ge(mean_out, B)
                for i in range(B, FC + DOWN_PAIRS + 1):
                    turn_pair(i - 1, GU_COLS if i <= FC else DOWN_COLS, 2 if i <= FC else 1)
                    for k in range(2 * (i - B), min(2 * (i - B) + 2, NH // 2)):
                        if k > 0:
                            pe.wait_ge(join_out, k)
                        for h in range(2):
                            for j in range(2):
                                n = 2 * h + j
                                mm = pe.matmul(join_ps[0:QH, k % 2, n * P:(n + 1) * P],
                                               wuq_t[:, 2 * k + h, j * QH:(j + 1) * QH], wuk_t[:, 2 * k + h, :],
                                               start=True, stop=True)
                        mm.then_inc(join_mm, 1)

            @block.vector
            def _(dve):
                dve.sem_inc(quant, 2)

                def inverse(p, src, slot, pieces=1):
                    chain(dve.tensor_reduce(amax[:], src, AX.X, ALU.max, apply_absolute_value=True))
                    chain(dve.tensor_scalar(wsc[slot][:], amax[:], 1.0 / FP8_MAX, None, ALU.mult))
                    chain(dve.reciprocal(inv[slot][:, 0:1], wsc[slot][:]))
                    dve.tensor_scalar(inv[slot][:, 1:2], inv[slot][:, 0:1], 2.0 ** 20, None,
                                      ALU.mult).then_inc(inv_set, pieces)

                def round_piece(p, width, k, slot):
                    dve.wait_ge(piece_mm, p + 1)
                    if slot is not None:
                        dve.tensor_scalar(diag[k][:], ident[:], wsc[slot][:], None, ALU.mult)
                    dve.wait_ge(scaled, p + 1)
                    bits, y = mag[k][:, 0:width], summ[k][:, 0:width]
                    chain(magic_bits(dve, bits.bitcast(U32)))
                    chain(magic_add(dve, y, bits))
                    magic_sub(dve, qt[k][:, 0:width], y, bits).then_inc(quant, 1)

                def gu_pair(i, half, count, first=False):
                    dve.wait_ge(raw_in[half], 32 * count)
                    inverse(2 * i, raw[half][:, 0:D], 0)
                    if not first:
                        round_piece(2 * i - 1, D, 1, 1)
                    inverse(2 * i + 1, raw[half][:, D:2 * D], 1)
                    round_piece(2 * i, D, 0, 0)

                def rotate_keys(b, half, i, peeled=False):
                    if not peeled:
                        dve.wait_ge(table_out[half], i * KV_DMAS)
                    dve.wait_ge(kvc_out, b + 1)
                    chain(dve.tensor_tensor(rot[:], keys_of(half)[:, :, KVC:KVC + 2 * ROPE], rope_k[:], ALU.mult))
                    dve.tensor_tensor(key_rows[half][:, :, KVC:KW], rot[:, :, 0:ROPE], rot[:, :, ROPE:2 * ROPE],
                                      ALU.add).then_inc(rope_out, 1)

                dve.wait_ge(consts_in, 16 * 8)
                gu_pair(0, 0, 1, True)
                rotate_keys(0, 0, 0, True)
                gu_pair(1, 1, 1)
                rotate_keys(1, 1, 0, True)
                PER = 3 + 2 + 3 + 2 + 1
                start = chain.value
                with dve.Fori(1, B // 2) as i:
                    for half in range(2):
                        b = 2 * i + half
                        chain.turn(start, b - 2, PER)
                        gu_pair(b, half, i + 1)
                        rotate_keys(b, half, i)
                chain.turned(start, B - 2, PER)
                for i in range(B, FC):
                    gu_pair(i, i % 2, i // 2 + 1)
                for n in range(DOWN_PAIRS):
                    i = FC + n
                    dve.wait_ge(raw_in[i % 2], 32 * ((FC + 1 - i % 2) // 2) + 16 * (n // 2 + 1))
                    inverse(2 * i, raw[i % 2][:], n % 2, 2)
                    if n == 0:
                        round_piece(2 * i - 1, D, 1, 1)
                    else:
                        round_piece(2 * i - 1, F - DOWN_LO, 1, None)
                    round_piece(2 * i, DOWN_LO, 0, n % 2)
                round_piece(2 * (FC + DOWN_PAIRS) - 1, F - DOWN_LO, 1, None)

                chain(dve.tensor_copy(seg_f[:], seg_k[:]))
                chain(dve.tensor_scalar(seg_f[:], seg_f[:], row_c[:, 0:1], 0.0, ALU.add, ALU.max))
                chain(dve.tensor_scalar(seg_f[:], seg_f[:], float(LK - 1), row_c[:, 1:2], ALU.min, ALU.mult))
                chain(dve.tensor_tensor(row_idx[:], seg_f[:], row_base[:], ALU.add))
                chain(dve.tensor_copy(seg_rows[:], seg_i[:]))

        with ExitStack() as st:
            def sb(name, shape, dt=F32):
                return st.enter_context(nc.sbuf_tensor(name, shape, dt))

            def ps(name, shape, dt=F32):
                return st.enter_context(nc.psum_tensor(name, shape, dt))

            w_out = sb("w_out", [P, DC, D])
            x_t = [sb(f"x_t{k}", [P, DC, T]) for k in range(2)]
            qk = [[sb(f"qk{m}{k}", [P, NJ, T]) for k in range(2)] for m in range(4)]
            v = [sb(f"v{k}", [T, D]) for k in range(2)]
            prob = [sb(f"prob{k}", [T, HG, 2, T]) for k in range(2)]
            att = [sb(f"att{k}", [T, HG, T]) for k in range(2)]
            att_t = [sb(f"att_t{k}", [T, HG, T]) for k in range(2)]
            o_t = sb("o_t", [P, NJ, T])
            lam = sb("lam", [T, NJ, HG])
            smax = sb("smax", [T, HG, 2])
            ssum = sb("ssum", [T, HG, 2])
            sinv = sb("sinv", [T, HG, 2])

            proj_ps = ps("proj_ps", [P, 2, 512])
            score_ps = ps("score_ps", [T, HG, 512])
            att_ps = ps("att_ps", [T, 512])
            o_ps = ps("o_ps", [P, 512])

            lam_in = sem("lam_in")
            xt_in = [sem(f"xt_in{k}") for k in range(2)]
            proj_mm = sem("proj_mm")
            proj_out = sem("proj_out")
            score_mm = sem("score_mm")
            score_sub = sem("score_sub")
            prob_exp = sem("prob_exp")
            att_set = sem("att_set")
            att_turn = sem("att_turn")
            att_out = sem("att_out")
            pv_mm = sem("pv_mm")
            o_out = sem("o_out")
            y_mm = sem("y_mm")
            y_out = sem("y_out")

            block = st.enter_context(nc.Block())

            V = NPROJ - 1

            def projected(b, m):
                return NPROJ * b + m + 1

            @block.sync
            def _(sp):
                for k in range(2):
                    sp.dma_start(x_t[k][:], a["x_t"][k]).then_inc(xt_in[k], 16)
                sp.dma_start(w_out[:], a["w_attn_o"]).then_inc(w_out_sem, 16)
                sp.dma_start(lam[:], a["lam"]).then_inc(lam_in, 16)
                with sp.Fori(1, B // 2) as i:
                    for half in range(2):
                        b = 2 * i + half
                        sp.wait_ge(proj_mm, projected(b - 2, V))
                        sp.dma_start(x_t[half][:], a["x_t"][b]).then_inc(xt_in[half], 16)

            @block.tensor
            def _(pe):
                def project(b, half, i, m, bank):
                    if m == 0:
                        pe.wait_ge(xt_in[half], 16 * (i + 1))
                    if m == V:
                        for c in range(DC):
                            mm = pe.matmul(proj_ps[0:T, bank, :], x_t[half][:, c, :], w_in[:, V, c, :],
                                           start=(c == 0), stop=(c == DC - 1))
                    else:
                        for j in range(NJ):
                            for c in range(DC):
                                mm = pe.matmul(proj_ps[:, bank, j * T:(j + 1) * T],
                                               w_in[:, m, c, j * P:(j + 1) * P], x_t[half][:, c, :],
                                               start=(c == 0), stop=(c == DC - 1))
                    mm.then_inc(proj_mm, 1)

                def scores(b, half, j, first=False):
                    if j == 0:
                        pe.wait_ge(proj_out, projected(b, 3))
                    if not (first and j == 0):
                        pe.wait_ge(score_sub, 4 * b + j)
                    for s in range(2):
                        for r in range(HG):
                            rows = slice(r * HD, (r + 1) * HD)
                            mm = pe.matmul(score_ps[:, r, s * T:(s + 1) * T], qk[2 * s][half][rows, j, :],
                                           qk[2 * s + 1][half][rows, j, :], start=True, stop=True)
                    mm.then_inc(score_mm, 1)

                def turn(b, j, first=False):
                    pe.wait_ge(att_set, 4 * b + j + 1)
                    if not (first and j == 0):
                        pe.wait_ge(att_out, 4 * b + j)
                    for r in range(HG):
                        mm = pe.transpose(att_ps[:, r * T:(r + 1) * T], att[j % 2][:, r, :], ident[0:T, 0:T])
                    mm.then_inc(att_turn, 1)

                def heads_out(b, half, j, first=False):
                    pe.wait_ge(att_out, 4 * b + j + 1)
                    if j == 0:
                        pe.wait_ge(proj_out, projected(b, V))
                        if not first:
                            pe.wait_ge(o_out, b)
                    for r in range(HG):
                        h = HG * j + r
                        mm = pe.matmul(o_ps[r * HD:(r + 1) * HD, j * T:(j + 1) * T],
                                       v[half][:, h * HD:(h + 1) * HD], att_t[j % 2][:, r, :],
                                       start=True, stop=True)
                    if j == NJ - 1:
                        mm.then_inc(pv_mm, 1)

                def join_heads(b):
                    pe.wait_ge(o_out, b + 1)
                    for j in range(NJ):
                        mm = pe.matmul(proj_ps[0:T, 1, :], o_t[:, j, :], w_out[:, j, :],
                                       start=(j == 0), stop=(j == NJ - 1))
                    mm.then_inc(y_mm, 1)

                def batch(b, half, i, first=False, last=False):
                    def ahead(m, bank):
                        if not last:
                            project(b + 1, 1 - half, i + half, m, bank)

                    scores(b, half, 0, first)
                    if not first:
                        turn(b - 1, 2)
                    project(b, half, i, V, 0)
                    ahead(0, 1)
                    if not first:
                        heads_out(b - 1, 1 - half, 2)

                    scores(b, half, 1)
                    if not first:
                        turn(b - 1, 3)
                    pe.wait_ge(proj_out, projected(b, V))
                    ahead(1, 0)
                    if not first:
                        heads_out(b - 1, 1 - half, 3)

                    scores(b, half, 2)
                    turn(b, 0, first)
                    if not last:
                        pe.wait_ge(proj_out, projected(b + 1, 0))
                    if not first:
                        join_heads(b - 1)
                    if not last:
                        pe.wait_ge(proj_out, projected(b + 1, 1))
                    ahead(2, 0)
                    heads_out(b, half, 0, first)

                    scores(b, half, 3)
                    turn(b, 1)
                    if not first:
                        pe.wait_ge(y_out, b)
                    ahead(3, 1)
                    heads_out(b, half, 1)

                pe.wait_ge(w_in_sem, 16 * NPROJ)
                for m in range(V):
                    if m >= 2:
                        pe.wait_ge(proj_out, m - 1)
                    project(0, 0, 0, m, m % 2)
                batch(0, 0, 0, first=True)
                pe.wait_ge(w_out_sem, 16)
                batch(1, 1, 0)
                with pe.Fori(1, B // 2 - 1) as i:
                    for half in range(2):
                        batch(2 * i + half, half, i)
                batch(B - 2, 0, B // 2 - 1)
                batch(B - 1, 1, B // 2 - 1, last=True)
                for j in (2, 3):
                    turn(B - 1, j)
                    heads_out(B - 1, 1, j)
                join_heads(B - 1)

            @block.scalar
            def _(act):
                def store(b, half, m, bank):
                    act.wait_ge(proj_mm, projected(b, m))
                    if m == V:
                        act.activation(v[half][:], proj_ps[0:T, bank, :], ACT.Copy).then_inc(proj_out, 1)
                    else:
                        act.activation(qk[m][half][:], proj_ps[:, bank, 0:NJ * T].rearrange("p (j t) -> p j t", j=NJ),
                                       ACT.Copy, scale=1.0 if m % 2 else HD ** -0.5).then_inc(proj_out, 1)

                def exp(b, j):
                    act.wait_ge(score_sub, 4 * b + j + 1)
                    act.activation(prob[j % 2][:], prob[j % 2][:], ACT.Exp).then_inc(prob_exp, 1)

                def store_att(b, j):
                    act.wait_ge(att_turn, 4 * b + j + 1)
                    act.activation(att_t[j % 2][:], att_ps[:, 0:HG * T].rearrange("p (r t) -> p r t", r=HG),
                                   ACT.Copy).then_inc(att_out, 1)

                def store_heads(b):
                    act.wait_ge(pv_mm, b + 1)
                    act.activation(o_t[:], o_ps[:, 0:NJ * T].rearrange("p (j t) -> p j t", j=NJ),
                                   ACT.Copy).then_inc(o_out, 1)

                def batch(b, half, first=False, last=False):
                    def ahead(m, bank):
                        if not last:
                            store(b + 1, 1 - half, m, bank)

                    if not first:
                        store_att(b - 1, 2)
                    exp(b, 0)
                    store(b, half, V, 0)
                    ahead(0, 1)
                    if not first:
                        store_att(b - 1, 3)
                    exp(b, 1)
                    ahead(1, 0)
                    if not first:
                        store_heads(b - 1)
                    store_att(b, 0)
                    exp(b, 2)
                    ahead(2, 0)
                    store_att(b, 1)
                    exp(b, 3)
                    ahead(3, 1)

                for m in range(V):
                    store(0, 0, m, m % 2)
                batch(0, 0, first=True)
                batch(1, 1)
                with act.Fori(1, B // 2 - 1) as i:
                    for half in range(2):
                        batch(2 * i + half, half)
                batch(B - 2, 0)
                batch(B - 1, 1, last=True)
                store_att(B - 1, 2)
                store_att(B - 1, 3)
                store_heads(B - 1)
                act.wait_ge(var_set, 1)
                act.activation(rstd[:], rstd[:], ACT.Sqrt).then_inc(std_set, 1)

            @block.vector
            def _(dve):
                def shift(b, j):
                    dve.wait_ge(score_mm, 4 * b + j + 1)
                    s = score_ps[:, :, 0:2 * T].rearrange("p r (s k) -> p r s k", s=2)
                    chain(dve.tensor_reduce(smax[:], s, AX.X, ALU.max))
                    dve.tensor_tensor(prob[j % 2][:], s, smax[:].unsqueeze(3).broadcast_to([T, HG, 2, T]),
                                      ALU.subtract).then_inc(score_sub, 1)

                def combine(b, j):
                    p = prob[j % 2]
                    dve.wait_ge(prob_exp, 4 * b + j + 1)
                    chain(dve.tensor_reduce(ssum[:], p[:], AX.X, ALU.add))
                    chain(dve.reciprocal(sinv[:], ssum[:]))
                    chain(dve.tensor_tensor(sinv[:, :, 1], sinv[:, :, 1], lam[:, j, :], ALU.mult))
                    chain(dve.tensor_tensor(p[:], p[:], sinv[:].unsqueeze(3).broadcast_to([T, HG, 2, T]), ALU.mult))
                    dve.tensor_tensor(att[j % 2][:], p[:, :, 0, :], p[:, :, 1, :], ALU.subtract).then_inc(att_set, 1)

                def add_y(b):
                    dve.wait_ge(y_mm, b + 1)
                    x_b = x_all[:, b, :]
                    chain(dve.tensor_tensor(x_b, x_b, proj_ps[0:T, 1, :], ALU.add))
                    dve.nop().then_inc(y_out, 1)
                    chain(dve.bn_stats(stats[:, b, :], x_b))

                def batch(b, first=False):
                    shift(b, 0)
                    if not first:
                        combine(b - 1, 3)
                    shift(b, 1)
                    combine(b, 0)
                    shift(b, 2)
                    combine(b, 1)
                    if not first:
                        add_y(b - 1)
                    shift(b, 3)
                    combine(b, 2)

                PER = NJ * 5 + 2
                dve.wait_ge(lam_in, 16)
                dve.wait_ge(x_in, 16)
                batch(0, True)
                start = chain.value
                with dve.Fori(1, B) as b:
                    chain.turn(start, b - 1, PER)
                    batch(b)
                chain.turned(start, B - 1, PER)
                combine(B - 1, 3)
                add_y(B - 1)
                layer_norm(dve, 1)

        weights.close()

        with ExitStack() as st:
            def sb(name, shape, dt=F32):
                return st.enter_context(nc.sbuf_tensor(name, shape, dt))

            def ps(name, shape, dt=F32):
                return st.enter_context(nc.psum_tensor(name, shape, dt))

            wvo = sb("wvo", [P, NH, D])
            wuv_t = sb("wuv_t", [P, NH, KVC])
            wqr = sb("wqr", [QH, 2, NH * ROPE])
            q_all = sb("q_all", [P, 2, T, NH])
            k_t = sb("k_t", [P, 2, NG * GK])
            rows_kv = [sb(f"rows_kv{k}", [P, NT, KW]) for k in range(2)]
            turned = sb("turned", [P, NT, 2, ROPE // 2])
            cos_q = sb("cos_q", [P, NT, 2, ROPE // 2])
            sin_q = sb("sin_q", [P, NT, 2, ROPE // 2])
            x_b = sb("x_b", [T, D])
            xb_t = sb("xb_t", [P, DC, T])
            qc_t = sb("qc_t", [QH, 2, T])
            prob = sb("xprob", [T, NG, GK])
            mask = sb("mask", [T, NG, GK])
            outside = sb("outside", [T, NG, GK], BF16)
            prob_t = sb("prob_t", [P, NT, T])
            oc_t = sb("oc_t", [P, NG, GQ, NH])
            idx_b = [sb(f"idx_b{k}", [P, NT], I32) for k in range(2)]
            windowed = sb("windowed", [T, B * NG])
            xmax = sb("xmax", [T, NG])
            xsum = sb("xsum", [T, NG])

            RING = 5
            ring = ps("ring", [P, RING, 512])
            s_ps = ps("s_ps", [P, NG * GK])

            cs_in = sem("cs_in")
            wqr_in = sem("wqr_in")
            uvw_in = sem("uvw_in")
            pads_set = sem("pads_set")
            rows_in = [sem(f"rows_in{k}") for k in range(2)]
            rows_rot = sem("rows_rot")
            pool_chain = sem("pool_chain")
            idx_out = sem("idx_out")
            idx_go = sem("idx_go")
            xb_out = sem("xb_out")
            vo_mm = sem("vo_mm")
            vo_out = sem("vo_out")
            fill = sem("fill")
            drain_act = sem("drain_act")
            drain_dve = sem("drain_dve")
            s_mm = sem("s_mm")
            s_sub = sem("s_sub")
            s_exp = sem("s_exp")
            p_set = sem("p_set")

            LEAD = "AA" + "AAAA" + "DD" + "AAAA"
            TAIL = "AA" + "AAAA" + "D"
            TURN = LEAD + TAIL + "-"
            Y = 6

            def place(b, m):
                return len(LEAD) + b * len(LEAD + TAIL) + m

            def slot(m):
                return (len(LEAD) + m) % RING

            def emptied(b, m, who, first):
                if m < 0 and first:
                    return LEAD[:m].count(who) + LEAD[m:m + 1 or None].count(who)
                before = b * TURN.count(who) + LEAD.count(who)
                return before + (TURN[:m + 1].count(who) if m >= 0 else -(TURN + " ")[m:-1].count(who))

            assert len(TURN) % RING == 0
            block = st.enter_context(nc.Block())

            @block.sync
            def _(sp):
                sp.dma_start(wqr[:], a["w_qr"]).then_inc(wqr_in, 16)
                sp.dma_start(cos_q[:], a["cos_q"]).then_inc(cs_in, 16)
                sp.dma_start(sin_q[:], a["sin_q"]).then_inc(cs_in, 16)
                sp.dma_start(wuv_t[:], a["w_uv_t"]).then_inc(uvw_in, 16)
                sp.dma_start(wvo[:], a["w_o"]).then_inc(uvw_in, 16)

            @block.gpsimd
            def _(pool):
                count = Chain(pool, pool_chain)

                def fetch(b, half, i, first=False):
                    if not first:
                        pool.wait_ge(fill, place(b - 2, len(LEAD) + Y))
                        pool.sem_inc(idx_go, 1)
                    pool.tensor_copy(idx_b[half][:], row_idx[:, bass.ds(b * NT, NT)]).then_inc(idx_out, 1)
                    pool.wait_ge(idx_out, b + 1)
                    pool.sem_inc(idx_go, 1)
                    for t in range(NT):
                        pool.indirect_dma_start(rows_kv[half][:, t, :], None, table[:],
                                                bass.IndirectOffsetOnAxis(idx_b[half][:, t:t + 1], 0))\
                            .then_inc(rows_in[half], 16)
                    pool.wait_ge(rows_in[half], 16 * NT * (i + 1))
                    pool.sem_inc(idx_go, 1)
                    k = rows_kv[half][:, :, KVC:KW].rearrange("p t (s r) -> p t s r", s=2)
                    pool.tensor_tensor(turned[:, :, 0, :], k[:, :, 1, :], sin_q[:, :, 0, :], ALU.mult)
                    count(pool.tensor_tensor(turned[:, :, 1, :], k[:, :, 0, :], sin_q[:, :, 1, :], ALU.mult))
                    count(pool.tensor_tensor(k, k, cos_q[:], ALU.mult))
                    pool.tensor_tensor(k, k, turned[:], ALU.add).then_inc(rows_rot, 1)

                def copy_x(b):
                    pool.tensor_copy(x_b[:], x_all[:, b, :]).then_inc(xb_out, 1)

                copy_x(0)
                pool.memset(q_all[0:ROPE, 1, :, :], 0.0).then_inc(pads_set, 1)
                pool.memset(k_t[0:ROPE, 1, :], 0.0).then_inc(pads_set, 1)
                pool.wait_ge(cs_in, 32)
                fetch(0, 0, 0, True)
                pool.wait_ge(fill, 1)
                copy_x(1)
                fetch(1, 1, 0, True)
                start = count.value
                with pool.Fori(1, B // 2) as i:
                    for half in range(2):
                        b = 2 * i + half
                        count.turn(start, b - 2, 2)
                        pool.wait_ge(fill, place(b - 2, 1))
                        pool.sem_inc(idx_go, 1)
                        copy_x(b)
                        fetch(b, half, i)

            @block.tensor
            def _(pe):
                def lead(b, half, i, ahead=True, first=False):
                    def emptied_here(m, who):
                        return emptied(b, m, who, first) if ahead else LEAD[:m + 1].count(who)

                    def bank(m):
                        n = slot(m) if ahead else m % RING
                        if ahead or m >= RING:
                            for drain, who in ((drain_act, "A"), (drain_dve, "D")):
                                if not isinstance(emptied_here(m - RING, who), int) or emptied_here(m - RING, who):
                                    pe.wait_ge(drain, emptied_here(m - RING, who))
                        return ring[:, n, :]

                    r = bank(0)
                    pe.wait_ge(xb_out, b + 2 if ahead else 1)
                    for c in range(DC):
                        mm = pe.transpose(r[:, c * T:(c + 1) * T], x_b[:, c * P:(c + 1) * P], ident[0:T, 0:T])
                    mm.then_inc(fill, 1)
                    r = bank(1)
                    pe.wait_ge(drain_act, emptied_here(0, "A"))
                    for j in range(2):
                        for c in range(DC):
                            mm = pe.matmul(r[0:QH, j * T:(j + 1) * T], wdq[:, c, j * QH:(j + 1) * QH], xb_t[:, c, :],
                                           start=(c == 0), stop=(c == DC - 1))
                    mm.then_inc(fill, 1)
                    for k in range(6):
                        r = bank(2 + k)
                        if k == 0:
                            pe.wait_ge(drain_act, emptied_here(1, "A"))
                        for h in range(4):
                            for j in range(2):
                                if k < 4:
                                    w = wqn[:, j, 4 * k + h, :]
                                else:
                                    pair = 4 * (k - 4) + h
                                    w = wqr[:, j, pair * P:(pair + 1) * P]
                                mm = pe.matmul(r[:, h * T:(h + 1) * T], w, qc_t[:, j, :],
                                               start=(j == 0), stop=(j == 1))
                        mm.then_inc(fill, 1)
                    pe.wait_ge(rows_rot, b + 2 if ahead else 1)
                    for k in range(4):
                        r = bank(8 + k)
                        for t in range(4):
                            rows = rows_kv[half][:, 4 * (k % 2) + t, :]
                            cols = rows[:, 0:KVC] if k < 2 else rows[:, KW - P:KW]
                            mm = pe.transpose(r[:, t * P:(t + 1) * P], cols, ident[:])
                        mm.then_inc(fill, 1)

                def scores(b, first=False):
                    for drain, who in ((drain_act, "A"), (drain_dve, "D")):
                        pe.wait_ge(drain, LEAD.count(who) if first else emptied(b - 1, len(LEAD) - 1, who, False))
                    for g in range(NG):
                        for part in range(2):
                            q = q_all[:, part, g * GQ:(g + 1) * GQ, :].rearrange("p q h -> p (q h)")
                            mm = pe.matmul(s_ps[0:T, g * GK:(g + 1) * GK], q, k_t[:, part, g * GK:(g + 1) * GK],
                                           start=(part == 0), stop=(part == 1))
                    mm.then_inc(s_mm, 1)

                def tail(b, half, last):
                    at = 0 if last else len(LEAD)

                    def done(m):
                        n = b * TURN.count("A") + LEAD.count("A") + TAIL[:m + 1].count("A")
                        pe.wait_ge(drain_act, n if last else n + LEAD.count("A"))

                    def bank(m):
                        if last and m >= RING:
                            done(m - RING)
                        else:
                            for drain, who in ((drain_act, "A"), (drain_dve, "D")):
                                pe.wait_ge(drain, emptied(b, at + m - RING, who, False))
                        return ring[:, slot(at + m), :]

                    pe.wait_ge(p_set, b + 1)
                    flat = prob[:].rearrange("p g k -> p (g k)")
                    for k in range(2):
                        r = bank(k)
                        for t in range(4):
                            n = 4 * k + t
                            mm = pe.transpose(r[:, t * T:(t + 1) * T], flat[:, n * P:(n + 1) * P], ident[0:T, 0:T])
                        mm.then_inc(fill, 1)
                    for k in range(2):
                        even, odd = bank(2 + 2 * k), bank(3 + 2 * k)
                        done(k)
                        for t in range(4):
                            n = 4 * k + t
                            for r, rows in ((even, slice(0, GK)), (odd, slice(GK, P))):
                                mm = pe.matmul(r[:, t * T:(t + 1) * T], rows_kv[half][rows, n, 0:KVC],
                                               prob_t[rows, n, :], start=True, stop=True)
                                if t == 3:
                                    mm.then_inc(fill, 1)
                    r = bank(Y)
                    done(Y - 1)
                    oc = oc_t[:].rearrange("p g q h -> p (g q) h")
                    for h in range(NH):
                        mm = pe.matmul(r[0:T, :], oc[:, :, h], wvo[:, h, :], start=(h == 0), stop=(h == NH - 1))
                    mm.then_inc(fill, 1)

                pe.wait_ge(pads_set, 2)
                pe.wait_ge(wqr_in, 16)
                pe.wait_ge(xwq_in, 16)
                lead(0, 0, 0, ahead=False)
                scores(0, first=True)
                lead(0, 1, 0, first=True)
                pe.wait_ge(uvw_in, 32)
                pe.wait_ge(s_sub, 1)
                for h in range(NH):
                    if h >= 2:
                        pe.wait_ge(vo_out, h - 1)
                    pe.matmul(s_ps[:, (h % 2) * 512:(h % 2 + 1) * 512], wuv_t[:, h, :], wvo[:, h, :],
                              start=True, stop=True).then_inc(vo_mm, 1)
                pe.wait_ge(vo_out, NH)
                tail(0, 0, False)
                scores(1)
                with pe.Fori(0, B // 2 - 1) as i:
                    for k in range(2):
                        b = 2 * i + 1 + k
                        lead(b, k, i + 1)
                        tail(b, 1 - k, False)
                        scores(b + 1)
                tail(B - 1, 1, True)

            @block.scalar
            def _(act):
                def store(count, bank, dst, rows=P, width=512, scale=1.0, **kw):
                    src = ring[rows if isinstance(rows, slice) else slice(0, rows), bank, 0:width]
                    if kw:
                        src = src.rearrange("p (u v) -> p u v", **kw)
                    act.wait_ge(fill, count)
                    act.activation(dst, src, ACT.Copy, scale=scale).then_inc(drain_act, 1)

                def lead(b, ahead, between):
                    def put(m, dst, **kw):
                        if ahead:
                            store(place(b, m) + 1, slot(m), dst, **kw)
                        else:
                            store(m + 1, m % RING, dst, **kw)

                    put(0, xb_t[:], width=DC * T, u=DC)
                    put(1, qc_t[:], rows=QH, width=2 * T, scale=(XHD + ROPE) ** -0.5, u=2)
                    between()
                    for k in range(4):
                        put(2 + k, q_all[:, 0, :, 4 * k:4 * k + 4].rearrange("p t h -> p h t"), width=4 * T, u=4)
                    for k in range(2):
                        put(8 + k, k_t[:, 0, k * 512:(k + 1) * 512])
                    for k in range(2):
                        put(10 + k, k_t[ROPE:P, 1, k * 512:(k + 1) * 512], rows=slice(ROPE, P))

                def exp(b):
                    act.wait_ge(s_sub, b + 1)
                    act.activation(prob[:], prob[:], ACT.Exp).then_inc(s_exp, 1)

                def tail(b, last):
                    def put(m, dst, **kw):
                        m += 0 if last else len(LEAD)
                        store(place(b, m) + 1, slot(m), dst, **kw)

                    for k in range(2):
                        put(k, prob_t[:, 4 * k:4 * k + 4, :], width=4 * T, u=4)
                    oc = oc_t[:].rearrange("p (s e) q h -> p s e (q h)", e=2)
                    for k in range(2):
                        for odd in range(2):
                            put(2 + 2 * k + odd, oc[:, 4 * k:4 * k + 4, odd, :], width=4 * T, u=4)

                lead(0, False, lambda: None)
                lead(0, True, lambda: exp(0))
                for h in range(NH):
                    act.wait_ge(vo_mm, h + 1)
                    act.activation(wvo[:, h, :], s_ps[:, (h % 2) * 512:(h % 2 + 1) * 512], ACT.Copy).then_inc(vo_out, 1)
                tail(0, False)
                with act.Fori(1, B - 1) as b:
                    lead(b, True, lambda: exp(b))
                    tail(b, False)
                exp(B - 1)
                tail(B - 1, True)
                act.wait_ge(var_set, 2)
                act.activation(rstd[:], rstd[:], ACT.Sqrt).then_inc(std_set, 1)

            @block.vector
            def _(dve):
                def rotary_queries(b, ahead):
                    for k in range(2):
                        m = 6 + k
                        dve.wait_ge(fill, place(b, m) + 1 if ahead else m + 1)
                        src = ring[:, slot(m) if ahead else m % RING, 0:4 * T].rearrange("p (h t) -> p h t", h=4)
                        dst = q_all[ROPE:P, 1, :, 8 * k:8 * k + 8].rearrange("p t (h e) -> p e h t", e=2)
                        dve.tensor_copy(dst[:, 0], src[0:ROPE])
                        dve.tensor_copy(dst[:, 1], src[ROPE:P]).then_inc(drain_dve, 1)

                def window(b):
                    segs = seg_rows[:, bass.ds(b * NG, NG)]
                    chain(dve.tensor_tensor(mask[:], segs.unsqueeze(2).broadcast_to([T, NG, GK]),
                                            off_mask[:].unsqueeze(1).broadcast_to([T, NG, GK]), ALU.add))
                    chain(dve.tensor_scalar(outside[:], mask[:], 0.0, None, ALU.is_lt))
                    chain(dve.scalar_tensor_tensor(outside[:], mask[:], float(LK - 1), outside[:], ALU.is_gt, ALU.max))
                    chain(dve.tensor_copy(outside[:, :, GK - 1], windowed[:, bass.ds(b * NG, NG)]))

                def shift(b):
                    dve.wait_ge(s_mm, b + 1)
                    chain(dve.scalar_tensor_tensor(prob[:], outside[:], NEG,
                                                   s_ps[0:T].rearrange("p (g k) -> p g k", g=NG), ALU.mult, ALU.add))
                    chain(dve.tensor_reduce(xmax[:], prob[:], AX.X, ALU.max))
                    dve.tensor_tensor(prob[:], prob[:], xmax[:].unsqueeze(2).broadcast_to([T, NG, GK]),
                                      ALU.subtract).then_inc(s_sub, 1)

                def normalise(b):
                    dve.wait_ge(s_exp, b + 1)
                    chain(dve.tensor_reduce(xsum[:], prob[:], AX.X, ALU.add))
                    chain(dve.reciprocal(xsum[:], xsum[:]))
                    dve.tensor_tensor(prob[:], prob[:], xsum[:].unsqueeze(2).broadcast_to([T, NG, GK]),
                                      ALU.mult).then_inc(p_set, 1)

                def add_y(b, last=False):
                    m = Y if last else len(LEAD) + Y
                    dve.wait_ge(fill, place(b, m) + 1)
                    x = x_all[:, b, :]
                    chain(dve.tensor_tensor(x, x, ring[0:T, slot(m), :], ALU.add))
                    dve.nop().then_inc(drain_dve, 1)
                    chain(dve.bn_stats(stats[:, b, :], x))

                chain(dve.tensor_scalar(windowed[:], seg_rows[:], 0.0, None, ALU.is_ge))
                chain(dve.scalar_tensor_tensor(windowed[:], seg_rows[:], float(LK - 1 + SPAN - 1), windowed[:],
                                               ALU.is_le, ALU.mult))
                dve.wait_ge(pads_set, 2)
                window(0)
                rotary_queries(0, False)
                shift(0)
                rotary_queries(0, True)
                normalise(0)
                window(1)
                add_y(0)
                shift(1)
                start = chain.value
                PER = 2 + 4 + 2 + 2
                with dve.Fori(0, B - 2) as turn:
                    chain.turn(start, turn, PER)
                    b = turn + 1
                    rotary_queries(b, True)
                    normalise(b)
                    window(b + 1)
                    add_y(b)
                    shift(b + 1)
                chain.turned(start, B - 2, PER)
                normalise(B - 1)
                add_y(B - 1, True)
                layer_norm(dve, 2)

        with ExitStack() as st:
            def sb(name, shape, dt=F32):
                return st.enter_context(nc.sbuf_tensor(name, shape, dt))

            def ps(name, shape, dt=F32):
                return st.enter_context(nc.psum_tensor(name, shape, dt))

            xy = sb("xy", [T, D])
            xmag = sb("xmag", [T, D])
            xq = sb("xq", [T, D], BF16)
            xq_t = sb("xq_t", [P, DC, T], BF16)
            gate = sb("gate", [T, 2, 512])
            upv = sb("upv", [T, 2, 512])
            hid = sb("hid", [T, F])
            hy = sb("hy", [T, F])
            hmag = sb("hmag", [T, F])
            hq = sb("hq", [T, F], BF16)
            hq_t = sb("hq_t", [P, FC, T], BF16)
            ysum = sb("ysum", [T, D])
            xs = [sb(f"xs{k}", [T, 4]) for k in range(2)]
            hs = [sb(f"hs{k}", [T, 4]) for k in range(2)]

            gu_ps = ps("gu_ps", [T, 2, 2, 512])
            xt_ps = ps("xt_ps", [P, 1024], BF16)
            ht_ps = ps("ht_ps", [P, 2048], BF16)
            y3_ps = ps("y3_ps", [T, 512])

            xinv_set = sem("xinv_set")
            x_scaled = sem("x_scaled")
            xq_set = sem("xq_set")
            xt_mm = sem("xt_mm")
            xt_out = sem("xt_out")
            gu_mm = sem("gu_mm")
            gu_out = sem("gu_out")
            gate_set = sem("gate_set")
            silu_out = sem("silu_out")
            hinv_set = sem("hinv_set")
            h_scaled = sem("h_scaled")
            hq_set = sem("hq_set")
            ht_mm = sem("ht_mm")
            ht_out = sem("ht_out")
            y3_mm = sem("y3_mm")
            y3_out = sem("y3_out")
            normed = sem("normed")
            stored = sem("stored")

            NCH = len(FCH)
            block = st.enter_context(nc.Block())

            @block.sync
            def _(sp):
                for b in range(B):
                    sp.wait_ge(normed, b + 1)
                    sp.dma_start(out[b], x_all[:, b, :]).then_inc(stored, 16)
                sp.wait_ge(stored, 16 * B)

            @block.tensor
            def _(pe):
                def turn_x(b):
                    pe.wait_ge(xq_set, b + 1)
                    for c in range(DC):
                        mm = pe.transpose(xt_ps[:, c * P:c * P + T], xq[:, c * P:(c + 1) * P], identb[0:T, 0:T])
                    mm.then_inc(xt_mm, 1)

                def gate_up(b, half, n):
                    if n == 0:
                        pe.wait_ge(xt_out, b + 1)
                    at, width = FCH[n]
                    pe.wait_ge(gu_out, NCH * b + n + 1)
                    for m, w in enumerate((gate_w, up_w)):
                        for c in range(DC):
                            mm = pe.matmul(gu_ps[:, (NCH * half + n) % 2, m, 0:width], xq_t[:, c, :],
                                           w[:, c, at:at + width], start=(c == 0), stop=(c == DC - 1))
                    mm.then_inc(gu_mm, 1)

                def batch(b, half, last):
                    if not last:
                        turn_x(b + 1)
                        gate_up(b + 1, 1 - half, 0)
                        gate_up(b + 1, 1 - half, 1)
                    pe.wait_ge(hq_set, b + 1)
                    for c in range(FC):
                        mm = pe.transpose(ht_ps[:, c * P:c * P + T], hq[:, c * P:(c + 1) * P], identb[0:T, 0:T])
                    mm.then_inc(ht_mm, 1)
                    if not last:
                        gate_up(b + 1, 1 - half, 2)
                    pe.wait_ge(ht_out, b + 1)
                    pe.wait_ge(y3_out, b + 1)
                    for c in range(FC):
                        mm = pe.matmul(y3_ps[:], hq_t[:, c, :], down_w[:, c, :], start=(c == 0), stop=(c == FC - 1))
                    mm.then_inc(y3_mm, 1)

                turn_x(0)
                for n in range(NCH):
                    gate_up(0, 0, n)
                with pe.Fori(0, B // 2 - 1) as i:
                    for half in range(2):
                        batch(2 * i + half, half, False)
                batch(B - 2, 0, False)
                batch(B - 1, 1, True)

            @block.scalar
            def _(act):
                def scale_x(b, half):
                    act.wait_ge(xinv_set, b + 1)
                    act.activation(xmag[:], x_all[:, b, :], ACT.Copy, scale=xs[half][:, 3:4])
                    act.activation(xy[:], x_all[:, b, :], ACT.Copy, scale=xs[half][:, 2:3]).then_inc(x_scaled, 1)

                def store_x(b):
                    act.wait_ge(xt_mm, b + 1)
                    act.activation(xq_t[:], xt_ps[:, 0:DC * P].rearrange("p (c t) -> p c t", c=DC)[:, :, 0:T],
                                   ACT.Copy).then_inc(xt_out, 1)

                def batch(b, half, ahead):
                    for n, (at, width) in enumerate(FCH):
                        g = gate[:, (NCH * half + n) % 2, 0:width]
                        act.wait_ge(gate_set, NCH * b + n + 1)
                        act.activation(g, g, ACT.Silu).then_inc(silu_out, 1)
                    act.wait_ge(hinv_set, b + 1)
                    act.activation(hmag[:], hid[:], ACT.Copy, scale=hs[half][:, 3:4])
                    act.activation(hy[:], hid[:], ACT.Copy, scale=hs[half][:, 2:3]).then_inc(h_scaled, 1)
                    if ahead:
                        store_x(b + 1)
                    if ahead == 2:
                        scale_x(b + 2, half)
                    act.wait_ge(ht_mm, b + 1)
                    act.activation(hq_t[:], ht_ps[:, 0:FC * P].rearrange("p (c t) -> p c t", c=FC)[:, :, 0:T],
                                   ACT.Copy).then_inc(ht_out, 1)

                scale_x(0, 0)
                store_x(0)
                scale_x(1, 1)
                with act.Fori(0, B // 2 - 1) as i:
                    for half in range(2):
                        batch(2 * i + half, half, 2)
                batch(B - 2, 0, 1)
                batch(B - 1, 1, 0)
                act.wait_ge(var_set, 3)
                act.activation(rstd[:], rstd[:], ACT.Sqrt).then_inc(std_set, 1)

            @block.vector
            def _(dve):
                def scales(s, src, signal):
                    chain(dve.tensor_reduce(s[:, 0:1], src, AX.X, ALU.max, apply_absolute_value=True))
                    chain(dve.tensor_scalar(s[:, 1:2], s[:, 0:1], 1.0 / FP8_MAX, None, ALU.mult))
                    chain(dve.reciprocal(s[:, 2:3], s[:, 1:2]))
                    dve.tensor_scalar(s[:, 3:4], s[:, 2:3], 2.0 ** 20, None, ALU.mult).then_inc(signal, 1)

                def round_to(q, y, mag, signal):
                    chain(magic_bits(dve, mag[:].bitcast(U32)))
                    chain(magic_add(dve, y[:], mag[:]))
                    magic_sub(dve, q[:], y[:], mag[:]).then_inc(signal, 1)

                def round_x(b):
                    dve.wait_ge(x_scaled, b + 1)
                    round_to(xq, xy, xmag, xq_set)

                def gated(b, half, n):
                    at, width = FCH[n]
                    k = (NCH * half + n) % 2
                    dve.wait_ge(gu_mm, NCH * b + n + 1)
                    dve.scalar_tensor_tensor(gate[:, k, 0:width], gu_ps[:, k, 0, 0:width], xs[half][:, 1:2],
                                             gate_s[:, at:at + width], ALU.mult, ALU.mult).then_inc(gate_set, 1)
                    dve.scalar_tensor_tensor(upv[:, k, 0:width], gu_ps[:, k, 1, 0:width], xs[half][:, 1:2],
                                             up_s[:, at:at + width], ALU.mult, ALU.mult).then_inc(gu_out, 1)

                def hidden(b, half, n):
                    at, width = FCH[n]
                    k = (NCH * half + n) % 2
                    dve.wait_ge(silu_out, NCH * b + n + 1)
                    dve.wait_ge(gu_out, NCH * b + n + 3)
                    chain(dve.tensor_tensor(hid[:, at:at + width], gate[:, k, 0:width], upv[:, k, 0:width], ALU.mult))

                def add_y(b, half):
                    dve.wait_ge(y3_mm, b + 1)
                    chain(dve.scalar_tensor_tensor(ysum[:], y3_ps[:], hs[half][:, 1:2], down_s[:], ALU.mult, ALU.mult))
                    dve.nop().then_inc(y3_out, 1)
                    x = x_all[:, b, :]
                    chain(dve.tensor_tensor(x, x, ysum[:], ALU.add))
                    chain(dve.bn_stats(stats[:, b, :], x))

                def batch(b, half, ahead, first=False):
                    gated(b, half, 0)
                    gated(b, half, 1)
                    hidden(b, half, 0)
                    hidden(b, half, 1)
                    gated(b, half, 2)
                    hidden(b, half, 2)
                    scales(hs[half], hid[:], hinv_set)
                    if ahead:
                        round_x(b + 1)
                    if ahead == 2:
                        scales(xs[half], x_all[:, b + 2, :], xinv_set)
                    if not first:
                        add_y(b - 1, 1 - half)
                    dve.wait_ge(h_scaled, b + 1)
                    round_to(hq, hy, hmag, hq_set)

                dve.sem_inc(gu_out, 2)
                dve.sem_inc(y3_out, 1)
                scales(xs[0], x_all[:, 0, :], xinv_set)
                round_x(0)
                scales(xs[1], x_all[:, 1, :], xinv_set)
                batch(0, 0, 2, True)
                batch(1, 1, 2)
                start = chain.value
                PER = 3 + 3 + 2 + 3 + 3 + 2
                with dve.Fori(1, B // 2 - 1) as i:
                    for half in range(2):
                        chain.turn(start, 2 * i + half - 2, PER)
                        batch(2 * i + half, half, 2)
                chain.turned(start, B - 4, PER)
                batch(B - 2, 0, 1)
                batch(B - 1, 1, 0)
                add_y(B - 1, 1)
                layer_norm(dve, 3, normed)


def rope_tables():
    half = ROPE // 2
    inv_freq = (np.float32(1.0) / np.float32(10000.0) ** (np.arange(half, dtype=np.float32) / np.float32(half)))
    ang = np.arange(LK, dtype=np.float32)[:, None] * inv_freq.astype(np.float32)
    c, s = np.cos(ang), np.sin(ang)
    return np.concatenate([c, c, -s, s], axis=1).astype(np.float32)


def kernel(x, ctx_2048, itok_BxS_0_1023, L0_attn_q1_w, L0_attn_k1_w, L0_attn_q2_w, L0_attn_k2_w, L0_attn_v_w,
           L0_attn_o_w, L0_attn_lambda_param, L0_xattn_W_kvc, L0_xattn_W_dq, L0_xattn_W_uq, L0_xattn_W_qr,
           L0_xattn_W_uk, L0_xattn_W_kr, L0_xattn_W_uv, L0_xattn_W_o, L0_ffn_w_gate, L0_ffn_w_up, L0_ffn_w_down,
           L0_ffn_up_reorder_index, L0_ffn_down_reorder_index):
    import concourse.bacc as bacc
    from concourse.bass_utils import run_bass_kernel_spmd
    import ml_dtypes

    def rows(w):
        return np.ascontiguousarray(w.reshape(-1, P, w.shape[1]).transpose(1, 0, 2))

    def swap(w):
        w = w.reshape(w.shape[0], -1, 2, ROPE // 2)
        return w[:, :, ::-1, :].reshape(w.shape[0], -1)

    x, ctx, seg = np.asarray(x), np.asarray(ctx_2048), np.asarray(itok_BxS_0_1023)
    uq, uk, uv = (np.asarray(w) for w in (L0_xattn_W_uq, L0_xattn_W_uk, L0_xattn_W_uv))
    qr, kr = np.asarray(L0_xattn_W_qr), np.asarray(L0_xattn_W_kr)
    lam = np.asarray(L0_attn_lambda_param).reshape(1, NJ, HG)
    table = rope_tables()

    col = np.arange(GK)
    in_span = col < GQ * SPAN
    query = np.arange(T) // NH
    off = np.where(in_span[None, :] & (query[:, None] == col[None, :] // SPAN),
                   -(col % SPAN)[None, :], NEG).astype(np.float32)
    row_c = np.stack([np.where(in_span, -(col % SPAN), 0), in_span], 1).astype(np.float32)
    base = np.arange(B)[None, :] * TROWS + np.where(in_span, 0, LK)[:, None]
    base = np.repeat(np.concatenate([base, base]), NT, axis=1).astype(np.float32)
    groups = seg.reshape(B, NG, GQ)
    seg_rows = np.repeat(groups.transpose(2, 0, 1).reshape(GQ, B * NG), NH, axis=0)
    by_col = np.concatenate([np.repeat(groups, SPAN, axis=2), groups[:, :, 0:1]], axis=2)
    seg_keys = by_col.reshape(B * NT, P).T

    where = (2 * GQ * np.arange(NT)[None, :] + np.concatenate([col // SPAN, GQ + col // SPAN])[:, None]) % T
    cos_q = table[where][:, :, 0:ROPE].reshape(P, NT, 2, ROPE // 2)
    sin_q = -table[where][:, :, ROPE:2 * ROPE].reshape(P, NT, 2, ROPE // 2)
    arrays = {
        "x": x,
        "x_t": x.reshape(B, T, DC, P).transpose(0, 3, 2, 1),
        "w_in": np.stack([rows(np.asarray(w).T) for w in (L0_attn_q1_w, L0_attn_k1_w, L0_attn_q2_w, L0_attn_k2_w,
                                                          L0_attn_v_w)]),
        "w_attn_o": rows(np.asarray(L0_attn_o_w).T),
        "lam": np.broadcast_to(lam, (T, NJ, HG)),
        "ctx_t": ctx.reshape(B, LK, DC, P).transpose(0, 3, 2, 1),
        "w_kvc": rows(np.asarray(L0_xattn_W_kvc)), "w_kvc_t": np.asarray(L0_xattn_W_kvc).T,
        "w_kr2": np.concatenate([kr, swap(kr)], axis=1),
        "w_dq": rows(np.asarray(L0_xattn_W_dq)),
        "w_uq_t": uq.reshape(QC, NH, XHD).transpose(2, 1, 0), "w_uk_t": uk.reshape(KVC, NH, XHD).transpose(2, 1, 0),
        "w_qr": qr.reshape(2, QH, NH * ROPE).transpose(1, 0, 2), "cos_q": cos_q, "sin_q": sin_q,
        "w_uv_t": uv.reshape(KVC, NH, XHD).transpose(2, 1, 0), "w_o": rows(np.asarray(L0_xattn_W_o)),
        "w_gate": np.asarray(L0_ffn_w_gate), "w_up": np.asarray(L0_ffn_w_up),
        "w_down": np.asarray(L0_ffn_w_down).reshape(DC, P, F),
        "order": np.asarray(L0_ffn_down_reorder_index).reshape(FC, P).T,
        "seg_rows": seg_rows, "seg_keys": seg_keys,
        "ident": np.eye(P, dtype=np.float32), "identb": np.eye(P).astype(ml_dtypes.bfloat16),
        "off_mask": off, "row_c": np.concatenate([row_c, row_c]), "row_base": base,
        "rope_k": table.reshape(KTILES, KROWS, 2 * ROPE).transpose(1, 0, 2),
    }
    arrays = {n: np.ascontiguousarray(v) for n, v in arrays.items()}
    nc = bacc.Bacc("TRN2", target_bir_lowering=False, num_devices=1)
    ins = {n: nc.dram_tensor(f"in_{n}", v.shape, mybir.dt.from_np(v.dtype), kind="ExternalInput").ap()
           for n, v in arrays.items()}
    out = nc.dram_tensor("out", (B, T, D), F32, kind="ExternalOutput").ap()
    build(nc, ins, out)
    r = run_bass_kernel_spmd(nc, [{f"in_{n}": v for n, v in arrays.items()}], core_ids=[0])
    return r.results[0]["out"]
```

```python
from contextlib import ExitStack

import numpy as np

import concourse.bass as bass
from concourse import mybir

ALU = mybir.AluOpType
ACT = mybir.ActivationFunctionType
F32 = mybir.dt.float32
BF16 = mybir.dt.bfloat16
I32 = mybir.dt.int32
U32 = mybir.dt.uint32
AX = mybir.AxisListType

P = 128
B, T, D = 8, 112, 512
DC = D // P
NH, HD = 16, 32
HG = 4
NJ = NH // HG
NPROJ = 5
LK = 375
KTILES, KROWS = 3, 125
KVC, QC, ROPE, XHD = 128, 192, 64, 128
QH = QC // 2
SPAN = 9
GQ = 7
NG = T // GQ
GK = 64
NT = NG * GK // P
TROWS = LK + 1
KW = KVC + ROPE
F = 1408
FC = F // P
FCH = [(0, 512), (512, 512), (1024, 384)]
DOWN_LO = 6 * P
DOWN_COLS = ((0, DOWN_LO), (DOWN_LO, F))
FP8_MAX = 448.0
NEG = -1e30
EPS = 1e-5
MAGIC_MIN = 1.5 * 2.0 ** 14



class Chain:

    def __init__(self, eng, sem):
        self.eng, self.sem, self.base, self.n = eng, sem, 0, 0

    def mark(self, ins):
        ins.then_inc(self.sem, 1)
        self.n += 1
        return self.base + self.n

    def need(self, value):
        self.eng.wait_ge(self.sem, value)

    def __call__(self, ins):
        self.need(self.mark(ins))

    def turn(self, start, step, per):
        self.base, self.n = start + step * per, 0

    def turned(self, start, steps, per):
        assert self.n == per, (self.n, per)
        self.base, self.n = start + steps * per, 0

    @property
    def value(self):
        return self.base + self.n



def magic_bits(dve, scaled_bits):
    return dve.tensor_scalar(scaled_bits, scaled_bits, 0x7F800000, 0x00400000, ALU.bitwise_and, ALU.bitwise_or)


def magic_add(dve, y, magic):
    return dve.scalar_tensor_tensor(y, magic, MAGIC_MIN, y, ALU.max, ALU.add)


def magic_sub(dve, minus_q, summed, magic):
    return dve.scalar_tensor_tensor(minus_q, magic, MAGIC_MIN, summed, ALU.max, ALU.subtract)


class Pieces:

    def __init__(self, sb, sem, chain, ident, tag, width, raw_widths, slots):
        self.chain, self.ident = chain, ident
        self.raw = [sb(f"{tag}raw{k}", [P, n]) for k, n in enumerate(raw_widths)]
        self.mag = [sb(f"{tag}mag{k}", [P, width]) for k in range(2)]
        self.summ = [sb(f"{tag}summ{k}", [P, width]) for k in range(2)]
        self.qt = [sb(f"{tag}qt{k}", [P, width], BF16) for k in range(2)]
        self.diag = [sb(f"{tag}diag{k}", [P, P]) for k in range(2)]
        self.amax = sb(f"{tag}amax", [P, 1])
        self.wsc = [sb(f"{tag}wsc{k}", [P, 1]) for k in range(slots)]
        self.inv = [sb(f"{tag}inv{k}", [P, 2]) for k in range(slots)]
        self.raw_in = [sem(f"{tag}raw_in{k}") for k in range(2)]
        self.gathers = sem(f"{tag}gathers")
        self.order_set = sem(f"{tag}order_set")
        self.inv_set = sem(f"{tag}inv_set")
        self.scaled = sem(f"{tag}scaled")
        self.quant = sem(f"{tag}quant")
        self.piece_mm = sem(f"{tag}piece_mm")
        self.piece_out = sem(f"{tag}piece_out")

    def gather(self, pool, order, order_c, chunk, n, half, a):
        pool.tensor_copy(order_c[:], order[:, bass.ds(chunk, 1)]).then_inc(self.order_set, 1)
        pool.wait_ge(self.order_set, n + 1)
        pool.sem_inc(self.gathers, 1)
        for m, name in enumerate(("w_gate", "w_up")):
            pool.indirect_dma_start(self.raw[half][:, m * D:(m + 1) * D], None, a[name],
                                    bass.IndirectOffsetOnAxis(order_c[:], 0)).then_inc(self.raw_in[half], 16)

    def inverse(self, dve, src, slot, pieces=1):
        wsc, inv = self.wsc[slot], self.inv[slot]
        self.chain(dve.tensor_reduce(self.amax[:], src, AX.X, ALU.max, apply_absolute_value=True))
        self.chain(dve.tensor_scalar(wsc[:], self.amax[:], 1.0 / FP8_MAX, None, ALU.mult))
        self.chain(dve.reciprocal(inv[:, 0:1], wsc[:]))
        dve.tensor_scalar(inv[:, 1:2], inv[:, 0:1], 2.0 ** 20, None, ALU.mult).then_inc(self.inv_set, pieces)

    def scale(self, act, p, src, k, slot):
        act.wait_ge(self.inv_set, p + 1)
        act.wait_ge(self.quant, p + 1)
        width = src.shape[-1]
        act.activation(self.mag[k][:, 0:width], src, ACT.Copy, scale=self.inv[slot][:, 1:2])
        act.activation(self.summ[k][:, 0:width], src, ACT.Copy, scale=self.inv[slot][:, 0:1]).then_inc(self.scaled, 1)

    def round(self, dve, p, width, k, slot=None):
        dve.wait_ge(self.piece_mm, p + 1)
        if slot is not None:
            dve.tensor_scalar(self.diag[k][:], self.ident[:], self.wsc[slot][:], None, ALU.mult)
        dve.wait_ge(self.scaled, p + 1)
        bits, y = self.mag[k][:, 0:width], self.summ[k][:, 0:width]
        self.chain(magic_bits(dve, bits.bitcast(U32)))
        self.chain(magic_add(dve, y, bits))
        magic_sub(dve, self.qt[k][:, 0:width], y, bits).then_inc(self.quant, 1)

    def transpose(self, pe, p, width, k, bank, identb, ones, scales=True):
        pe.wait_ge(self.quant, p + 3)
        for h in range(width // P):
            mm = pe.transpose(bank.bitcast(BF16)[:, h * P:(h + 1) * P], self.qt[k][:, h * P:(h + 1) * P], identb[:])
        if scales:
            mm = pe.matmul(bank[0:T, 512 - P:512], ones[:, 0:T], self.diag[k][:], start=True, stop=True)
        mm.then_inc(self.piece_mm, 1)

    def store(self, act, p, width, bank, w, s=None):
        act.wait_ge(self.piece_mm, p + 3)
        ins = act.activation(w, bank.bitcast(BF16)[:, 0:width].rearrange("p (h n) -> p h n", n=P), ACT.Copy)
        if s is not None:
            ins = act.activation(s, bank[0:T, 512 - P:512], ACT.Copy)
        ins.then_inc(self.piece_out, 1)


def build(nc, a, out):
    table = nc.dram_tensor("key_table", [B * TROWS, KW], F32)

    table_rows = table[:].rearrange("(b r) n -> b r n", b=B)
    top = ExitStack()
    with top:
        def sem(name):
            return top.enter_context(nc.semaphore(name))

        def keep(name, shape, dt=F32):
            return top.enter_context(nc.sbuf_tensor(name, shape, dt))

        x_all = keep("x_all", [T, B, D])
        ident = keep("ident", [P, P])
        identb = keep("identb", [P, P], BF16)
        ones = keep("ones", [P, P])
        wdq = keep("wdq", [P, DC, QC])
        wqn = keep("wqn", [QH, 2, NH, XHD])
        gate_w = keep("gate_w", [P, DC, F], BF16)
        up_w = keep("up_w", [P, DC, F], BF16)
        down_w = keep("down_w", [P, FC, D], BF16)
        gate_s = keep("gate_s", [T, F])
        up_s = keep("up_s", [T, F])
        down_s = keep("down_s", [T, D])
        stats = keep("stats", [T, B, 6])
        mv = keep("mv", [T, B, 2])
        rstd = keep("rstd", [T, B])
        seg_rows = keep("seg_rows", [T, B * NG])
        row_idx = keep("row_idx", [P, B * NT], I32)
        off_mask = keep("off_mask", [T, GK])
        idx_b = [keep(f"idx_b{k}", [P, NT], I32) for k in range(2)]
        rows_kv = [keep(f"rows_kv{k}", [P, NT, KW]) for k in range(2)]
        turned = keep("turned", [P, NT, 2, ROPE // 2])
        cos_q = keep("cos_q", [P, NT, 2, ROPE // 2])
        sin_q = keep("sin_q", [P, NT, 2, ROPE // 2])

        consts_in = sem("consts_in")
        weights_in = sem("weights_in")
        xwq_in = sem("xwq_in")
        x_in = sem("x_in")
        dve_chain = sem("dve_chain")
        chain = Chain(nc.vector, dve_chain)

        var_set = sem("var_set")
        std_set = sem("std_set")

        cs_in = sem("cs_in")
        rows_in = [sem(f"rows_in{k}") for k in range(2)]
        rows_rot = sem("rows_rot")
        idx_out = sem("idx_out")
        idx_go = sem("idx_go")
        pool_chain = sem("pool_chain")
        count = Chain(nc.gpsimd, pool_chain)

        def fetch(pool, b, half, i):
            pool.tensor_copy(idx_b[half][:], row_idx[:, bass.ds(b * NT, NT)]).then_inc(idx_out, 1)
            pool.wait_ge(idx_out, b + 1)
            pool.sem_inc(idx_go, 1)
            for t in range(NT):
                pool.indirect_dma_start(rows_kv[half][:, t, :], None, table[:],
                                        bass.IndirectOffsetOnAxis(idx_b[half][:, t:t + 1], 0))\
                    .then_inc(rows_in[half], 16)
            pool.wait_ge(rows_in[half], 16 * NT * (i + 1))
            pool.sem_inc(idx_go, 1)
            k = rows_kv[half][:, :, KVC:KW].rearrange("p t (s r) -> p t s r", s=2)
            pool.tensor_tensor(turned[:, :, 0, :], k[:, :, 1, :], sin_q[:, :, 0, :], ALU.mult)
            count(pool.tensor_tensor(turned[:, :, 1, :], k[:, :, 0, :], sin_q[:, :, 1, :], ALU.mult))
            count(pool.tensor_tensor(k, k, cos_q[:], ALU.mult))
            pool.tensor_tensor(k, k, turned[:], ALU.add).then_inc(rows_rot, 1)

        NORM_STEPS = (range(0, B - 1), range(B - 1, B))

        def norm_variance(dve, step):
            bs = NORM_STEPS[step]
            for b in bs:
                last = dve.bn_aggr(mv[:, b, :], stats[:, b, :])
            chain(last)
            chain(dve.tensor_scalar(rstd[:, bs[0]:bs[-1] + 1], mv[:, bs[0]:bs[-1] + 1, 1], EPS, None, ALU.add))
            dve.nop().then_inc(var_set, 1)

        def norm_deviation(act, before, step):
            bs = NORM_STEPS[step]
            act.wait_ge(var_set, before + step + 1)
            act.activation(rstd[:, bs[0]:bs[-1] + 1], rstd[:, bs[0]:bs[-1] + 1], ACT.Sqrt).then_inc(std_set, 1)

        def normalise_x(dve, before, step, done=None):
            bs = NORM_STEPS[step]
            dve.wait_ge(std_set, before + step + 1)
            chain(dve.reciprocal(rstd[:, bs[0]:bs[-1] + 1], rstd[:, bs[0]:bs[-1] + 1]))
            for b in bs:
                last = dve.tensor_scalar(x_all[:, b, :], x_all[:, b, :], mv[:, b, 0:1], rstd[:, b:b + 1],
                                         ALU.subtract, ALU.mult)
                if done is not None:
                    last.then_inc(done, 1)
            if done is None:
                chain(last)

        weights = top.enter_context(ExitStack())
        w_in = weights.enter_context(nc.sbuf_tensor("w_in", [P, NPROJ, DC, D], F32))
        order = weights.enter_context(nc.sbuf_tensor("order", [P, FC], I32))
        order_c = [weights.enter_context(nc.sbuf_tensor(f"order_c{k}", [P, 1], I32)) for k in range(2)]
        EARLY = B // 2
        x_t = [weights.enter_context(nc.sbuf_tensor(f"x_t{k}", [P, DC, T], F32)) for k in range(2)]
        xt_in = [sem(f"xt_in{k}") for k in range(2)]
        w_in_sem = sem("w_in_sem")
        w_out_sem = sem("w_out_sem")

        with ExitStack() as st:
            def sb(name, shape, dt=F32):
                return st.enter_context(nc.sbuf_tensor(name, shape, dt))

            def ps(name, shape, dt=F32):
                return st.enter_context(nc.psum_tensor(name, shape, dt))

            ctx_uq = sb("ctx_uq", [P, NH * QC])
            ctx_t = [ctx_uq[:, k * DC * LK:(k + 1) * DC * LK].rearrange("p (c n) -> p c n", c=DC) for k in range(2)]
            wuq_t = ctx_uq[:].rearrange("p (h n) -> p h n", h=NH)
            wuk_t = sb("wuk_t", [P, NH, KVC])
            wkvx = sb("wkvx", [P, DC, 2 * P])
            wkvc_t = sb("wkvc_t", [P, D])
            wkr2 = sb("wkr2", [P, 2 * ROPE])
            rope_k = sb("rope_k", [KROWS, KTILES, 2 * ROPE])
            key_rows = [sb(f"key_rows{k}", [KROWS, KTILES, KW]) for k in range(2)]
            rot = sb("rot", [KROWS, KTILES, 2 * ROPE])
            mean_row = [sb(f"mean_row{k}", [1, KW]) for k in range(2)]
            pieces = Pieces(sb, sem, chain, ident, "", DOWN_LO, (2 * D, F), 3)
            seg_i = sb("seg_i", [T, B * NG], I32)
            seg_k = sb("seg_k", [P, B * NT], I32)
            seg_f = sb("seg_f", [P, B * NT])
            row_c = sb("row_c", [P, 2])
            row_base = sb("row_base", [P, B * NT])

            key_ps = ps("key_ps", [P, 2, 1024])
            join_ps = ps("join_ps", [P, 2, 512])
            mean_ps = join_ps[0:1, 1, 0:KW]
            piece_ps = ps("piece_ps", [P, 2, 512])

            ctx_in = [sem(f"ctx_in{k}") for k in range(2)]
            key_mm = sem("key_mm")
            mean_mm = sem("mean_mm")
            kvc_out = sem("kvc_out")
            rope_out = sem("rope_out")
            mean_out = sem("mean_out")
            table_out = [sem(f"table_out{k}") for k in range(2)]
            wuq_in = sem("wuq_in")
            wuq_rest_in = sem("wuq_rest_in")
            join_mm = sem("join_mm")
            join_out = sem("join_out")
            ones_set = sem("ones_set")
            ord_in = sem("ord_in")

            block = st.enter_context(nc.Block())
            KV_DMAS = 2 * 16
            UQ_FIRST = 6
            assert UQ_FIRST * QC <= DC * LK
            GU, DOWN = 0, 1
            COLS = (((0, D), (0, D)), DOWN_COLS)

            def keys_of(half):
                return key_ps[0:KROWS, half, 0:768].rearrange("p (k n) -> p k n", k=KTILES)

            @block.sync
            def _(sp):
                for t_, n_ in ((wkvc_t, "w_kvc_t"), (wkr2, "w_kr2")):
                    sp.dma_start(t_[:], a[n_]).then_inc(weights_in, 16)
                sp.dma_start(wkvx[:, :, 0:P], a["w_kvc"]).then_inc(weights_in, 16)
                sp.dma_start(ctx_t[0], a["ctx_t"][0]).then_inc(ctx_in[0], 16)
                for t_, n_ in ((ident, "ident"), (identb, "identb"), (off_mask, "off_mask"),
                               (rope_k, "rope_k"), (row_c, "row_c"), (row_base, "row_base"),
                               (seg_i, "seg_rows"), (seg_k, "seg_keys")):
                    sp.dma_start(t_[:], a[n_]).then_inc(consts_in, 16)
                sp.dma_start(ctx_t[1], a["ctx_t"][1]).then_inc(ctx_in[1], 16)

                def store_keys(b, half):
                    sp.wait_ge(kvc_out, b + 1)
                    sp.wait_ge(rope_out, b + 1)
                    sp.dma_start(table_rows[b, 0:LK].rearrange("(k p) n -> p k n", k=KTILES),
                                 key_rows[half][:]).then_inc(table_out[half], 16)

                def store_mean(b, half):
                    sp.wait_ge(mean_out, b + 1)
                    sp.dma_start(table_rows[b, LK:TROWS], mean_row[half][:]).then_inc(table_out[half], 16)

                def turn(b, half, first=False):
                    sp.wait_ge(key_mm, b + 1)
                    sp.dma_start(ctx_t[half], a["ctx_t"][b + 2]).then_inc(ctx_in[half], 16)
                    if not first:
                        sp.dma_start(w_in[:, bass.ds(b - 1, 1)], a["w_in"][bass.ds(b - 1, 1)]
                                     .rearrange("m p c n -> p m c n")).then_inc(w_in_sem, 16)
                    store_keys(b, half)
                    if not first:
                        store_mean(b - 1, 1 - half)

                turn(0, 0, True)
                turn(1, 1)
                with sp.Fori(1, B // 2 - 1) as i:
                    for half in range(2):
                        turn(2 * i + half, half)
                sp.dma_start(wuk_t[:], a["w_uk_t"]).then_inc(wuq_in, 16)
                sp.wait_ge(key_mm, B - 1)
                sp.dma_start(wuq_t[:, 0:UQ_FIRST], a["w_uq_t"][:, 0:UQ_FIRST]).then_inc(wuq_in, 16)
                store_keys(B - 2, 0)
                store_mean(B - 3, 1)
                sp.wait_ge(key_mm, B)
                sp.dma_start(wuq_t[:, UQ_FIRST:NH], a["w_uq_t"][:, UQ_FIRST:NH]).then_inc(wuq_rest_in, 16)
                for k in range(2):
                    sp.dma_start(x_t[k][:], a["x_t"][k]).then_inc(xt_in[k], 16)
                store_mean(B - 2, 0)
                store_keys(B - 1, 1)
                store_mean(B - 1, 1)
                sp.dma_start(x_all[:], a["x"].rearrange("b t d -> t b d")).then_inc(x_in, 16)
                sp.dma_start(wdq[:], a["w_dq"]).then_inc(xwq_in, 16)
                for half in range(2):
                    sp.wait_ge(table_out[half], B // 2 * KV_DMAS)

            @block.gpsimd
            def _(pool):
                pool.memset(ones[:], 1.0).then_inc(ones_set, 1)
                pool.dma_start(order[:], a["order"]).then_inc(ord_in, 16)
                pool.wait_ge(ord_in, 16)
                pieces.gather(pool, order, order_c[0], 0, 0, GU, a)
                pool.dma_start(pieces.raw[DOWN][:], a["w_down"][0]).then_inc(pieces.raw_in[DOWN], 16)
                with pool.Fori(1, EARLY) as i:
                    pool.wait_ge(pieces.scaled, 4 * i - 2)
                    pool.sem_inc(pieces.gathers, 1)
                    pieces.gather(pool, order, order_c[0], i, i, GU, a)
                    pool.wait_ge(pieces.scaled, 4 * i)
                    pool.sem_inc(pieces.gathers, 1)
                    pool.dma_start(pieces.raw[DOWN][:], a["w_down"][i]).then_inc(pieces.raw_in[DOWN], 16)

            @block.scalar
            def _(act):
                act.sem_inc(pieces.piece_out, 2)
                act.wait_ge(join_mm, 1)
                act.activation(wkvx[:, :, P:2 * P], join_ps[:, 0, :].rearrange("p (c n) -> p c n", c=DC),
                               ACT.Copy).then_inc(join_out, 1)

                def scale_pair(b, kind):
                    for m, (at, end) in enumerate(COLS[kind]):
                        src = pieces.raw[GU][:, m * D:(m + 1) * D] if kind == GU else pieces.raw[DOWN][:, at:end]
                        pieces.scale(act, 2 * b + m, src, m, m if kind == GU else 2)

                def store_pair(b, i, kind):
                    for m, (at, end) in enumerate(COLS[kind]):
                        cols = bass.ds(i * P, P)
                        if kind == GU:
                            w, s = (gate_w, gate_s) if m == 0 else (up_w, up_s)
                            pieces.store(act, 2 * b + m, D, piece_ps[:, m, :], w[:, :, cols], s[:, cols])
                        else:
                            pieces.store(act, 2 * b + m, end - at, piece_ps[:, m, :],
                                         down_w[:, at // P:end // P, cols], down_s[:, cols] if m == 0 else None)

                def store_mean(b, half):
                    act.wait_ge(mean_mm, b + 1)
                    act.activation(mean_row[half][:], mean_ps, ACT.Copy, scale=1.0 / LK).then_inc(mean_out, 1)

                def turn(b, half, i, peeled=False):
                    scale_pair(b, half)
                    act.wait_ge(key_mm, b + 1)
                    if not peeled:
                        act.wait_ge(table_out[half], i * KV_DMAS)
                    act.activation(key_rows[half][:, :, 0:KVC], keys_of(half)[:, :, 0:KVC],
                                   ACT.Copy).then_inc(kvc_out, 1)
                    if not (peeled and half == 0):
                        store_mean(b - 1, 1 - half)
                        store_pair(b - 1, i - 1 + half, 1 - half)

                turn(0, 0, 0, True)
                turn(1, 1, 0, True)
                with act.Fori(1, B // 2) as i:
                    for half in range(2):
                        turn(2 * i + half, half, i)
                for k in range(NH // 2):
                    act.wait_ge(join_mm, k + 2)
                    act.activation(wqn[:, :, 2 * k:2 * k + 2, :],
                                   join_ps[0:QH, k % 2, :].rearrange("p (h j n) -> p j h n", h=2, j=2),
                                   ACT.Copy).then_inc(join_out, 1)
                store_mean(B - 1, 1)
                store_pair(B - 1, EARLY - 1, DOWN)

            @block.tensor
            def _(pe):
                pe.sem_inc(pieces.piece_mm, 2)
                pe.wait_ge(weights_in, 16 * 3)
                for c in range(DC):
                    mm = pe.matmul(join_ps[:, 0, c * P:(c + 1) * P], wkvc_t[:, c * P:(c + 1) * P], wkr2[:],
                                   start=True, stop=True)
                mm.then_inc(join_mm, 1)
                pe.wait_ge(join_out, 1)
                pe.wait_ge(ones_set, 1)

                def mean(b, half, first=False):
                    pe.wait_ge(kvc_out, b + 1)
                    pe.wait_ge(rope_out, b + 1)
                    if not first:
                        pe.wait_ge(mean_out, b)
                    for k in range(KTILES):
                        mm = pe.matmul(mean_ps, ones[0:KROWS, 0:1], key_rows[half][:, k, :],
                                       start=(k == 0), stop=(k == KTILES - 1))
                    mm.then_inc(mean_mm, 1)

                def turn_pair(b, kind):
                    for m, (at, end) in enumerate(COLS[kind]):
                        pe.wait_ge(pieces.piece_out, 2 * b + m + 1)
                        pieces.transpose(pe, 2 * b + m, end - at, m, piece_ps[:, m, :], identb, ones,
                                         kind == GU or m == 0)

                def turn(b, half, i, first=False):
                    pe.wait_ge(ctx_in[half], 16 * (i + 1))
                    if not (isinstance(b, int) and b < 2):
                        pe.wait_ge(rope_out, b - 1)
                    for k in range(KTILES):
                        for c in range(DC):
                            mm = pe.matmul(key_ps[0:KROWS, half, k * 256:(k + 1) * 256],
                                           ctx_t[half][:, c, k * KROWS:(k + 1) * KROWS], wkvx[:, c, :],
                                           start=(c == 0), stop=(c == DC - 1))
                    mm.then_inc(key_mm, 1)
                    if not first:
                        mean(b - 1, 1 - half, isinstance(b, int) and b == 1)
                        turn_pair(b - 1, 1 - half)

                turn(0, 0, 0, True)
                pe.wait_ge(consts_in, 16 * 8)
                turn(1, 1, 0)
                with pe.Fori(1, B // 2) as i:
                    for half in range(2):
                        turn(2 * i + half, half, i)
                pe.wait_ge(wuq_in, 2 * 16)
                pe.wait_ge(mean_out, B - 1)
                for k in range(NH // 2):
                    if k > 0:
                        pe.wait_ge(join_out, k)
                    if k == UQ_FIRST // 2:
                        pe.wait_ge(wuq_rest_in, 16)
                    for h in range(2):
                        for j in range(2):
                            n = 2 * h + j
                            mm = pe.matmul(join_ps[0:QH, k % 2, n * P:(n + 1) * P],
                                           wuq_t[:, 2 * k + h, j * QH:(j + 1) * QH], wuk_t[:, 2 * k + h, :],
                                           start=True, stop=True)
                    mm.then_inc(join_mm, 1)
                pe.wait_ge(join_out, 1 + NH // 2)
                mean(B - 1, 1)
                turn_pair(B - 1, DOWN)

            @block.vector
            def _(dve):
                dve.sem_inc(pieces.quant, 2)

                def pair(b, kind, count, first=False):
                    raw = pieces.raw[kind]
                    if kind == GU:
                        dve.wait_ge(pieces.raw_in[GU], 32 * count)
                        pieces.inverse(dve, raw[:, 0:D], 0)
                        if not first:
                            pieces.round(dve, 2 * b - 1, F - DOWN_LO, 1)
                        pieces.inverse(dve, raw[:, D:2 * D], 1)
                        pieces.round(dve, 2 * b, D, 0, 0)
                    else:
                        dve.wait_ge(pieces.raw_in[DOWN], 16 * count)
                        pieces.inverse(dve, raw[:], 2, 2)
                        pieces.round(dve, 2 * b - 1, D, 1, 1)
                        pieces.round(dve, 2 * b, DOWN_LO, 0, 2)

                def rotate_keys(b, half, i, peeled=False):
                    if not peeled:
                        dve.wait_ge(table_out[half], i * KV_DMAS)
                    dve.wait_ge(kvc_out, b + 1)
                    chain(dve.tensor_tensor(rot[:], keys_of(half)[:, :, KVC:KVC + 2 * ROPE], rope_k[:], ALU.mult))
                    dve.tensor_tensor(key_rows[half][:, :, KVC:KW], rot[:, :, 0:ROPE], rot[:, :, ROPE:2 * ROPE],
                                      ALU.add).then_inc(rope_out, 1)

                dve.wait_ge(consts_in, 16 * 8)
                pair(0, GU, 1, True)
                rotate_keys(0, 0, 0, True)
                pair(1, DOWN, 1)
                rotate_keys(1, 1, 0, True)
                PER = (3 + 3 + 2 + 2) + (3 + 2 + 2) + 2
                start = chain.value
                with dve.Fori(1, B // 2) as i:
                    chain.turn(start, i - 1, PER)
                    for kind in (GU, DOWN):
                        pair(2 * i + kind, kind, i + 1)
                        rotate_keys(2 * i + kind, kind, i)
                chain.turned(start, B // 2 - 1, PER)
                pieces.round(dve, 2 * B - 1, F - DOWN_LO, 1)

                chain(dve.tensor_copy(seg_f[:], seg_k[:]))
                chain(dve.tensor_scalar(seg_f[:], seg_f[:], row_c[:, 0:1], 0.0, ALU.add, ALU.max))
                chain(dve.tensor_scalar(seg_f[:], seg_f[:], float(LK - 1), row_c[:, 1:2], ALU.min, ALU.mult))
                chain(dve.tensor_tensor(row_idx[:], seg_f[:], row_base[:], ALU.add))
                chain(dve.tensor_copy(seg_rows[:], seg_i[:]))

        with ExitStack() as st:
            def sb(name, shape, dt=F32):
                return st.enter_context(nc.sbuf_tensor(name, shape, dt))

            def ps(name, shape, dt=F32):
                return st.enter_context(nc.psum_tensor(name, shape, dt))

            w_out = sb("w_out", [P, DC, D])
            qk = [[sb(f"qk{m}{k}", [P, NJ, T]) for k in range(2)] for m in range(4)]
            v = [sb(f"v{k}", [T, D]) for k in range(2)]
            prob = [sb(f"prob{k}", [T, HG, 2, T]) for k in range(2)]
            att = [sb(f"att{k}", [T, HG, T]) for k in range(2)]
            att_t = [sb(f"att_t{k}", [T, HG, T]) for k in range(2)]
            o_t = sb("o_t", [P, NJ, T])
            lam = sb("lam", [T, NJ, HG])
            smax = sb("smax", [T, HG, 2])
            ssum = sb("ssum", [T, HG, 2])
            sinv = sb("sinv", [T, HG, 2])

            gu = Pieces(sb, sem, chain, ident, "gu_", D, (2 * D, 2 * D), 2)
            assert EARLY + B - 1 == FC

            proj_ps = ps("proj_ps", [P, 2, 512])
            score_ps = ps("score_ps", [T, HG, 512])
            att_ps = ps("att_ps", [T, 512])
            o_ps = ps("o_ps", [P, 512])

            lam_in = sem("lam_in")
            proj_mm = sem("proj_mm")
            proj_out = sem("proj_out")
            score_mm = sem("score_mm")
            score_sub = sem("score_sub")
            prob_exp = sem("prob_exp")
            att_set = sem("att_set")
            att_turn = sem("att_turn")
            att_out = sem("att_out")
            pv_mm = sem("pv_mm")
            o_out = sem("o_out")
            y_mm = sem("y_mm")
            y_out = sem("y_out")

            block = st.enter_context(nc.Block())

            V = NPROJ - 1

            def projected(b, m):
                return NPROJ * b + m + 1

            @block.sync
            def _(sp):
                sp.dma_start(cos_q[:], a["cos_q"]).then_inc(cs_in, 16)
                sp.dma_start(sin_q[:], a["sin_q"]).then_inc(cs_in, 16)
                sp.dma_start(w_out[:], a["w_attn_o"]).then_inc(w_out_sem, 16)
                sp.dma_start(lam[:], a["lam"]).then_inc(lam_in, 16)
                with sp.Fori(1, B // 2) as i:
                    for half in range(2):
                        b = 2 * i + half
                        sp.wait_ge(proj_mm, projected(b - 2, V))
                        sp.dma_start(x_t[half][:], a["x_t"][b]).then_inc(xt_in[half], 16)

            @block.gpsimd
            def _(pool):
                for half in range(2):
                    gu.gather(pool, order, order_c[half], EARLY + half, half, half, a)
                with pool.Fori(1, (B - 2) // 2) as i:
                    for half in range(2):
                        b = 2 * i + half
                        pool.wait_ge(gu.scaled, 2 * b - 2)
                        pool.sem_inc(gu.gathers, 1)
                        gu.gather(pool, order, order_c[half], EARLY + b, b, half, a)
                pool.wait_ge(gu.scaled, 2 * (B - 2) - 2)
                gu.gather(pool, order, order_c[0], EARLY + B - 2, B - 2, 0, a)
                pool.wait_ge(cs_in, 32)
                fetch(pool, 0, 0, 0)
                fetch(pool, 1, 1, 0)

            @block.tensor
            def _(pe):
                def project(b, half, i, m, bank):
                    if m == 0:
                        pe.wait_ge(xt_in[half], 16 * (i + 1))
                    if m == V:
                        for c in range(DC):
                            mm = pe.matmul(proj_ps[0:T, bank, :], x_t[half][:, c, :], w_in[:, V, c, :],
                                           start=(c == 0), stop=(c == DC - 1))
                    else:
                        for j in range(NJ):
                            for c in range(DC):
                                mm = pe.matmul(proj_ps[:, bank, j * T:(j + 1) * T],
                                               w_in[:, m, c, j * P:(j + 1) * P], x_t[half][:, c, :],
                                               start=(c == 0), stop=(c == DC - 1))
                    mm.then_inc(proj_mm, 1)

                def scores(b, half, j, first=False):
                    if j == 0:
                        pe.wait_ge(proj_out, projected(b, 3))
                    if not (first and j == 0):
                        pe.wait_ge(score_sub, 4 * b + j)
                    for s in range(2):
                        for r in range(HG):
                            rows = slice(r * HD, (r + 1) * HD)
                            mm = pe.matmul(score_ps[:, r, s * T:(s + 1) * T], qk[2 * s][half][rows, j, :],
                                           qk[2 * s + 1][half][rows, j, :], start=True, stop=True)
                    mm.then_inc(score_mm, 1)

                def turn(b, j, first=False):
                    pe.wait_ge(att_set, 4 * b + j + 1)
                    if not (first and j == 0):
                        pe.wait_ge(att_out, 4 * b + j)
                    for r in range(HG):
                        mm = pe.transpose(att_ps[:, r * T:(r + 1) * T], att[j % 2][:, r, :], ident[0:T, 0:T])
                    mm.then_inc(att_turn, 1)

                def heads_out(b, half, j, first=False):
                    pe.wait_ge(att_out, 4 * b + j + 1)
                    if j == 0:
                        pe.wait_ge(proj_out, projected(b, V))
                        if not first:
                            pe.wait_ge(o_out, b)
                    for r in range(HG):
                        h = HG * j + r
                        mm = pe.matmul(o_ps[r * HD:(r + 1) * HD, j * T:(j + 1) * T],
                                       v[half][:, h * HD:(h + 1) * HD], att_t[j % 2][:, r, :],
                                       start=True, stop=True)
                    if j == NJ - 1:
                        mm.then_inc(pv_mm, 1)

                def join_heads(b):
                    pe.wait_ge(o_out, b + 1)
                    for j in range(NJ):
                        mm = pe.matmul(proj_ps[0:T, 0, :], o_t[:, j, :], w_out[:, j, :],
                                       start=(j == 0), stop=(j == NJ - 1))
                    mm.then_inc(y_mm, 1)

                def piece(p, k):
                    gu.transpose(pe, p, D, k, proj_ps[:, 1, :], identb, ones)

                def batch(b, half, i, first=False, last=False):
                    def ahead(m, bank):
                        if not last:
                            project(b + 1, 1 - half, i + half, m, bank)

                    scores(b, half, 0, first)
                    if not first:
                        turn(b - 1, 2)
                    project(b, half, i, V, 0)
                    if not (first or last):
                        pe.wait_ge(gu.piece_out, 2 * b + 1)
                    ahead(0, 1)
                    if not first:
                        heads_out(b - 1, 1 - half, 2)

                    scores(b, half, 1)
                    if not first:
                        turn(b - 1, 3)
                    pe.wait_ge(proj_out, projected(b, V))
                    ahead(1, 0)
                    if not first:
                        if last:
                            pe.wait_ge(gu.piece_out, 2 * b + 1)
                        else:
                            pe.wait_ge(proj_out, projected(b + 1, 0))
                        piece(2 * b - 1, 1)
                        heads_out(b - 1, 1 - half, 3)

                    scores(b, half, 2)
                    turn(b, 0, first)
                    if not last:
                        pe.wait_ge(proj_out, projected(b + 1, 1))
                    if not first:
                        join_heads(b - 1)
                        if not last:
                            pe.wait_ge(gu.piece_out, 2 * b + 2)
                    ahead(2, 1)
                    heads_out(b, half, 0, first)

                    scores(b, half, 3)
                    turn(b, 1)
                    if not first:
                        pe.wait_ge(y_out, b)
                    ahead(3, 0)
                    if not last:
                        pe.wait_ge(proj_out, projected(b + 1, 2))
                        piece(2 * b, 0)
                    heads_out(b, half, 1)

                pe.sem_inc(gu.piece_mm, 2)
                pe.wait_ge(w_in_sem, 16 * NPROJ)
                for m in range(V):
                    if m >= 2:
                        pe.wait_ge(proj_out, m - 1)
                    project(0, 0, 0, m, m % 2)
                batch(0, 0, 0, first=True)
                pe.wait_ge(w_out_sem, 16)
                batch(1, 1, 0)
                with pe.Fori(1, B // 2 - 1) as i:
                    for half in range(2):
                        batch(2 * i + half, half, i)
                batch(B - 2, 0, B // 2 - 1)
                batch(B - 1, 1, B // 2 - 1, last=True)
                for j in (2, 3):
                    turn(B - 1, j)
                    heads_out(B - 1, 1, j)
                join_heads(B - 1)

            @block.scalar
            def _(act):
                def store(b, half, m, bank):
                    act.wait_ge(proj_mm, projected(b, m))
                    if m == V:
                        act.activation(v[half][:], proj_ps[0:T, bank, :], ACT.Copy).then_inc(proj_out, 1)
                    else:
                        act.activation(qk[m][half][:], proj_ps[:, bank, 0:NJ * T].rearrange("p (j t) -> p j t", j=NJ),
                                       ACT.Copy, scale=1.0 if m % 2 else HD ** -0.5).then_inc(proj_out, 1)

                def exp(b, j):
                    act.wait_ge(score_sub, 4 * b + j + 1)
                    act.activation(prob[j % 2][:], prob[j % 2][:], ACT.Exp).then_inc(prob_exp, 1)

                def store_att(b, j):
                    act.wait_ge(att_turn, 4 * b + j + 1)
                    act.activation(att_t[j % 2][:], att_ps[:, 0:HG * T].rearrange("p (r t) -> p r t", r=HG),
                                   ACT.Copy).then_inc(att_out, 1)

                def store_heads(b):
                    act.wait_ge(pv_mm, b + 1)
                    act.activation(o_t[:], o_ps[:, 0:NJ * T].rearrange("p (j t) -> p j t", j=NJ),
                                   ACT.Copy).then_inc(o_out, 1)

                def scale_piece(b, half, m):
                    gu.scale(act, 2 * b + m, gu.raw[half][:, m * D:(m + 1) * D], m, m)

                def store_piece(b, m, w, s):
                    cols = bass.ds((EARLY + b) * P, P)
                    gu.store(act, 2 * b + m, D, proj_ps[:, 1, :], w[:, :, cols], s[:, cols])

                def batch(b, half, first=False, last=False):
                    def ahead(m, bank):
                        if not last:
                            store(b + 1, 1 - half, m, bank)

                    if not first:
                        store_att(b - 1, 2)
                    exp(b, 0)
                    store(b, half, V, 0)
                    ahead(0, 1)

                    if not first:
                        store_att(b - 1, 3)
                    exp(b, 1)
                    if not last:
                        scale_piece(b, half, 0)
                    ahead(1, 0)
                    if not first:
                        store_piece(b - 1, 1, up_w, up_s)
                        store_heads(b - 1)

                    store_att(b, 0)
                    exp(b, 2)
                    ahead(2, 1)

                    store_att(b, 1)
                    exp(b, 3)
                    ahead(3, 0)
                    if not last:
                        scale_piece(b, half, 1)
                        store_piece(b, 0, gate_w, gate_s)

                act.sem_inc(gu.piece_out, 2)
                for m in range(V):
                    store(0, 0, m, m % 2)
                batch(0, 0, first=True)
                batch(1, 1)
                with act.Fori(1, B // 2 - 1) as i:
                    for half in range(2):
                        batch(2 * i + half, half)
                batch(B - 2, 0)
                batch(B - 1, 1, last=True)
                store_att(B - 1, 2)
                norm_deviation(act, 0, 0)
                store_att(B - 1, 3)
                store_heads(B - 1)
                norm_deviation(act, 0, 1)

            @block.vector
            def _(dve):
                def shift(b, j):
                    dve.wait_ge(score_mm, 4 * b + j + 1)
                    s = score_ps[:, :, 0:2 * T].rearrange("p r (s k) -> p r s k", s=2)
                    chain(dve.tensor_reduce(smax[:], s, AX.X, ALU.max))
                    dve.tensor_tensor(prob[j % 2][:], s, smax[:].unsqueeze(3).broadcast_to([T, HG, 2, T]),
                                      ALU.subtract).then_inc(score_sub, 1)

                def combine(b, j):
                    p = prob[j % 2]
                    dve.wait_ge(prob_exp, 4 * b + j + 1)
                    chain(dve.tensor_reduce(ssum[:], p[:], AX.X, ALU.add))
                    chain(dve.reciprocal(sinv[:], ssum[:]))
                    chain(dve.tensor_tensor(sinv[:, :, 1], sinv[:, :, 1], lam[:, j, :], ALU.mult))
                    chain(dve.tensor_tensor(p[:], p[:], sinv[:].unsqueeze(3).broadcast_to([T, HG, 2, T]), ALU.mult))
                    dve.tensor_tensor(att[j % 2][:], p[:, :, 0, :], p[:, :, 1, :], ALU.subtract).then_inc(att_set, 1)

                def add_y(b):
                    dve.wait_ge(y_mm, b + 1)
                    x_b = x_all[:, b, :]
                    chain(dve.tensor_tensor(x_b, x_b, proj_ps[0:T, 0, :], ALU.add))
                    dve.nop().then_inc(y_out, 1)
                    chain(dve.bn_stats(stats[:, b, :], x_b))

                def inverse(b, half, i, m):
                    if m == 0:
                        dve.wait_ge(gu.raw_in[half], 32 * (i + 1))
                    gu.inverse(dve, gu.raw[half][:, m * D:(m + 1) * D], m)

                def batch(b, half, i, first=False, last=False):
                    shift(b, 0)
                    if not first:
                        combine(b - 1, 3)
                    if not last:
                        inverse(b, half, i, 0)
                    shift(b, 1)
                    combine(b, 0)
                    if not last:
                        gu.round(dve, 2 * b, D, 0, 0)
                    shift(b, 2)
                    combine(b, 1)
                    if not first:
                        add_y(b - 1)
                    if last:
                        norm_variance(dve, 0)
                    else:
                        inverse(b, half, i, 1)
                    shift(b, 3)
                    combine(b, 2)
                    if not last:
                        gu.round(dve, 2 * b + 1, D, 1, 1)

                PER = NJ * 5 + 2 + 2 * (3 + 2)
                dve.sem_inc(gu.quant, 2)
                dve.wait_ge(lam_in, 16)
                dve.wait_ge(x_in, 16)
                batch(0, 0, 0, first=True)
                batch(1, 1, 0)
                start = chain.value
                with dve.Fori(1, B // 2 - 1) as i:
                    for half in range(2):
                        b = 2 * i + half
                        chain.turn(start, b - 2, PER)
                        batch(b, half, i)
                chain.turned(start, B - 4, PER)
                batch(B - 2, 0, B // 2 - 1)
                batch(B - 1, 1, B // 2 - 1, last=True)
                combine(B - 1, 3)
                normalise_x(dve, 0, 0)
                add_y(B - 1)
                norm_variance(dve, 1)
                normalise_x(dve, 0, 1)

        weights.close()
        xq_t = keep("xq_t", [P, B, DC, T], BF16)
        xq_s = keep("xq_s", [T, B])

        with ExitStack() as st:
            def sb(name, shape, dt=F32):
                return st.enter_context(nc.sbuf_tensor(name, shape, dt))

            def ps(name, shape, dt=F32):
                return st.enter_context(nc.psum_tensor(name, shape, dt))

            wvo = sb("wvo", [P, NH, D])
            wuv_t = sb("wuv_t", [P, NH, KVC])
            wqr = sb("wqr", [QH, 2, NH * ROPE])
            q_all = sb("q_all", [P, 2, T, NH])
            k_t = sb("k_t", [P, 2, NG * GK])
            x_b = sb("x_b", [T, D])
            xb_t = sb("xb_t", [P, DC, T])
            qc_t = sb("qc_t", [QH, 2, T])
            prob = sb("xprob", [T, NG, GK])
            mask = sb("mask", [T, NG, GK])
            outside = sb("outside", [T, NG, GK], BF16)
            prob_t = sb("prob_t", [P, NT, T])
            oc_t = sb("oc_t", [P, NG, GQ, NH])
            windowed = sb("windowed", [T, B * NG])
            mask_rows = mask[:].rearrange("t g k -> t (g k)")
            xy, xmag = mask_rows[:, 0:D], mask_rows[:, D:2 * D]
            xq = sb("xq", [T, D], BF16)
            xs = sb("xs", [T, 4])
            stats_b = sb("stats_b", [T, 6])
            mv_b = sb("mv_b", [T, 2])
            rstd_b = sb("rstd_b", [T, 1])
            xmax = sb("xmax", [T, NG])
            xsum = sb("xsum", [T, NG])

            RING = 5
            ring = ps("ring", [P, RING, 512])
            s_ps = ps("s_ps", [P, NG * GK])

            wqr_in = sem("wqr_in")
            uvw_in = sem("uvw_in")
            pads_set = sem("pads_set")
            xb_out = sem("xb_out")
            vo_mm = sem("vo_mm")
            vo_out = sem("vo_out")
            fill = sem("fill")
            drain_act = sem("drain_act")
            drain_dve = sem("drain_dve")
            s_mm = sem("s_mm")
            s_sub = sem("s_sub")
            s_exp = sem("s_exp")
            p_set = sem("p_set")
            xinv_set = sem("xinv_set")
            x_scaled = sem("x_scaled")
            xq_set = sem("xq_set")
            dve_go = sem("dve_go")

            START = "AA" + "AAAA" + "DD" + "AAAA" + "---" + "AA" + "-" + "AAAA" + "DD" + "-"
            PT, KT, PV, XT, QCT, Y, QN, QR, XQ = 0, 2, 6, 10, 11, 12, 13, 17, 19
            TURN = "AA" + "AAAA" + "AAAA" + "A" + "A" + "D" + "AAAA" + "DD" + "A"
            ENDS = {B - 2: "AA" + "AAAA" + "AAAA" + "--D-------", B - 1: "AA" + "----" + "AAAA" + "--D-----AA"}
            AHEAD0, AHEAD1 = 0, 15
            LOOPED = B - 2
            assert len(START) % RING == 0 and len(TURN) % RING == 0

            def letters(b):
                return START if isinstance(b, int) and b < 0 else ENDS.get(b, TURN) if isinstance(b, int) else TURN

            def filled(b, m, who="AD"):
                def n(text):
                    return sum(text.count(w) for w in who)

                here = n(letters(b)[:m + 1])
                if isinstance(b, int) and b < 0:
                    return here
                if isinstance(b, int) and b == B - 1:
                    return n(START) + LOOPED * n(TURN) + n(ENDS[B - 2]) + here
                return n(START) + b * n(TURN) + here

            def last_user(b, m):
                back, n = 0, m - RING
                while True:
                    if n >= 0:
                        text = letters(b if back == 0 else b - 1)
                        if text[n] != "-":
                            return text[n], filled(b if back == 0 else b - 1, n, text[n])
                        n -= RING
                    elif isinstance(b, int) and b < 0:
                        return None, 0
                    else:
                        assert back == 0
                        back, n = 1, n + len(letters(b - 1 if isinstance(b, int) else b))

            block = st.enter_context(nc.Block())

            @block.sync
            def _(sp):
                sp.dma_start(wqr[:], a["w_qr"]).then_inc(wqr_in, 16)
                sp.dma_start(wuv_t[:], a["w_uv_t"]).then_inc(uvw_in, 16)
                sp.dma_start(wvo[:], a["w_o"]).then_inc(uvw_in, 16)

            @block.gpsimd
            def _(pool):
                def copy_x(b):
                    pool.tensor_copy(x_b[:], x_all[:, b, :]).then_inc(xb_out, 1)

                pool.memset(q_all[0:ROPE, 1, :, :], 0.0).then_inc(pads_set, 1)
                pool.memset(k_t[0:ROPE, 1, :], 0.0).then_inc(pads_set, 1)
                start = count.value
                with pool.Fori(1, B // 2) as i:
                    for half in range(2):
                        b = 2 * i + half
                        count.turn(start, b - 2, 2)
                        pool.wait_ge(fill, filled(b - 3, QCT))
                        pool.sem_inc(idx_go, 1)
                        copy_x(b)
                        pool.wait_ge(fill, filled(b - 2, PV + 3))
                        pool.sem_inc(idx_go, 1)
                        fetch(pool, b, half, i)

            @block.tensor
            def _(pe):
                drains = {"A": drain_act, "D": drain_dve}

                def bank(b, m):
                    who, n = last_user(b, m)
                    if who is not None:
                        pe.wait_ge(drains[who], n)
                    return ring[:, m % RING, :]

                def stored(b, m):
                    who = letters(b)[m]
                    pe.wait_ge(drains[who], filled(b, m, who))

                def turn_x(b, m, batch, direct=False):
                    r = bank(b, m)
                    if not direct:
                        pe.wait_ge(xb_out, batch - 1)
                    x = x_all[:, batch, :] if direct else x_b[:]
                    for c in range(DC):
                        mm = pe.transpose(r[:, c * T:(c + 1) * T], x[:, c * P:(c + 1) * P], ident[0:T, 0:T])
                    mm.then_inc(fill, 1)

                def make_qc(b, m):
                    r = bank(b, m)
                    stored(b, m - 1)
                    for j in range(2):
                        for c in range(DC):
                            mm = pe.matmul(r[0:QH, j * T:(j + 1) * T], wdq[:, c, j * QH:(j + 1) * QH], xb_t[:, c, :],
                                           start=(c == 0), stop=(c == DC - 1))
                    mm.then_inc(fill, 1)

                def make_queries(b, m, qc):
                    stored(b, qc)
                    for k in range(6):
                        r = bank(b, m + k)
                        for h in range(4):
                            for j in range(2):
                                if k < 4:
                                    w = wqn[:, j, 4 * k + h, :]
                                else:
                                    pair = 4 * (k - 4) + h
                                    w = wqr[:, j, pair * P:(pair + 1) * P]
                                mm = pe.matmul(r[:, h * T:(h + 1) * T], w, qc_t[:, j, :],
                                               start=(j == 0), stop=(j == 1))
                        mm.then_inc(fill, 1)

                def turn_keys(b, m, batch, half):
                    pe.wait_ge(rows_rot, batch + 1)
                    for k in range(4):
                        r = bank(b, m + k)
                        for t in range(4):
                            rows = rows_kv[half][:, 4 * (k % 2) + t, :]
                            cols = rows[:, 0:KVC] if k < 2 else rows[:, KW - P:KW]
                            mm = pe.transpose(r[:, t * P:(t + 1) * P], cols, ident[:])
                        mm.then_inc(fill, 1)

                def scores(b, keys, queries=None):
                    stored(b, keys + 3)
                    if queries is None:
                        pe.wait_ge(drain_dve, filled(b - 1, QR + 1, "D"))
                    else:
                        stored(b, queries + 1)
                    for g in range(NG):
                        for part in range(2):
                            q = q_all[:, part, g * GQ:(g + 1) * GQ, :].rearrange("p q h -> p (q h)")
                            mm = pe.matmul(s_ps[0:T, g * GK:(g + 1) * GK], q, k_t[:, part, g * GK:(g + 1) * GK],
                                           start=(part == 0), stop=(part == 1))
                    mm.then_inc(s_mm, 1)

                def turn_probs(b):
                    pe.wait_ge(p_set, b + 1)
                    flat = prob[:].rearrange("p g k -> p (g k)")
                    for k in range(2):
                        r = bank(b, PT + k)
                        for t in range(4):
                            n = 4 * k + t
                            mm = pe.transpose(r[:, t * T:(t + 1) * T], flat[:, n * P:(n + 1) * P], ident[0:T, 0:T])
                        mm.then_inc(fill, 1)

                def attend(b, half):
                    for k in range(2):
                        even, odd = bank(b, PV + 2 * k), bank(b, PV + 2 * k + 1)
                        stored(b, PT + k)
                        for t in range(4):
                            n = 4 * k + t
                            for r, rows in ((even, slice(0, GK)), (odd, slice(GK, P))):
                                mm = pe.matmul(r[:, t * T:(t + 1) * T], rows_kv[half][rows, n, 0:KVC],
                                               prob_t[rows, n, :], start=True, stop=True)
                                if t == 3:
                                    mm.then_inc(fill, 1)

                def join_heads(b):
                    r = bank(b, Y)
                    stored(b, PV + 3)
                    oc = oc_t[:].rearrange("p g q h -> p (g q) h")
                    for h in range(NH):
                        mm = pe.matmul(r[0:T, :], oc[:, :, h], wvo[:, h, :], start=(h == 0), stop=(h == NH - 1))
                    mm.then_inc(fill, 1)

                def turn_rounded_x(b, m, batch):
                    r = bank(b, m)
                    pe.wait_ge(xq_set, batch + 1)
                    for c in range(DC):
                        mm = pe.transpose(r.bitcast(BF16)[:, c * P:c * P + T], xq[:, c * P:(c + 1) * P],
                                          identb[0:T, 0:T])
                    mm.then_inc(fill, 1)

                def turn(b, half):
                    turn_probs(b)
                    turn_keys(b, KT, b + 1, 1 - half)
                    attend(b, half)
                    turn_x(b, XT, b + 2)
                    scores(b, KT)
                    make_qc(b, QCT)
                    join_heads(b)
                    make_queries(b, QN, QCT)
                    turn_rounded_x(b, XQ, b)

                turn_x(-1, AHEAD0, 0, direct=True)
                make_qc(-1, AHEAD0 + 1)
                pe.wait_ge(wqr_in, 16)
                make_queries(-1, AHEAD0 + 2, AHEAD0 + 1)
                turn_keys(-1, AHEAD0 + 8, 0, 0)
                turn_x(-1, AHEAD1, 1, direct=True)
                pe.wait_ge(pads_set, 2)
                scores(-1, AHEAD0 + 8, AHEAD0 + 6)
                make_qc(-1, AHEAD1 + 1)
                make_queries(-1, AHEAD1 + 3, AHEAD1 + 1)
                pe.wait_ge(uvw_in, 32)
                pe.wait_ge(s_sub, 1)
                for h in range(NH):
                    if h >= 2:
                        pe.wait_ge(vo_out, h - 1)
                    pe.matmul(s_ps[:, (h % 2) * 512:(h % 2 + 1) * 512], wuv_t[:, h, :], wvo[:, h, :],
                              start=True, stop=True).then_inc(vo_mm, 1)
                pe.wait_ge(vo_out, NH)
                turn(0, 0)
                turn(1, 1)
                with pe.Fori(1, LOOPED // 2) as i:
                    for half in range(2):
                        turn(2 * i + half, half)
                turn_probs(B - 2)
                turn_keys(B - 2, KT, B - 1, 1)
                attend(B - 2, 0)
                scores(B - 2, KT)
                join_heads(B - 2)
                turn_probs(B - 1)
                attend(B - 1, 1)
                join_heads(B - 1)
                turn_rounded_x(B - 1, XQ - 1, B - 2)
                turn_rounded_x(B - 1, XQ, B - 1)

            @block.scalar
            def _(act):
                def store(b, m, dst, rows=P, width=512, scale=1.0, **kw):
                    src = ring[rows if isinstance(rows, slice) else slice(0, rows), m % RING, 0:width]
                    if kw:
                        src = src.rearrange("p (u v) -> p u v", **kw)
                    act.wait_ge(fill, filled(b, m))
                    act.activation(dst, src, ACT.Copy, scale=scale).then_inc(drain_act, 1)

                def store_x(b, m):
                    store(b, m, xb_t[:], width=DC * T, u=DC)

                def store_qc(b, m):
                    store(b, m, qc_t[:], rows=QH, width=2 * T, scale=(XHD + ROPE) ** -0.5, u=2)

                def store_queries(b, m, ks=range(4)):
                    for k in ks:
                        store(b, m + k, q_all[:, 0, :, 4 * k:4 * k + 4].rearrange("p t h -> p h t"), width=4 * T, u=4)

                def store_keys(b, m):
                    for k in range(2):
                        store(b, m + k, k_t[:, 0, k * 512:(k + 1) * 512])
                    for k in range(2):
                        store(b, m + 2 + k, k_t[ROPE:P, 1, k * 512:(k + 1) * 512], rows=slice(ROPE, P))

                def store_probs(b):
                    for k in range(2):
                        store(b, PT + k, prob_t[:, 4 * k:4 * k + 4, :], width=4 * T, u=4)

                def store_outputs(b):
                    oc = oc_t[:].rearrange("p (s e) q h -> p s e (q h)", e=2)
                    for k in range(2):
                        for odd in range(2):
                            store(b, PV + 2 * k + odd, oc[:, 4 * k:4 * k + 4, odd, :], width=4 * T, u=4)

                def exp(b):
                    act.wait_ge(s_sub, b + 1)
                    act.activation(prob[:], prob[:], ACT.Exp).then_inc(s_exp, 1)

                def deviation(b):
                    act.wait_ge(var_set, 2 + b + 1)
                    act.activation(rstd_b[:], rstd_b[:], ACT.Sqrt).then_inc(std_set, 1)

                def scale_x(b):
                    act.wait_ge(xinv_set, b + 1)
                    act.activation(xmag, x_all[:, b, :], ACT.Copy, scale=xs[:, 3:4])
                    act.activation(xy, x_all[:, b, :], ACT.Copy, scale=xs[:, 2:3]).then_inc(x_scaled, 1)

                def store_rounded_x(b, m, batch):
                    act.wait_ge(fill, filled(b, m))
                    src = ring[:, m % RING, :].bitcast(BF16)[:, 0:DC * P].rearrange("p (c t) -> p c t", c=DC)
                    act.activation(xq_t[:, batch], src[:, :, 0:T], ACT.Copy).then_inc(drain_act, 1)

                store_x(-1, AHEAD0)
                store_qc(-1, AHEAD0 + 1)
                store_queries(-1, AHEAD0 + 2)
                store_keys(-1, AHEAD0 + 8)
                store_x(-1, AHEAD1)
                store_qc(-1, AHEAD1 + 1)
                exp(0)
                store_queries(-1, AHEAD1 + 3)
                for h in range(NH):
                    act.wait_ge(vo_mm, h + 1)
                    act.activation(wvo[:, h, :], s_ps[:, (h % 2) * 512:(h % 2 + 1) * 512], ACT.Copy).then_inc(vo_out, 1)

                def first_half(b):
                    store_probs(b)
                    store_keys(b, KT)
                    store_outputs(b)
                    store_x(b, XT)
                    store_qc(b, QCT)

                def second_half(b):
                    exp(b + 1)
                    store_queries(b, QN, (0,))
                    deviation(b)
                    store_queries(b, QN, (1, 2))
                    scale_x(b)
                    store_queries(b, QN, (3,))
                    store_rounded_x(b, XQ, b)

                first_half(0)
                with act.Fori(0, LOOPED - 1) as b:
                    second_half(b)
                    first_half(b + 1)
                second_half(LOOPED - 1)
                store_probs(B - 2)
                store_keys(B - 2, KT)
                store_outputs(B - 2)
                exp(B - 1)
                store_probs(B - 1)
                store_outputs(B - 1)
                for b in (B - 2, B - 1):
                    deviation(b)
                    scale_x(b)
                store_rounded_x(B - 1, XQ - 1, B - 2)
                store_rounded_x(B - 1, XQ, B - 1)

            @block.vector
            def _(dve):
                def rotary_queries(b, at):
                    for k in range(2):
                        dve.wait_ge(fill, filled(b, at + k))
                        src = ring[:, (at + k) % RING, 0:4 * T].rearrange("p (h t) -> p h t", h=4)
                        dst = q_all[ROPE:P, 1, :, 8 * k:8 * k + 8].rearrange("p t (h e) -> p e h t", e=2)
                        dve.tensor_copy(dst[:, 0], src[0:ROPE])
                        dve.tensor_copy(dst[:, 1], src[ROPE:P]).then_inc(drain_dve, 1)

                def window(b):
                    segs = seg_rows[:, bass.ds(b * NG, NG)]
                    chain(dve.tensor_tensor(mask[:], segs.unsqueeze(2).broadcast_to([T, NG, GK]),
                                            off_mask[:].unsqueeze(1).broadcast_to([T, NG, GK]), ALU.add))
                    chain(dve.tensor_scalar(outside[:], mask[:], 0.0, None, ALU.is_lt))
                    chain(dve.scalar_tensor_tensor(outside[:], mask[:], float(LK - 1), outside[:], ALU.is_gt, ALU.max))
                    chain(dve.tensor_copy(outside[:, :, GK - 1], windowed[:, bass.ds(b * NG, NG)]))

                def shift(b):
                    dve.wait_ge(s_mm, b + 1)
                    chain(dve.scalar_tensor_tensor(prob[:], outside[:], NEG,
                                                   s_ps[0:T].rearrange("p (g k) -> p g k", g=NG), ALU.mult, ALU.add))
                    chain(dve.tensor_reduce(xmax[:], prob[:], AX.X, ALU.max))
                    dve.tensor_tensor(prob[:], prob[:], xmax[:].unsqueeze(2).broadcast_to([T, NG, GK]),
                                      ALU.subtract).then_inc(s_sub, 1)

                def normalise(b):
                    dve.wait_ge(s_exp, b + 1)
                    chain(dve.tensor_reduce(xsum[:], prob[:], AX.X, ALU.add))
                    chain(dve.reciprocal(xsum[:], xsum[:]))
                    dve.tensor_tensor(prob[:], prob[:], xsum[:].unsqueeze(2).broadcast_to([T, NG, GK]),
                                      ALU.mult).then_inc(p_set, 1)

                def add_y(b):
                    dve.wait_ge(fill, filled(b, Y))
                    x = x_all[:, b, :]
                    chain(dve.tensor_tensor(x, x, ring[0:T, Y % RING, :], ALU.add))
                    dve.nop().then_inc(drain_dve, 1)

                def normalise_and_round(b, last=False):
                    x = x_all[:, b, :]
                    chain(dve.bn_stats(stats_b[:], x))
                    dve.sem_inc(dve_go, 1)
                    chain(dve.bn_aggr(mv_b[:], stats_b[:]))
                    chain(dve.tensor_scalar(rstd_b[:], mv_b[:, 1:2], EPS, None, ALU.add))
                    dve.nop().then_inc(var_set, 1)
                    dve.wait_ge(std_set, 2 + b + 1)
                    chain(dve.reciprocal(rstd_b[:], rstd_b[:]))
                    chain(dve.tensor_scalar(x, x, mv_b[:, 0:1], rstd_b[:, 0:1], ALU.subtract, ALU.mult))
                    dve.sem_inc(dve_go, 1)
                    chain(dve.tensor_reduce(xs[:, 0:1], x, AX.X, ALU.max, apply_absolute_value=True))
                    chain(dve.tensor_scalar(xs[:, 1:2], xs[:, 0:1], 1.0 / FP8_MAX, None, ALU.mult))
                    chain(dve.reciprocal(xs[:, 2:3], xs[:, 1:2]))
                    dve.tensor_scalar(xs[:, 3:4], xs[:, 2:3], 2.0 ** 20, None, ALU.mult).then_inc(xinv_set, 1)
                    dve.tensor_copy(xq_s[:, bass.ds(b, 1)], xs[:, 1:2])
                    dve.wait_ge(x_scaled, b + 1)
                    if last:
                        dve.wait_ge(fill, filled(B - 1, XQ - 1))
                    chain(magic_bits(dve, xmag.bitcast(U32)))
                    chain(magic_add(dve, xy, xmag))
                    magic_sub(dve, xq[:], xy, xmag).then_inc(xq_set, 1)

                chain(dve.tensor_scalar(windowed[:], seg_rows[:], 0.0, None, ALU.is_ge))
                chain(dve.scalar_tensor_tensor(windowed[:], seg_rows[:], float(LK - 1 + SPAN - 1), windowed[:],
                                               ALU.is_le, ALU.mult))
                dve.wait_ge(pads_set, 2)
                window(0)
                rotary_queries(-1, AHEAD0 + 6)
                shift(0)
                window(1)
                normalise(0)
                rotary_queries(-1, AHEAD1 + 7)
                start = chain.value
                PER = 2 + 4 + 2 + 1 + 8 + 2
                with dve.Fori(0, LOOPED) as b:
                    chain.turn(start, b, PER)
                    shift(b + 1)
                    window(b + 2)
                    normalise(b + 1)
                    add_y(b)
                    normalise_and_round(b)
                    rotary_queries(b, QR)
                chain.turned(start, LOOPED, PER)
                shift(B - 1)
                normalise(B - 1)
                add_y(B - 2)
                normalise_and_round(B - 2)
                add_y(B - 1)
                normalise_and_round(B - 1, last=True)

        with ExitStack() as st:
            def sb(name, shape, dt=F32):
                return st.enter_context(nc.sbuf_tensor(name, shape, dt))

            def ps(name, shape, dt=F32):
                return st.enter_context(nc.psum_tensor(name, shape, dt))

            gate = sb("gate", [T, 2, 512])
            upv = sb("upv", [T, 2, 512])
            hid = [sb(f"hid{k}", [T, F]) for k in range(2)]
            hy = sb("hy", [T, F])
            hmag = sb("hmag", [T, F])
            hq = sb("hq", [T, F], BF16)
            hq_t = sb("hq_t", [P, FC, T], BF16)
            ysum = sb("ysum", [T, D])
            xs_b = [sb(f"xs_b{k}", [T, 1]) for k in range(2)]
            hs = [sb(f"hs{k}", [T, 4]) for k in range(2)]

            gu_ps = ps("gu_ps", [T, 2, 2, 512])
            ht_ps = ps("ht_ps", [P, 2048], BF16)
            y3_ps = ps("y3_ps", [T, 512])

            gu_mm = sem("gu_mm")
            gu_out = sem("gu_out")
            gate_set = sem("gate_set")
            silu_out = sem("silu_out")
            hid_go = sem("hid_go")
            hid_set = sem("hid_set")
            hinv_set = sem("hinv_set")
            h_scaled = sem("h_scaled")
            hq_set = sem("hq_set")
            ht_mm = sem("ht_mm")
            ht_out = sem("ht_out")
            y3_mm = sem("y3_mm")
            y3_out = sem("y3_out")
            normed = sem("normed")
            stored = sem("stored")

            NCH = len(FCH)
            block = st.enter_context(nc.Block())

            @block.sync
            def _(sp):
                for b in range(B):
                    sp.wait_ge(normed, b + 1)
                    sp.dma_start(out[b], x_all[:, b, :]).then_inc(stored, 16)
                sp.wait_ge(stored, 16 * B)

            @block.tensor
            def _(pe):
                def gate_up(b, half, n):
                    at, width = FCH[n]
                    pe.wait_ge(gu_out, NCH * b + n + 1)
                    for m, w in enumerate((gate_w, up_w)):
                        for c in range(DC):
                            mm = pe.matmul(gu_ps[:, (NCH * half + n) % 2, m, 0:width], xq_t[:, b, c, :],
                                           w[:, c, at:at + width], start=(c == 0), stop=(c == DC - 1))
                    mm.then_inc(gu_mm, 1)

                def batch(b, half, ahead=NCH):
                    pe.wait_ge(hq_set, b + 1)
                    for c in range(FC):
                        mm = pe.transpose(ht_ps[:, c * P:c * P + T], hq[:, c * P:(c + 1) * P], identb[0:T, 0:T])
                    mm.then_inc(ht_mm, 1)
                    if ahead:
                        gate_up(b + 2, half, 1)
                    pe.wait_ge(ht_out, b + 1)
                    pe.wait_ge(y3_out, b + 1)
                    for c in range(FC):
                        mm = pe.matmul(y3_ps[:], hq_t[:, c, :], down_w[:, c, :], start=(c == 0), stop=(c == FC - 1))
                    mm.then_inc(y3_mm, 1)
                    if ahead:
                        gate_up(b + 2, half, 2)
                    if ahead == NCH:
                        gate_up(b + 3, 1 - half, 0)

                for b, n in ((0, 0), (0, 1), (0, 2), (1, 0), (1, 1), (1, 2), (2, 0)):
                    gate_up(b, b % 2, n)
                with pe.Fori(0, B // 2 - 2) as i:
                    for half in range(2):
                        batch(2 * i + half, half)
                batch(B - 4, 0)
                batch(B - 3, 1, NCH - 1)
                batch(B - 2, 0, 0)
                batch(B - 1, 1, 0)

            @block.scalar
            def _(act):
                def silu(b, half, n):
                    g = gate[:, (NCH * half + n) % 2, 0:FCH[n][1]]
                    act.wait_ge(gate_set, NCH * b + n + 1)
                    act.activation(g, g, ACT.Silu).then_inc(silu_out, 1)

                def batch(b, half, last=False):
                    act.wait_ge(hinv_set, b + 1)
                    act.activation(hmag[:], hid[half][:], ACT.Copy, scale=hs[half][:, 3:4])
                    act.activation(hy[:], hid[half][:], ACT.Copy, scale=hs[half][:, 2:3]).then_inc(h_scaled, 1)
                    if not last:
                        for n in range(NCH):
                            silu(b + 1, 1 - half, n)
                    act.wait_ge(ht_mm, b + 1)
                    act.activation(hq_t[:], ht_ps[:, 0:FC * P].rearrange("p (c t) -> p c t", c=FC)[:, :, 0:T],
                                   ACT.Copy).then_inc(ht_out, 1)

                act.sem_inc(h_scaled, 2)
                for n in range(NCH):
                    silu(0, 0, n)
                with act.Fori(0, B // 2 - 1) as i:
                    for half in range(2):
                        batch(2 * i + half, half)
                batch(B - 2, 0)
                batch(B - 1, 1, True)
                norm_deviation(act, 2 + B, 0)
                norm_deviation(act, 2 + B, 1)

            @block.gpsimd
            def _(pool):
                def hidden(b, half, n):
                    at, width = FCH[n]
                    k = (NCH * half + n) % 2
                    if n == 0:
                        pool.wait_ge(h_scaled, b + 1)
                    pool.wait_ge(silu_out, NCH * b + n + 1)
                    pool.wait_ge(gu_out, NCH * b + n + 3)
                    pool.sem_inc(hid_go, 1)
                    pool.tensor_tensor(hid[half][:, at:at + width], gate[:, k, 0:width], upv[:, k, 0:width],
                                       ALU.mult).then_inc(hid_set, 1)

                pool.sem_inc(hid_set, 2)
                with pool.Fori(0, B // 2) as i:
                    for half in range(2):
                        for n in range(NCH):
                            hidden(2 * i + half, half, n)

            @block.vector
            def _(dve):
                def free_to_gate(b, n):
                    dve.wait_ge(gu_mm, NCH * b + n + 1)
                    dve.wait_ge(hid_set, NCH * b + n + 1)

                def scaled_gate(b, half, n):
                    at, width = FCH[n]
                    k = (NCH * half + n) % 2
                    free_to_gate(b, n)
                    dve.scalar_tensor_tensor(gate[:, k, 0:width], gu_ps[:, k, 0, 0:width], xs_b[half][:, 0:1],
                                             gate_s[:, at:at + width], ALU.mult, ALU.mult).then_inc(gate_set, 1)

                def scaled_up(b, half, n):
                    at, width = FCH[n]
                    k = (NCH * half + n) % 2
                    dve.scalar_tensor_tensor(upv[:, k, 0:width], gu_ps[:, k, 1, 0:width], xs_b[half][:, 0:1],
                                             up_s[:, at:at + width], ALU.mult, ALU.mult).then_inc(gu_out, 1)

                def y_product(b, half):
                    dve.wait_ge(y3_mm, b + 1)
                    return chain.mark(dve.scalar_tensor_tensor(ysum[:], y3_ps[:], hs[half][:, 1:2], down_s[:],
                                                               ALU.mult, ALU.mult))

                def batch(b, half, first=False, last=False):
                    s, at, other = hs[half], FCH[-1][0], 1 - half
                    scaled_gate(b, half, 2)
                    scaled_up(b, half, 2)
                    dve.wait_ge(hid_set, NCH * b + NCH + 1)
                    dve.tensor_reduce(s[:, 0:1], hid[half][:, 0:at], AX.X, ALU.max, apply_absolute_value=True)
                    if not last:
                        chain.mark(dve.tensor_copy(xs_b[other][:], xq_s[:, bass.ds(b + 1, 1)]))
                    dve.wait_ge(hid_set, NCH * b + NCH + 2)
                    reduced = chain.mark(dve.tensor_reduce(s[:, 1:2], hid[half][:, at:F], AX.X, ALU.max,
                                                           apply_absolute_value=True))
                    chain.need(reduced)
                    chain(dve.tensor_scalar(s[:, 1:2], s[:, 1:2], s[:, 0:1], 1.0 / FP8_MAX, ALU.max, ALU.mult))
                    chain(dve.reciprocal(s[:, 2:3], s[:, 1:2]))
                    dve.tensor_scalar(s[:, 3:4], s[:, 2:3], 2.0 ** 20, None, ALU.mult).then_inc(hinv_set, 1)
                    if not last:
                        for n in range(2):
                            scaled_gate(b + 1, other, n)
                            scaled_up(b + 1, other, n)
                    dve.wait_ge(h_scaled, b + 3)
                    magic = chain.mark(magic_bits(dve, hmag[:].bitcast(U32)))
                    if not first:
                        product = y_product(b - 1, other)
                    chain.need(magic)
                    rounded = chain.mark(magic_add(dve, hy[:], hmag[:]))
                    if not first:
                        x = x_all[:, b - 1, :]
                        chain.need(product)
                        dve.nop().then_inc(y3_out, 1)
                        summed = chain.mark(dve.tensor_tensor(x, x, ysum[:], ALU.add))
                    chain.need(rounded)
                    magic_sub(dve, hq[:], hy[:], hmag[:]).then_inc(hq_set, 1)
                    if not first:
                        chain.need(summed)
                        chain(dve.bn_stats(stats[:, b - 1, :], x))

                dve.sem_inc(gu_out, 2)
                dve.sem_inc(y3_out, 1)
                chain(dve.tensor_copy(xs_b[0][:], xq_s[:, 0:1]))
                for n in range(2):
                    scaled_gate(0, 0, n)
                    scaled_up(0, 0, n)
                batch(0, 0, first=True)
                batch(1, 1)
                start = chain.value
                PER = 4 + 3 + 2
                with dve.Fori(1, B // 2 - 1) as i:
                    for half in range(2):
                        chain.turn(start, 2 * i + half - 2, PER)
                        batch(2 * i + half, half)
                chain.turned(start, B - 4, PER)
                batch(B - 2, 0)
                batch(B - 1, 1, last=True)
                norm_variance(dve, 0)
                normalise_x(dve, 2 + B, 0, normed)
                chain.need(y_product(B - 1, 1))
                x = x_all[:, B - 1, :]
                chain(dve.tensor_tensor(x, x, ysum[:], ALU.add))
                chain(dve.bn_stats(stats[:, B - 1, :], x))
                norm_variance(dve, 1)
                normalise_x(dve, 2 + B, 1, normed)


def rope_tables():
    half = ROPE // 2
    inv_freq = (np.float32(1.0) / np.float32(10000.0) ** (np.arange(half, dtype=np.float32) / np.float32(half)))
    ang = np.arange(LK, dtype=np.float32)[:, None] * inv_freq.astype(np.float32)
    c, s = np.cos(ang), np.sin(ang)
    return np.concatenate([c, c, -s, s], axis=1).astype(np.float32)


def kernel(x, ctx_2048, itok_BxS_0_1023, L0_attn_q1_w, L0_attn_k1_w, L0_attn_q2_w, L0_attn_k2_w, L0_attn_v_w,
           L0_attn_o_w, L0_attn_lambda_param, L0_xattn_W_kvc, L0_xattn_W_dq, L0_xattn_W_uq, L0_xattn_W_qr,
           L0_xattn_W_uk, L0_xattn_W_kr, L0_xattn_W_uv, L0_xattn_W_o, L0_ffn_w_gate, L0_ffn_w_up, L0_ffn_w_down,
           L0_ffn_up_reorder_index, L0_ffn_down_reorder_index):
    import concourse.bacc as bacc
    from concourse.bass_utils import run_bass_kernel_spmd
    import ml_dtypes

    def rows(w):
        return np.ascontiguousarray(w.reshape(-1, P, w.shape[1]).transpose(1, 0, 2))

    def swap(w):
        w = w.reshape(w.shape[0], -1, 2, ROPE // 2)
        return w[:, :, ::-1, :].reshape(w.shape[0], -1)

    x, ctx, seg = np.asarray(x), np.asarray(ctx_2048), np.asarray(itok_BxS_0_1023)
    uq, uk, uv = (np.asarray(w) for w in (L0_xattn_W_uq, L0_xattn_W_uk, L0_xattn_W_uv))
    qr, kr = np.asarray(L0_xattn_W_qr), np.asarray(L0_xattn_W_kr)
    lam = np.asarray(L0_attn_lambda_param).reshape(1, NJ, HG)
    table = rope_tables()

    col = np.arange(GK)
    in_span = col < GQ * SPAN
    query = np.arange(T) // NH
    off = np.where(in_span[None, :] & (query[:, None] == col[None, :] // SPAN),
                   -(col % SPAN)[None, :], NEG).astype(np.float32)
    row_c = np.stack([np.where(in_span, -(col % SPAN), 0), in_span], 1).astype(np.float32)
    base = np.arange(B)[None, :] * TROWS + np.where(in_span, 0, LK)[:, None]
    base = np.repeat(np.concatenate([base, base]), NT, axis=1).astype(np.float32)
    groups = seg.reshape(B, NG, GQ)
    seg_rows = np.repeat(groups.transpose(2, 0, 1).reshape(GQ, B * NG), NH, axis=0)
    by_col = np.concatenate([np.repeat(groups, SPAN, axis=2), groups[:, :, 0:1]], axis=2)
    seg_keys = by_col.reshape(B * NT, P).T

    where = (2 * GQ * np.arange(NT)[None, :] + np.concatenate([col // SPAN, GQ + col // SPAN])[:, None]) % T
    cos_q = table[where][:, :, 0:ROPE].reshape(P, NT, 2, ROPE // 2)
    sin_q = -table[where][:, :, ROPE:2 * ROPE].reshape(P, NT, 2, ROPE // 2)
    arrays = {
        "x": x,
        "x_t": x.reshape(B, T, DC, P).transpose(0, 3, 2, 1),
        "w_in": np.stack([rows(np.asarray(w).T) for w in (L0_attn_q1_w, L0_attn_k1_w, L0_attn_q2_w, L0_attn_k2_w,
                                                          L0_attn_v_w)]),
        "w_attn_o": rows(np.asarray(L0_attn_o_w).T),
        "lam": np.broadcast_to(lam, (T, NJ, HG)),
        "ctx_t": ctx.reshape(B, LK, DC, P).transpose(0, 3, 2, 1),
        "w_kvc": rows(np.asarray(L0_xattn_W_kvc)), "w_kvc_t": np.asarray(L0_xattn_W_kvc).T,
        "w_kr2": np.concatenate([kr, swap(kr)], axis=1),
        "w_dq": rows(np.asarray(L0_xattn_W_dq)),
        "w_uq_t": uq.reshape(QC, NH, XHD).transpose(2, 1, 0), "w_uk_t": uk.reshape(KVC, NH, XHD).transpose(2, 1, 0),
        "w_qr": qr.reshape(2, QH, NH * ROPE).transpose(1, 0, 2), "cos_q": cos_q, "sin_q": sin_q,
        "w_uv_t": uv.reshape(KVC, NH, XHD).transpose(2, 1, 0), "w_o": rows(np.asarray(L0_xattn_W_o)),
        "w_gate": np.asarray(L0_ffn_w_gate), "w_up": np.asarray(L0_ffn_w_up),
        "w_down": np.asarray(L0_ffn_w_down).reshape(DC, P, F),
        "order": np.asarray(L0_ffn_down_reorder_index).reshape(FC, P).T,
        "seg_rows": seg_rows, "seg_keys": seg_keys,
        "ident": np.eye(P, dtype=np.float32), "identb": np.eye(P).astype(ml_dtypes.bfloat16),
        "off_mask": off, "row_c": np.concatenate([row_c, row_c]), "row_base": base,
        "rope_k": table.reshape(KTILES, KROWS, 2 * ROPE).transpose(1, 0, 2),
    }
    arrays = {n: np.ascontiguousarray(v) for n, v in arrays.items()}
    nc = bacc.Bacc("TRN2", target_bir_lowering=False, num_devices=1)
    ins = {n: nc.dram_tensor(f"in_{n}", v.shape, mybir.dt.from_np(v.dtype), kind="ExternalInput").ap()
           for n, v in arrays.items()}
    out = nc.dram_tensor("out", (B, T, D), F32, kind="ExternalOutput").ap()
    build(nc, ins, out)
    r = run_bass_kernel_spmd(nc, [{f"in_{n}": v for n, v in arrays.items()}], core_ids=[0])
    return r.results[0]["out"]
```
